# Optimizing a Trainium2 kernel written in Bass

```python
import numpy as np
import jax
import jax.numpy as jnp

def _softmax(x, axis=-1):
    return jax.nn.softmax(x, axis=axis)

def _gelu(x):
    return jax.nn.gelu(x, approximate=True)

def _silu(x):
    return jax.nn.silu(x)

def _sigmoid(x):
    return jax.nn.sigmoid(x)

def _layernorm(x, axis=-1, eps=1e-05):
    m = jnp.mean(x, axis=axis, keepdims=True)
    v = jnp.var(x, axis=axis, keepdims=True)
    return (x - m) / jnp.sqrt(v + eps)

def _scatter_add(tgt, idx, src, axis=0):
    return tgt.at[idx].add(src)

def _segment_sum(src, seg, n):
    return jax.ops.segment_sum(src, seg, n)
kernel_name = 'mk_sandwich_d1_jaxref_r8_e79bdc'

def setup_inputs(seed: int=0):
    np.random.seed(seed)
    _w = jnp.asarray

    def _L0_attn_setup():
        import jax, jax.numpy as jnp
        import numpy as np
        import math
        EMBED_DIM = 256
        HEAD_NUM = 2
        B, S = (2, 512)
        key = jax.random.key(seed)
        ks = jax.random.split(key, 9)
        bf16 = jnp.bfloat16
        d = EMBED_DIM
        scale = 1.0 / math.sqrt(d)
        base = jax.random.normal(ks[0], (B, S, d), dtype=bf16)

        def lin(k):
            kw, kb = jax.random.split(k)
            W = jax.random.uniform(kw, (d, d), dtype=jnp.float32, minval=-scale, maxval=scale).astype(bf16)
            b = jax.random.uniform(kb, (d,), dtype=jnp.float32, minval=-scale, maxval=scale).astype(bf16)
            return (W, b)
        Wq, bq = lin(ks[1])
        Wk, bk = lin(ks[2])
        Wv, bv = lin(ks[3])
        Wo, bo = lin(ks[4])
        return {'base': base, 'Wq': Wq, 'bq': bq, 'Wk': Wk, 'bk': bk, 'Wv': Wv, 'bv': bv, 'Wo': Wo, 'bo': bo}
    _L0_attn_in = _L0_attn_setup()

    def _L0_ffn_setup():
        import jax, jax.numpy as jnp
        import numpy as np
        B, S, H, F, E, K = (2, 128, 256, 688, 8, 2)
        key = jax.random.key(seed)
        k0, k1, k2, k3, k4 = jax.random.split(key, 5)
        x = jax.random.normal(k0, (B, S, H), dtype=jnp.float32)
        router_w = jax.random.normal(k1, (E, H), dtype=jnp.float32) * 0.02
        gate_w = jax.random.normal(k2, (E, F, H), dtype=jnp.float32) * 0.02
        up_w = jax.random.normal(k3, (E, F, H), dtype=jnp.float32) * 0.02
        down_w = jax.random.normal(k4, (E, H, F), dtype=jnp.float32) * 0.02
        return {'x': x, 'router_w': router_w, 'gate_w': gate_w, 'up_w': up_w, 'down_w': down_w}
    _L0_ffn_in = _L0_ffn_setup()
    _d = {'L0_attn_base': _L0_attn_in['base'], 'L0_attn_Wq': _L0_attn_in['Wq'], 'L0_attn_bq': _L0_attn_in['bq'], 'L0_attn_Wk': _L0_attn_in['Wk'], 'L0_attn_bk': _L0_attn_in['bk'], 'L0_attn_Wv': _L0_attn_in['Wv'], 'L0_attn_bv': _L0_attn_in['bv'], 'L0_attn_Wo': _L0_attn_in['Wo'], 'L0_attn_bo': _L0_attn_in['bo'], 'L0_ffn_router_w': _L0_ffn_in['router_w'], 'L0_ffn_gate_w': _L0_ffn_in['gate_w'], 'L0_ffn_up_w': _L0_ffn_in['up_w'], 'L0_ffn_down_w': _L0_ffn_in['down_w']}
    _x0 = _d['L0_attn_base']
    _d['L0_attn_base'] = jax.random.normal(jax.random.fold_in(jax.random.key(seed), 1), (16, 256, 256), dtype=_x0.dtype)
    del _x0
    return _d

def reference(L0_attn_base, L0_attn_Wq, L0_attn_bq, L0_attn_Wk, L0_attn_bk, L0_attn_Wv, L0_attn_bv, L0_attn_Wo, L0_attn_bo, L0_ffn_router_w, L0_ffn_gate_w, L0_ffn_up_w, L0_ffn_down_w):

    def _L0_attn_ref(base, Wq, bq, Wk, bk, Wv, bv, Wo, bo):
        import jax, jax.numpy as jnp
        import numpy as np
        import math
        EMBED_DIM = 256
        HEAD_NUM = 2
        B, S = (2, 512)
        H = HEAD_NUM
        b, s, d = base.shape
        hd = d // H
        relu = jax.nn.relu
        q = relu(base @ Wq.T + bq)
        k = relu(base @ Wk.T + bk)
        v = relu(base @ Wv.T + bv)

        def split_heads(x):
            return x.reshape(b, s, H, hd).transpose(0, 2, 1, 3)
        q, k, v = (split_heads(q), split_heads(k), split_heads(v))
        scale = 1.0 / math.sqrt(hd)
        scores = jnp.einsum('bhqd,bhkd->bhqk', q, k) * jnp.asarray(scale, q.dtype)
        attn = jax.nn.softmax(scores, axis=-1)
        y = jnp.einsum('bhqk,bhkd->bhqd', attn, v)
        y = y.transpose(0, 2, 1, 3).reshape(b, s, d)
        y = relu(y @ Wo.T + bo)
        return y.astype(base.dtype)

    def _L0_ffn_ref(x, router_w, gate_w, up_w, down_w):
        import jax, jax.numpy as jnp
        import numpy as np
        B, S, H, F, E, K = (2, 128, 256, 688, 8, 2)
        b, s, h = x.shape
        xf = x.reshape(-1, h)
        logits = xf @ router_w.T
        top_v, top_i = jax.lax.top_k(logits, K)
        probs = jax.nn.softmax(top_v.astype(jnp.float32), axis=-1).astype(logits.dtype)
        combine = jnp.sum(jax.nn.one_hot(top_i, E, dtype=x.dtype) * probs[..., None], axis=1)
        g = jnp.einsum('th,efh->etf', xf, gate_w)
        u = jnp.einsum('th,efh->etf', xf, up_w)
        y = jnp.einsum('etf,ehf->eth', jax.nn.silu(g) * u, down_w)
        out = jnp.einsum('te,eth->th', combine, y)
        return out.reshape(b, s, h)
    x = L0_attn_base
    x = x + _layernorm(_L0_attn_ref(_layernorm(x, axis=-1), L0_attn_Wq, L0_attn_bq, L0_attn_Wk, L0_attn_bk, L0_attn_Wv, L0_attn_bv, L0_attn_Wo, L0_attn_bo), axis=-1)
    x = x + _layernorm(_L0_ffn_ref(_layernorm(x, axis=-1), L0_ffn_router_w, L0_ffn_gate_w, L0_ffn_up_w, L0_ffn_down_w), axis=-1)
    return x

_drawn_inputs = setup_inputs


def setup_inputs(seed=0):
    import zlib

    import numpy as np

    out = dict(_drawn_inputs(seed))
    spreads = {}
    factors = {}
    for name, (base, spread) in spreads.items():
        noise = np.random.default_rng([zlib.crc32(name.encode()), seed]).standard_normal(out[name].shape)
        drawn = base * np.exp(spread * noise) if base else spread * noise
        out[name] = jnp.asarray(drawn.astype(out[name].dtype))
    for name, factor in factors.items():
        out[name] = (out[name] * factor).astype(out[name].dtype)
    return out
```

```python
import concourse.bass as bass
from concourse import mybir
from contextlib import ExitStack

BATCHES, SEQ, DIM, HEADS = 16, 256, 256, 2
HEAD_DIM = DIM // HEADS
EXPERTS, FFN, TOP_K = 8, 688, 2
P = 128
TOKENS = BATCHES * SEQ
ROW_TILES = SEQ // P
CHUNKS = DIM // P
SLOTS = TOKENS * TOP_K
MOE_TILES = (SLOTS + EXPERTS * (P - 1)) // P
REGION = TOKENS + P
DUMMY_ROW = EXPERTS * REGION
ROW_WORDS = DIM // 2 + 2
NOWHERE = 1 << 20
HALF = FFN // 2
PIECES = (128, 128, HALF - 256)
PARTS = 3
EPS = 1e-5
TAIL_ROWS = 4
TAIL_GROUPS = TOKENS // (P * TAIL_ROWS)


def build(nc, base, wqT, wkT, wvT, woT, bq, bk, bv, bo, routerT, gate_up, down, out):
    fp32, bf16, i32 = mybir.dt.float32, mybir.dt.bfloat16, mybir.dt.int32
    ALU, ACT, AX = mybir.AluOpType, mybir.ActivationFunctionType, mybir.AxisListType

    dispatched = nc.dram_tensor("dispatched", [DUMMY_ROW + P, ROW_WORDS], i32, kind="Internal").ap()
    expert_out = nc.dram_tensor("expert_out", [SLOTS, DIM], fp32, kind="Internal").ap()
    residual = nc.dram_tensor("residual", [TOKENS, DIM], bf16, kind="Internal").ap()

    ctx = ExitStack()
    with ctx:
        def sb(name, shape, dt):
            return ctx.enter_context(nc.sbuf_tensor(name, shape, dt))

        def pb(name):
            return ctx.enter_context(nc.psum_tensor(name, [P, 512], fp32))

        def sem(name):
            return ctx.enter_context(nc.semaphore(name))

        gu_w = sb("gu_w", [P, EXPERTS * CHUNKS * PARTS, 2 * FFN], bf16)
        down_w = sb("down_w", [P, EXPERTS, 6 * DIM], fp32)
        stage = sb("stage", [P, 2 * FFN], fp32)
        payload = sb("payload", [P, 8, ROW_WORDS], i32)
        attn_w = sb("attn_w", [P, 4, CHUNKS, DIM], bf16)
        qk_bias = sb("qk_bias", [P, 2, HEADS], bf16)
        qk_biasf = sb("qk_biasf", [P, 2, HEADS], fp32)
        row_bias = sb("row_bias", [P, 2, DIM], bf16)
        router32 = sb("router32", [P, CHUNKS, EXPERTS], fp32)
        router_w = sb("router_w", [P, PARTS, CHUNKS, EXPERTS], bf16)
        identf = sb("identf", [P, P], fp32)
        ident = sb("ident", [P, P], bf16)
        before = sb("before", [P, P], bf16)
        ones = sb("ones", [P, P], bf16)
        y_buf = sb("y_buf", [P, 3, DIM], fp32)
        xT_buf = sb("xT_buf", [P, 3, CHUNKS, P], bf16)
        meta = sb("meta", [P, 3, 2], i32)
        hT = sb("hT", [P, 2, 3, P], fp32)
        ln_stats = sb("ln_stats", [P, 3, ROW_TILES, 6], fp32)
        ln_mv = sb("ln_mv", [P, 3, ROW_TILES, 2], bf16)
        ln_var = sb("ln_var", [P, 3, ROW_TILES], bf16)
        ln_std = sb("ln_std", [P, 3, ROW_TILES], bf16)
        ln_inv = sb("ln_inv", [P, 3, ROW_TILES], fp32)
        ln_sum = sb("ln_sum", [P, 3, ROW_TILES], fp32)
        ln_mean = sb("ln_mean", [P, 3, ROW_TILES], bf16)
        half = sb("half", [P, ROW_TILES], bf16)
        pace = sb("pace", [P, 1], bf16)
        minus_half = sb("minus_half", [P, TAIL_ROWS], fp32)
        tail_var = sb("tail_var", [P, 2, TAIL_ROWS], fp32)
        sm_max = sb("sm_max", [P, 4], fp32)
        sm_total = sb("sm_total", [P, 4], fp32)
        sm_sum = sb("sm_sum", [P, 4], bf16)
        sm_inv = sb("sm_inv", [P, 4], fp32)
        logits = sb("logits", [P, ROW_TILES, EXPERTS], fp32)
        above = sb("above", [P, ROW_TILES, EXPERTS, EXPERTS], fp32)
        level = sb("level", [P, ROW_TILES, EXPERTS, EXPERTS], fp32)
        lower = sb("lower", [P, EXPERTS, EXPERTS], fp32)
        rank = sb("rank", [P, ROW_TILES, EXPERTS], fp32)
        chosen = sb("chosen", [P, ROW_TILES, TOP_K, EXPERTS], fp32)
        picked = sb("picked", [P, ROW_TILES, TOP_K, EXPERTS], fp32)
        picked2 = sb("picked2", [P, ROW_TILES, TOP_K, EXPERTS], fp32)
        top = sb("top", [P, ROW_TILES, TOP_K], fp32)
        gap = sb("gap", [P, ROW_TILES], fp32)
        gap_exp = sb("gap_exp", [P, ROW_TILES], fp32)
        denom = sb("denom", [P, ROW_TILES], fp32)
        prob = sb("prob", [P, ROW_TILES, TOP_K], fp32)
        mask = sb("mask", [P, ROW_TILES, EXPERTS], bf16)
        count = sb("count", [P, 2, EXPERTS], bf16)
        place = sb("place", [P, ROW_TILES, EXPERTS], fp32)
        region_start = sb("region_start", [P, EXPERTS], fp32)
        slotf = sb("slotf", [P, ROW_TILES, TOP_K], fp32)
        slot = sb("slot", [P, 2, ROW_TILES * TOP_K], i32)
        dest = sb("dest", [P, ROW_TILES, TOP_K], i32)
        pad_place = sb("pad_place", [P, EXPERTS], fp32)
        pad_slot = sb("pad_slot", [P, EXPERTS], i32)
        pad_row = sb("pad_row", [P, ROW_WORDS], i32)
        total = sb("total", [P, EXPERTS], fp32)
        tile_first = sb("tile_first", [1, 32], fp32)
        tiles_of = sb("tiles_of", [1, EXPERTS], fp32)
        tiles_upto = sb("tiles_upto", [1, EXPERTS], fp32)
        tile_no = sb("tile_no", [1, MOE_TILES], fp32)
        tile_expert = sb("tile_expert", [1, MOE_TILES], fp32)
        tile_skipped = sb("tile_skipped", [1, MOE_TILES], fp32)
        tile_local = sb("tile_local", [1, MOE_TILES], fp32)
        tile_rowf = sb("tile_rowf", [1, MOE_TILES], fp32)
        table = sb("table", [1, 2, MOE_TILES], i32)
        tail_stats = sb("tail_stats", [P, 2, TAIL_ROWS, 6], fp32)
        tail_mv = sb("tail_mv", [P, 2, TAIL_ROWS, 2], fp32)
        tail_inv = sb("tail_inv", [P, 2, TAIL_ROWS], fp32)
        tail_shift = sb("tail_shift", [P, 2, TAIL_ROWS], fp32)

        work = down_w[:, EXPERTS // 2:, :].rearrange("p e n -> p (e n)").bitcast(bf16)
        used = [0]

        def carve(n):
            used[0] += n
            return work[:, used[0] - n:used[0]]

        def carve2(n):
            return carve(2 * n).rearrange("p (b n) -> p b n", b=2)

        W = ROW_TILES * DIM
        x_in, x_again, x1 = carve2(W), carve2(W), carve2(W)
        q_sb, k_sb, v_sb = carve2(W), carve2(W), carve2(W)
        xn, xnT, oo, yT, xfT = carve(W), carve(W), carve(W), carve(W), carve(W)
        probs, probsT = carve(4 * SEQ), carve(4 * SEQ)

        def rows(ap):
            return ap.rearrange("p (t d) -> p t d", t=ROW_TILES)

        gated = stage[:, 0:FFN].rearrange("p (a n) -> p a n", a=2)
        hidden = stage[:, FFN:2 * FFN].rearrange("p (a n) -> p a n", a=2)
        reached = stage[0:1, 0:MOE_TILES * EXPERTS].rearrange("p (j e) -> p j e", e=EXPERTS)
        passed = stage[0:1, MOE_TILES * EXPERTS:2 * MOE_TILES * EXPERTS].rearrange("p (j e) -> p j e", e=EXPERTS)
        filled = stage[0:1, 0:EXPERTS * 32].rearrange("p (e i) -> p e i", i=32)
        TW = TAIL_ROWS * DIM
        over = gu_w[:, :, :].rearrange("p a n -> p (a n)")
        tail_y = over[:, 0:TAIL_GROUPS * 2 * TW * 2].bitcast(fp32).rearrange(
            "p (g k r d) -> p g k r d", g=TAIL_GROUPS, k=TOP_K, d=DIM)
        tail_x = over[:, TAIL_GROUPS * 4 * TW:TAIL_GROUPS * 5 * TW].rearrange(
            "p (g r d) -> p g r d", g=TAIL_GROUPS, d=DIM)
        tail_xs = over[:, TAIL_GROUPS * 5 * TW:TAIL_GROUPS * 5 * TW + 4 * TW].bitcast(fp32).rearrange(
            "p (g r d) -> p g r d", g=2, d=DIM)

        bank = [pb(f"bank{n}") for n in range(8)]
        ps_xT = bank[0][:, :].bitcast(bf16)[:, 0:512].rearrange("p (c t) -> p c t", c=CHUNKS)
        ps_xfT = bank[0][:, :].bitcast(bf16)[:, 512:1024].rearrange("p (c t) -> p c t", c=CHUNKS)
        ps_q, ps_k = bank[1][:, :], bank[2][:, :]
        ps_s = [bank[3][:, :], bank[4][:, :]]
        ps_pT = bank[5][:, :].bitcast(bf16)
        ps_y = bank[6][:, :]
        ps_o = bank[7][:, :]
        ps_logits = bank[7][:, 0:ROW_TILES * EXPERTS]
        ps_place = bank[7][:, 64:64 + ROW_TILES * EXPERTS]
        ps_total = bank[7][:, 128:128 + EXPERTS]
        ps_gate, ps_up = [bank[0], bank[2]], [bank[1], bank[3]]
        ps_hT, ps_out, ps_x = [bank[4], bank[5]], bank[6], bank[7]

        s_const = sem("s_const")
        s_ident = sem("s_ident")
        s_attn_w = sem("s_attn_w")
        s_small = sem("s_small")
        s_prep = sem("s_prep")
        s_router = sem("s_router")
        s_x = [sem(f"s_x_in{n}") for n in range(2)]
        s_xa = [sem(f"s_x_again{n}") for n in range(2)]
        s_xn = sem("s_xn")
        s_xT_ps = sem("s_xT_ps")
        s_xT = sem("s_xT")
        s_var = [sem(f"s_var{n}") for n in range(3)]
        s_root = [sem(f"s_root{n}") for n in range(3)]
        s_paced = sem("s_paced")
        s_tvar, s_troot = sem("s_tvar"), sem("s_troot")
        s_q_ps, s_k_ps, s_v_ps = sem("s_q_ps"), sem("s_k_ps"), sem("s_v_ps")
        s_q_raw, s_k_raw, s_v_raw = sem("s_q_raw"), sem("s_k_raw"), sem("s_v_raw")
        s_q, s_k, s_v = sem("s_q"), sem("s_k"), sem("s_v")
        s_v_sum = sem("s_v_sum")
        s_s_ps, s_s = sem("s_s_ps"), sem("s_s")
        s_sub, s_exp, s_p = sem("s_sub"), sem("s_exp"), sem("s_p")
        s_pT_ps, s_pT = sem("s_pT_ps"), sem("s_pT")
        s_y_ps, s_y = sem("s_y_ps"), sem("s_y")
        s_o_ps, s_o = sem("s_o_ps"), sem("s_o")
        s_x1, s_x1_saved = sem("s_x1"), [sem(f"s_x1_saved{n}") for n in range(2)]
        s_xf, s_xfT_ps, s_xfT = sem("s_xf"), sem("s_xfT_ps"), sem("s_xfT")
        s_lg_ps, s_mask = sem("s_lg_ps"), sem("s_mask")
        s_gap, s_gexp = sem("s_gap"), sem("s_gexp")
        s_place_ps, s_slot = sem("s_place_ps"), sem("s_slot")
        s_sent = [sem(f"s_sent{n}") for n in range(2)]
        s_stage, s_hi, s_r1, s_mid, s_lo = sem("s_stage"), sem("s_hi"), sem("s_r1"), sem("s_mid"), sem("s_lo")
        s_down = sem("s_down")
        c_ln1, c_sm, c_out, c_rt = sem("c_ln1"), sem("c_sm"), sem("c_out"), sem("c_rt")
        s_total_ps, s_pad, s_pad_sent, s_table = sem("s_total_ps"), sem("s_pad"), sem("s_pad_sent"), sem("s_table")
        c_tab = sem("c_tab")
        s_pay = [sem(f"s_pay{n}") for n in range(3)]
        s_xrow_ps, s_xrow, s_meta = sem("s_xrow_ps"), sem("s_xrow"), sem("s_meta")
        s_gu = [sem("s_gu0"), sem("s_gu1")]
        s_gated = [sem("s_gated0"), sem("s_gated1")]
        s_h = [sem("s_h0"), sem("s_h1")]
        s_hT_ps = [sem("s_hT_ps0"), sem("s_hT_ps1")]
        s_hT = [sem("s_hT0"), sem("s_hT1")]
        s_out_ps, s_out = sem("s_out_ps"), sem("s_out")
        s_scat = [sem(f"s_scat{n}") for n in range(3)]
        s_ty = [sem(f"s_ty{n}") for n in range(TAIL_GROUPS)]
        s_tx = [sem(f"s_tx{n}") for n in range(TAIL_GROUPS)]
        c_tail = sem("c_tail")
        s_tshift, s_txs, s_tdone = sem("s_tshift"), sem("s_txs"), sem("s_tdone")
        s_stored = sem("s_stored")

        def wait(eng, semaphore, value):
            if isinstance(value, int) and value <= 0:
                return
            eng.wait_ge(semaphore, value)

        def chain(eng, semaphore, start):
            n = [0]

            def link(ins):
                n[0] += 1
                ins.then_inc(semaphore, 1)
                eng.wait_ge(semaphore, start + n[0])
            return link, n

        def attention_rounds(eng, round_):
            for i in range(4):
                round_(i, i % 2)
            with eng.Fori(2, BATCHES // 2) as pair:
                round_(2 * pair, 0)
                round_(2 * pair + 1, 1)
            round_(BATCHES, 0)
            round_(BATCHES + 1, 1)

        def has(i, lag):
            return not isinstance(i, int) or 0 <= i - lag < BATCHES

        def expert_tiles(eng, tile):
            for j in range(4):
                tile(j, j % 3)
            with eng.Fori(1, (MOE_TILES - 2) // 3) as r:
                for n in range(3):
                    tile(3 * r + 1 + n, (1 + n) % 3)
            tile(MOE_TILES - 1, (MOE_TILES - 1) % 3)
        assert (MOE_TILES - 2) % 3 == 0

        block = ctx.enter_context(nc.Block())

        @block.sync
        def _(sp):
            base_rows = base.rearrange("b (t p) d -> b p t d", p=P)
            for n, w in enumerate((wqT, wkT, wvT, woT)):
                sp.dma_start(attn_w[:, n, :, :], w.rearrange("(c p) n -> p c n", p=P)).then_inc(s_attn_w, 16)

            def load_x(b, buf):
                if not (isinstance(b, int) and b < 2):
                    wait(sp, s_xn, b - 1)
                sp.dma_start(rows(x_in[:, buf, :]), base_rows[b]).then_inc(s_x[buf], 16)

            load_x(0, 0)
            sp.dma_start(qk_bias[:, 0, :], bq.rearrange("(h p) -> p h", p=P),
                         allow_slow_non_contiguous=True).then_inc(s_small, 16)
            sp.dma_start(qk_bias[:, 1, :], bk.rearrange("(h p) -> p h", p=P),
                         allow_slow_non_contiguous=True).then_inc(s_small, 16)
            sp.dma_start(row_bias[:, 0, :], bv.rearrange("(a d) -> a d", a=1).to_broadcast([P, DIM])
                         ).then_inc(s_small, 16)
            sp.dma_start(row_bias[:, 1, :], bo.rearrange("(a d) -> a d", a=1).to_broadcast([P, DIM])
                         ).then_inc(s_small, 16)
            sp.dma_start(router32[:, :, :], routerT.rearrange("(c p) e -> p c e", p=P)).then_inc(s_small, 16)
            load_x(1, 1)

            def round_(i, par):
                if has(i, 2):
                    wait(sp, s_x1, i - 2)
                    sp.dma_start(rows(x_again[:, par, :]), base_rows[i - 2]).then_inc(s_xa[par], 16)
                if has(i, 0):
                    wait(sp, s_lo, i)
                    sp.dma_start(stage[:, :], gate_up[i]).then_inc(s_stage, 16)
                if has(i, 2):
                    wait(sp, s_x1, i - 1)
                    sp.dma_start(residual[bass.ds((i - 2) * SEQ, SEQ), :].rearrange("(t p) d -> p t d", p=P),
                                 rows(x1[:, par, :])).then_inc(s_x1_saved[par], 16)

            round_(0, 0)
            round_(1, 1)
            sp.dma_start(down_w[:, 0:EXPERTS // 2, :], down[0:EXPERTS // 2, :, :].rearrange("e p n -> p e n")
                         ).then_inc(s_down, 16)
            for i in (2, 3):
                load_x(i, i % 2)
                round_(i, i % 2)
            with sp.Fori(2, BATCHES // 2) as pair:
                load_x(2 * pair, 0)
                round_(2 * pair, 0)
                load_x(2 * pair + 1, 1)
                round_(2 * pair + 1, 1)
            round_(BATCHES, 0)
            round_(BATCHES + 1, 1)

            sp.wait_ge(s_table, 2)
            for n in range(2):
                sp.wait_ge(s_x1_saved[n], 16 * BATCHES // 2)
            sp.wait_ge(s_lg_ps, BATCHES)
            sp.dma_start(down_w[:, EXPERTS // 2:, :], down[EXPERTS // 2:, :, :].rearrange("e p n -> p e n")
                         ).then_inc(s_down, 16)

            for n in range(2):
                sp.wait_ge(s_sent[n], 16 * ROW_TILES * TOP_K * BATCHES // 2)
            sp.wait_ge(s_pad_sent, 16 * (EXPERTS + 1))

            def load_rows(j, buf):
                if not (isinstance(j, int) and j < 3):
                    wait(sp, s_meta, j - 2)
                row = sp.value_load(table[0:1, 0, bass.ds(j, 1)], min_val=0, max_val=DUMMY_ROW)
                sp.dma_start(payload[:, buf, :], dispatched[bass.ds(row, P), :]).then_inc(s_pay[buf], 16)
            for j in range(3):
                load_rows(j, j)
            with sp.Fori(1, MOE_TILES // 3) as r:
                for n in range(3):
                    load_rows(3 * r + n, n)
            for j in range(MOE_TILES // 3 * 3, MOE_TILES):
                load_rows(j, j % 3)

            tok = residual.rearrange("(g p r) d -> g p r d", p=P, r=TAIL_ROWS)
            eo = expert_out.rearrange("(k g p r) d -> g p k r d", k=TOP_K, p=P, r=TAIL_ROWS)
            of = out.rearrange("(g p r) d -> g p r d", p=P, r=TAIL_ROWS)
            sp.wait_ge(s_gu[1], MOE_TILES)
            for g in range(TAIL_GROUPS):
                sp.dma_start(tail_x[:, g], tok[g]).then_inc(s_tx[g], 16)
            for n in range(3):
                sp.wait_ge(s_scat[n], 16 * len(range(n, MOE_TILES, 3)))
            for g in range(TAIL_GROUPS):
                for k in range(TOP_K):
                    sp.dma_start(tail_y[:, g, k], eo[g, :, k]).then_inc(s_ty[g], 16)
            for g in range(TAIL_GROUPS):
                sp.wait_ge(s_tdone, g + 1)
                sp.dma_start(of[g], tail_y[:, g, 0]).then_inc(s_stored, 16)
            sp.wait_ge(s_stored, 16 * TAIL_GROUPS)

        @block.gpsimd
        def _(pool):
            pool.memset(ones[:, :], 1.0).then_inc(s_const, 1)
            pool.memset(half[:, :], 0.5).then_inc(s_const, 1)
            pool.memset(minus_half[:, :], -0.5).then_inc(s_const, 1)
            pool.memset(ident[:, :], 0.0).then_inc(s_ident, 1)
            pool.memset(identf[:, :], 0.0).then_inc(s_ident, 1)
            pool.memset(before[:, :], 1.0).then_inc(s_ident, 1)
            pool.memset(lower[:, :, :], 1.0).then_inc(s_ident, 1)
            pool.memset(pad_row[:, :], 0).then_inc(s_ident, 1)
            pool.wait_ge(s_ident, 5)
            for m in (ident, identf):
                pool.affine_select(out=m[:, :], in_=m[:, :], compare_op=ALU.not_equal, fill=1.0, base=0,
                                   pattern=[[-1, P]], channel_multiplier=1).then_inc(s_const, 1)
            pool.affine_select(out=before[:, :], in_=before[:, :], compare_op=ALU.is_gt, fill=0.0, base=0,
                               pattern=[[1, P]], channel_multiplier=-1).then_inc(s_const, 1)
            pool.affine_select(out=lower[:, :, :], in_=lower[:, :, :], compare_op=ALU.is_gt, fill=0.0, base=0,
                               pattern=[[1, EXPERTS], [-1, EXPERTS]], channel_multiplier=0).then_inc(s_const, 1)
            pool.memset(pad_row[:, DIM // 2:DIM // 2 + 1], NOWHERE).then_inc(s_const, 1)
            pool.memset(count[:, 0, :], 0.0).then_inc(s_const, 1)
            pool.iota(dest[:, :, :], pattern=[[P, ROW_TILES], [TOKENS, TOP_K]], base=0,
                      channel_multiplier=1).then_inc(s_const, 1)
            pool.iota(region_start[:, :], pattern=[[REGION, EXPERTS]], base=0, channel_multiplier=0,
                      allow_small_or_imprecise_dtypes=True).then_inc(s_const, 1)
            pool.iota(pad_place[:, :], pattern=[[REGION, EXPERTS]], base=0, channel_multiplier=1,
                      allow_small_or_imprecise_dtypes=True).then_inc(s_const, 1)
            pool.iota(tile_first[:, :], pattern=[[P, 32]], base=0, channel_multiplier=0,
                      allow_small_or_imprecise_dtypes=True).then_inc(s_const, 1)
            pool.iota(tile_no[:, :], pattern=[[1, MOE_TILES]], base=0, channel_multiplier=0,
                      allow_small_or_imprecise_dtypes=True).then_inc(s_const, 1)
            pool.wait_ge(s_const, CONSTS)
            pool.dma_start(dispatched[DUMMY_ROW:DUMMY_ROW + P, :], pad_row[:, :]).then_inc(s_pad_sent, 16)

            last_row, last_slot = pool.to_reg(DUMMY_ROW - 1), pool.to_reg(SLOTS - 1)

            def carry_wait(earlier):
                wait(pool, s_paced, earlier)
                pool.tensor_tensor(pace[:, :], half[:, 0:1], half[:, 0:1], ALU.mult).then_inc(s_paced, 1)

            def dispatch(b, par):
                pool.wait_ge(s_slot, b + 1)
                carry_wait(b)
                for t in range(ROW_TILES):
                    for k in range(TOP_K):
                        n = t * TOP_K + k
                        pool.indirect_dma_start(
                            out=dispatched, out_offset=bass.IndirectOffsetOnAxis(ap=slot[:, par, n:n + 1], axis=0),
                            in_=payload[:, par * 4 + n, :], in_offset=None,
                            bounds_check=last_row, oob_is_err=False).then_inc(s_sent[par], 16)
            def root(which, b):
                pool.wait_ge(s_var[which], b + 1)
                pool.tensor_tensor(ln_std[:, which, :], ln_var[:, which, :], half[:, :], ALU.pow
                                   ).then_inc(s_root[which], 1)

            def round_(i, par):
                if has(i, 0):
                    root(0, i)
                if has(i, 2):
                    root(1, i - 2)
                    root(2, i - 2)
                if has(i, 3):
                    dispatch(i - 3, 1 - par)
            for i in range(3):
                round_(i, i % 2)
            round_(3, 1)
            with pool.Fori(2, BATCHES // 2) as pair:
                round_(2 * pair, 0)
                round_(2 * pair + 1, 1)
            for i in range(BATCHES, BATCHES + 3):
                round_(i, i % 2)

            pool.wait_ge(s_pad, 1)
            for e in range(EXPERTS):
                pool.indirect_dma_start(
                    out=dispatched, out_offset=bass.IndirectOffsetOnAxis(ap=pad_slot[:, e:e + 1], axis=0),
                    in_=pad_row[:, :], in_offset=None,
                    bounds_check=last_row, oob_is_err=False).then_inc(s_pad_sent, 16)

            def send_back(j, buf):
                pool.wait_ge(s_out, j + 1)
                carry_wait(BATCHES + j)
                pool.indirect_dma_start(
                    out=expert_out, out_offset=bass.IndirectOffsetOnAxis(ap=meta[:, buf, 0:1], axis=0),
                    in_=y_buf[:, buf, :], in_offset=None,
                    bounds_check=last_slot, oob_is_err=False).then_inc(s_scat[buf], 16)
            expert_tiles(pool, send_back)

            for g in range(TAIL_GROUPS):
                pool.wait_ge(s_tvar, g + 1)
                pool.tensor_tensor(tail_inv[:, g % 2, :], tail_var[:, g % 2, :], minus_half[:, :], ALU.pow
                                   ).then_inc(s_troot, 1)

        @block.scalar
        def _(act):
            act.wait_ge(s_small, 16 * 5)
            act.activation(qk_biasf[:, :, :], qk_bias[:, :, :], ACT.Copy).then_inc(s_prep, 1)

            def round_(i, par):
                other = 1 - par
                if has(i, 2):
                    act.wait_ge(s_o_ps, i - 1)
                    wait(act, s_xf, i - 2)
                    act.activation(oo[:, :], ps_o, ACT.Copy).then_inc(s_o, 1)
                if has(i, 1):
                    wait(act, s_pT_ps, i - 1)
                    for n in range(2):
                        act.wait_ge(s_s_ps, 2 * i - 1 + n)
                        act.activation(probs[:, n * 512:(n + 1) * 512], ps_s[n], ACT.Copy).then_inc(s_s, 1)
                    act.wait_ge(s_sub, i)
                    act.activation(probs[:, :], probs[:, :], ACT.Exp).then_inc(s_exp, 1)
                if has(i, 0):
                    act.wait_ge(s_xT_ps, i + 1)
                    wait(act, s_v_ps, i)
                    act.activation(xnT[:, :], ps_xT.rearrange("p c t -> p (c t)"), ACT.Copy).then_inc(s_xT, 1)
                    wait(act, s_s_ps, 2 * (i - 1))
                    for raw, ps, dst, done in ((s_q_ps, ps_q, q_sb, s_q_raw), (s_k_ps, ps_k, k_sb, s_k_raw)):
                        act.wait_ge(raw, i + 1)
                        act.activation(dst[:, par, :], ps, ACT.Copy).then_inc(done, 1)
                    wait(act, s_y_ps, i - 1)
                    act.wait_ge(s_v_ps, i + 1)
                    act.activation(v_sb[:, par, :], ps_q, ACT.Copy).then_inc(s_v_raw, 1)
                    act.wait_ge(s_stage, 16 * (i + 1))
                    act.activation(gu_w[:, bass.ds(i * PARTS, 1), :].rearrange("p a n -> p (a n)"),
                                   stage[:, :], ACT.Copy).then_inc(s_hi, 1)
                if has(i, 1):
                    act.wait_ge(s_y_ps, i)
                    wait(act, s_o_ps, i - 1)
                    act.activation(yT[:, :], ps_y, ACT.Copy).then_inc(s_y, 1)
                if has(i, 2):
                    act.wait_ge(s_xfT_ps, i - 1)
                    wait(act, s_lg_ps, i - 2)
                    act.activation(xfT[:, :], ps_xfT.rearrange("p c t -> p (c t)"), ACT.Copy).then_inc(s_xfT, 1)
                if has(i, 0):
                    act.wait_ge(s_r1, i + 1)
                    act.activation(gu_w[:, bass.ds(i * PARTS + 1, 1), :].rearrange("p a n -> p (a n)"),
                                   stage[:, :], ACT.Copy).then_inc(s_mid, 1)
                if has(i, 2):
                    act.wait_ge(s_gap, i - 1)
                    act.activation(gap_exp[:, :], gap[:, :], ACT.Exp).then_inc(s_gexp, 1)
            attention_rounds(act, round_)

            def weighted_out(j, buf, sent):
                act.wait_ge(s_out_ps, j + 1)
                act.wait_ge(s_meta, j + 1)
                wait(act, s_scat[buf], sent)
                act.activation(y_buf[:, buf, :], ps_out[:, 0:DIM], ACT.Copy,
                               scale=meta[:, buf, 1:2].bitcast(fp32)).then_inc(s_out, 1)

            def tile(j):
                for n in range(2):
                    act.wait_ge(s_gu[n], j + 1)
                    wait(act, s_h[n], j)
                    act.activation(gated[:, n, :], ps_gate[n][:, 0:HALF], ACT.Silu).then_inc(s_gated[n], 1)

            tile(0)
            for n in range(3):
                tile(1 + n)
                weighted_out(n, n, 0)
            with act.Fori(1, (MOE_TILES - 2) // 3) as r:
                for n in range(3):
                    tile(3 * r + 1 + n)
                    weighted_out(3 * r + n, n, 16 * r)
            last = MOE_TILES - 1
            tile(last)
            for j in (last - 1, last):
                weighted_out(j, j % 3, 16 * (j // 3))

            for g in range(TAIL_GROUPS):
                act.wait_ge(s_tx[g], 16)
                act.wait_ge(s_tshift, g + 1)
                wait(act, s_tdone, g - 1)
                for r in range(TAIL_ROWS):
                    ins = act.activation(tail_xs[:, g % 2, r, :], tail_x[:, g, r, :], ACT.Identity,
                                         bias=tail_shift[:, g % 2, r:r + 1])
                ins.then_inc(s_txs, 1)

        @block.tensor
        def _(pe):
            pe.wait_ge(s_const, CONSTS)
            pe.wait_ge(s_attn_w, 16 * 4)

            def transpose_rows(dst, src):
                for c in range(CHUNKS):
                    for t in range(ROW_TILES):
                        last = pe.transpose(dst[:, c, t * P:(t + 1) * P], src(t, c), ident[:, :])
                return last

            def round_(i, par):
                other = 1 - par
                xT3 = xnT[:, :].rearrange("p (c t) -> p c t", c=CHUNKS)
                if has(i, 2):
                    pe.wait_ge(s_y, i - 1)
                    wait(pe, s_slot, i - 2)
                    y3 = yT[:, :].rearrange("p (c t) -> p c t", c=CHUNKS)
                    for t in range(ROW_TILES):
                        for c in range(CHUNKS):
                            last = pe.matmul(ps_o[:, t * DIM:(t + 1) * DIM], y3[:, c, t * P:(t + 1) * P],
                                             attn_w[:, 3, c, :], start=(c == 0), stop=(c == CHUNKS - 1))
                    last.then_inc(s_o_ps, 1)
                if has(i, 1):
                    pe.wait_ge(s_q, i)
                    pe.wait_ge(s_k, i)
                    wait(pe, s_s, 2 * (i - 1))
                    for h in range(HEADS):
                        for t in range(ROW_TILES):
                            last = pe.matmul(ps_s[h][:, t * SEQ:(t + 1) * SEQ],
                                             q_sb[:, other, h * SEQ + t * P:h * SEQ + (t + 1) * P],
                                             k_sb[:, other, h * SEQ:(h + 1) * SEQ], start=True, stop=True)
                        last.then_inc(s_s_ps, 1)
                if has(i, 0):
                    pe.wait_ge(s_xn, i + 1)
                    wait(pe, s_xT, i)
                    transpose_rows(ps_xT, lambda t, c: xn[:, t * DIM + c * P:t * DIM + (c + 1) * P]
                                   ).then_inc(s_xT_ps, 1)
                    pe.wait_ge(s_xT, i + 1)
                    for n, ps, done, before_ in ((0, ps_q, s_q_ps, s_v_raw), (1, ps_k, s_k_ps, s_k_raw)):
                        wait(pe, before_, i)
                        for h in range(HEADS):
                            for c in range(CHUNKS):
                                last = pe.matmul(ps[:, h * SEQ:(h + 1) * SEQ],
                                                 attn_w[:, n, c, h * HEAD_DIM:(h + 1) * HEAD_DIM],
                                                 xT3[:, c, :], start=(c == 0), stop=(c == CHUNKS - 1))
                        last.then_inc(done, 1)
                    pe.wait_ge(s_q_raw, i + 1)
                    for t in range(ROW_TILES):
                        for c in range(CHUNKS):
                            last = pe.matmul(ps_q[:, t * DIM:(t + 1) * DIM], xT3[:, c, t * P:(t + 1) * P],
                                             attn_w[:, 2, c, :], start=(c == 0), stop=(c == CHUNKS - 1))
                    last.then_inc(s_v_ps, 1)
                if has(i, 1):
                    pe.wait_ge(s_p, i)
                    wait(pe, s_pT, i - 1)
                    for h in range(HEADS):
                        for kt in range(ROW_TILES):
                            for t in range(ROW_TILES):
                                o = (h * ROW_TILES + kt) * SEQ + t * P
                                s = (h * ROW_TILES + t) * SEQ + kt * P
                                last = pe.transpose(ps_pT[:, o:o + P], probs[:, s:s + P], ident[:, :])
                    last.then_inc(s_pT_ps, 1)
                    pe.wait_ge(s_pT, i)
                    pe.wait_ge(s_v, i)
                    wait(pe, s_y, i - 1)
                    for h in range(HEADS):
                        for kt in range(ROW_TILES):
                            o = (h * ROW_TILES + kt) * SEQ
                            last = pe.matmul(ps_y[:, h * SEQ:(h + 1) * SEQ],
                                             v_sb[:, other, kt * DIM + h * HEAD_DIM:kt * DIM + (h + 1) * HEAD_DIM],
                                             probsT[:, o:o + SEQ], start=(kt == 0), stop=(kt == ROW_TILES - 1))
                    last.then_inc(s_y_ps, 1)
                if has(i, 2):
                    pe.wait_ge(s_xf, i - 1)
                    wait(pe, s_xfT, i - 2)
                    transpose_rows(ps_xfT, lambda t, c: payload[:, par * 4 + t * TOP_K, c * 64:(c + 1) * 64]
                                   .bitcast(bf16)).then_inc(s_xfT_ps, 1)
                    pe.wait_ge(s_xfT, i - 1)
                    pe.wait_ge(s_router, 1)
                    f3 = xfT[:, :].rearrange("p (c t) -> p c t", c=CHUNKS)
                    for t in range(ROW_TILES):
                        for n in range(CHUNKS * PARTS):
                            c, part = n % CHUNKS, n // CHUNKS
                            last = pe.matmul(ps_logits[:, t * EXPERTS:(t + 1) * EXPERTS],
                                             f3[:, c, t * P:(t + 1) * P], router_w[:, part, c, :],
                                             start=(n == 0), stop=(n == CHUNKS * PARTS - 1))
                    last.then_inc(s_lg_ps, 1)
                    pe.wait_ge(s_mask, i - 1)
                    for t in range(ROW_TILES):
                        dst = ps_place[:, t * EXPERTS:(t + 1) * EXPERTS]
                        pe.matmul(dst, before[:, :], mask[:, t, :], start=True, stop=False)
                        for u in range(t):
                            pe.matmul(dst, ones[:, :], mask[:, u, :], start=False, stop=False)
                        last = pe.matmul(dst, ones[:, :], count[:, par, :], start=False, stop=True)
                    last.then_inc(s_place_ps, 1)
            attention_rounds(pe, round_)

            pe.wait_ge(s_slot, BATCHES)
            pe.matmul(ps_total, ones[:, :], count[:, 0, :], start=True, stop=True).then_inc(s_total_ps, 1)

            def rows_transposed(j, buf, uses):
                pe.wait_ge(s_pay[buf], uses)
                wait(pe, s_xrow, j)
                psx = ps_x[:, :].bitcast(bf16)
                for c in range(CHUNKS):
                    last = pe.transpose(psx[:, c * P:(c + 1) * P],
                                        payload[:, buf, c * 64:(c + 1) * 64].bitcast(bf16), ident[:, :])
                last.then_inc(s_xrow_ps, 1)

            def gate_up_half(j, buf, n, first):
                if n == 0:
                    pe.wait_ge(s_xrow, j + 1)
                wait(pe, s_h[n], j)
                for m in range(CHUNKS * PARTS):
                    c = m // PARTS
                    for at, ps in ((0, ps_gate[n]), (FFN, ps_up[n])):
                        last = pe.matmul(ps[:, 0:HALF], xT_buf[:, buf, c, :],
                                         gu_w[:, bass.ds(first + m, 1), at + n * HALF:at + (n + 1) * HALF]
                                         .rearrange("p a n -> p (a n)"),
                                         start=(m == 0), stop=(m == CHUNKS * PARTS - 1))
                last.then_inc(s_gu[n], 1)

            def hidden_transposed(j, n):
                pe.wait_ge(s_h[n], j + 1)
                wait(pe, s_hT[n], j)
                for m, size in enumerate(PIECES):
                    last = pe.transpose(ps_hT[n][0:size, m * P:(m + 1) * P],
                                        hidden[:, n, m * P:m * P + size], identf[:, :])
                last.then_inc(s_hT_ps[n], 1)

            def down_half(j, n, expert):
                pe.wait_ge(s_hT[n], j + 1)
                if n == 0:
                    wait(pe, s_out, j)
                for m, size in enumerate(PIECES):
                    at = (3 * n + m) * DIM
                    last = pe.matmul(ps_out[:, 0:DIM], hT[0:size, n, m, :],
                                     down_w[0:size, bass.ds(expert, 1), at:at + DIM]
                                     .rearrange("p a n -> p (a n)"),
                                     start=(n == 0 and m == 0), stop=(n == 1 and m == 2))
                if n == 1:
                    last.then_inc(s_out_ps, 1)

            def expert_of(j):
                return pe.value_load(table[0:1, 1, bass.ds(j, 1)], min_val=0, max_val=EXPERTS - 1)

            def tile(j, buf, last_tile, expert, before_expert, uses):
                first = expert * (CHUNKS * PARTS)
                gate_up_half(j, buf, 0, first)
                if before_expert is not None:
                    hidden_transposed(j - 1, 1)
                    down_half(j - 1, 0, before_expert)
                if not last_tile:
                    rows_transposed(j + 1, (buf + 1) % 3, uses)
                gate_up_half(j, buf, 1, first)
                hidden_transposed(j, 0)
                if before_expert is not None:
                    down_half(j - 1, 1, before_expert)

            pe.wait_ge(s_table, 2)
            rows_transposed(0, 0, 16)
            pe.wait_ge(s_lo, BATCHES)
            e0 = expert_of(0)
            tile(0, 0, False, e0, None, 16)
            pe.wait_ge(s_down, 16 * 2)

            def three_tiles(r):
                es = [expert_of(3 * r + n) for n in range(4)]
                for n in range(3):
                    uses = 16 * (r + 1) if n == 0 else 16 * (r + 2)
                    tile(3 * r + 1 + n, (1 + n) % 3, False, es[n + 1], es[n], uses)
            three_tiles(0)
            with pe.Fori(1, (MOE_TILES - 2) // 3) as r:
                three_tiles(r)
            last = MOE_TILES - 1
            e1 = expert_of(last - 1)
            e2 = expert_of(last)
            tile(last, last % 3, True, e2, e1, 0)
            hidden_transposed(last, 1)
            down_half(last, 0, e2)
            down_half(last, 1, e2)

        @block.vector
        def _(dve):
            n_prep = [0]

            def prep(ins):
                n_prep[0] += 1
                ins.then_inc(s_prep, 1)
                dve.wait_ge(s_prep, n_prep[0] + 1)
            dve.wait_ge(s_small, 16 * 5)
            dve.wait_ge(s_const, CONSTS)
            prep(dve.tensor_copy(router_w[:, 0], router32[:, :, :]))
            prep(dve.tensor_tensor(router32[:, :, :], router32[:, :, :], router_w[:, 0], ALU.subtract))
            prep(dve.tensor_copy(router_w[:, 1], router32[:, :, :]))
            dve.tensor_tensor(router_w[:, 2], router32[:, :, :], router_w[:, 1], ALU.subtract).then_inc(s_router, 1)

            def norm_stats(link, which, src):
                for t in range(ROW_TILES):
                    ins = dve.bn_stats(ln_stats[:, which, t, :], src[:, t, :])
                link(ins)
                dve.tensor_tensor(ln_sum[:, which, :], ln_stats[:, which, :, 1], ln_stats[:, which, :, 4], ALU.add)
                for t in range(ROW_TILES):
                    ins = dve.bn_aggr(ln_mv[:, which, t, :], ln_stats[:, which, t, :])
                link(ins)
                dve.tensor_scalar(ln_mean[:, which, :], ln_sum[:, which, :], 0.5, None, ALU.mult)
                dve.tensor_scalar(ln_var[:, which, :], ln_mv[:, which, :, 1], EPS_BF16, None, ALU.add
                                  ).then_inc(s_var[which], 1)

            def norm_rows(link, which, b, src, dsts, centred):
                dve.wait_ge(s_root[which], b + 1)
                link(dve.reciprocal(ln_inv[:, which, :], ln_std[:, which, :]))
                for t in range(ROW_TILES):
                    ins = dve.tensor_scalar(centred[:, t, :], src[:, t, :], ln_mean[:, which, t:t + 1],
                                            None, ALU.subtract)
                link(ins)
                for d in dsts:
                    for t in range(ROW_TILES):
                        ins = dve.tensor_scalar(d(t), centred[:, t, :], ln_inv[:, which, t:t + 1], None, ALU.mult)
                return ins

            def softmax_differences(i, other, link):
                dve.wait_ge(s_s, 2 * i)
                link(dve.tensor_scalar(probs[:, :], probs[:, :], SCALE_BF16, None, ALU.mult))
                p4 = probs[:, :].rearrange("p (u n) -> p u n", u=4)
                link(dve.tensor_reduce(sm_max[:, :], p4, AX.X, ALU.max))
                for u in range(4):
                    ins = dve.tensor_scalar(p4[:, u, :], p4[:, u, :], sm_max[:, u:u + 1], None, ALU.subtract)
                ins.then_inc(s_sub, 1)

            def softmax_quotients(i, link):
                dve.wait_ge(s_exp, i)
                p4 = probs[:, :].rearrange("p (u n) -> p u n", u=4)
                link(dve.tensor_reduce(sm_total[:, :], p4, AX.X, ALU.add))
                link(dve.tensor_copy(sm_sum[:, :], sm_total[:, :]))
                link(dve.reciprocal(sm_inv[:, :], sm_sum[:, :]))
                for u in range(4):
                    ins = dve.tensor_scalar(p4[:, u, :], p4[:, u, :], sm_inv[:, u:u + 1], None, ALU.mult)
                ins.then_inc(s_p, 1)

            def projections(i, par):
                for n, (dst, raw, done) in enumerate(((q_sb, s_q_raw, s_q), (k_sb, s_k_raw, s_k))):
                    dve.wait_ge(raw, i + 1)
                    for h in range(HEADS):
                        d = dst[:, par, h * SEQ:(h + 1) * SEQ]
                        ins = dve.tensor_scalar(d, d, qk_biasf[:, n, h:h + 1], 0.0, ALU.add, ALU.max)
                    ins.then_inc(done, 1)
                dve.wait_ge(s_v_raw, i + 1)
                v = rows(v_sb[:, par, :])
                dve.tensor_tensor(v, v, row_bias[:, 0:1, :].to_broadcast([P, ROW_TILES, DIM]), ALU.add
                                  ).then_inc(s_v_sum, 1)
                dve.wait_ge(s_v_sum, i + 1)
                dve.tensor_scalar(v, v, 0.0, None, ALU.max).then_inc(s_v, 1)

            def output_bias(i, link):
                dve.wait_ge(s_o, i - 1)
                o = rows(oo[:, :])
                link(dve.tensor_tensor(o, o, row_bias[:, 1:2, :].to_broadcast([P, ROW_TILES, DIM]), ALU.add))
                link(dve.tensor_scalar(o, o, 0.0, None, ALU.max))
                norm_stats(link, 1, o)

            def residual_sum(i, par, pair, link):
                o = rows(oo[:, :])
                link(norm_rows(link, 1, i - 2, o, [lambda t: o[:, t, :]], o))
                dve.wait_ge(s_xa[par], 16 * pair)
                wait(dve, s_x1_saved[par], 16 * (pair - 1))
                z = rows(x1[:, par, :])
                dve.tensor_tensor(z, rows(x_again[:, par, :]), o, ALU.add).then_inc(s_x1, 1)
                dve.wait_ge(s_x1, i - 1)
                norm_stats(link, 2, z)

            def expert_input(i, par, pair, link):
                wait(dve, s_sent[par], 16 * ROW_TILES * TOP_K * (pair - 1))
                norm_rows(link, 2, i - 2, rows(x1[:, par, :]), [
                    (lambda t, k=k: payload[:, par * 4 + t * TOP_K + k, 0:DIM // 2].bitcast(bf16))
                    for k in range(TOP_K)], rows(oo[:, :])).then_inc(s_xf, 1)

            def route(i, par, link):
                dve.wait_ge(s_lg_ps, i - 1)
                link(dve.tensor_copy(logits[:, :, :], ps_logits.rearrange("p (t e) -> p t e", t=ROW_TILES)))
                for t in range(ROW_TILES):
                    mine = logits[:, t, :].unsqueeze(2).to_broadcast([P, EXPERTS, EXPERTS])
                    theirs = logits[:, t, :].unsqueeze(1).to_broadcast([P, EXPERTS, EXPERTS])
                    dve.tensor_tensor(above[:, t], theirs, mine, ALU.is_gt)
                    ins = dve.tensor_tensor(level[:, t], theirs, mine, ALU.is_ge)
                link(ins)
                for t in range(ROW_TILES):
                    ins = dve.tensor_tensor(level[:, t], level[:, t], lower[:, :, :], ALU.mult)
                link(ins)
                link(dve.tensor_tensor(above[:, :, :, :], above[:, :, :, :], level[:, :, :, :], ALU.max))
                link(dve.tensor_reduce(rank[:, :, :], above[:, :, :, :], AX.X, ALU.add))
                dve.tensor_scalar(mask[:, :, :], rank[:, :, :], float(TOP_K), None, ALU.is_lt).then_inc(s_mask, 1)
                for k in range(TOP_K):
                    ins = dve.tensor_scalar(chosen[:, :, k, :], rank[:, :, :], float(k), None, ALU.is_equal)
                link(ins)
                for k in range(TOP_K):
                    ins = dve.tensor_tensor(picked[:, :, k, :], chosen[:, :, k, :], logits[:, :, :], ALU.mult)
                link(ins)
                link(dve.tensor_reduce(top[:, :, :], picked[:, :, :, :], AX.X, ALU.add))
                dve.tensor_tensor(gap[:, :], top[:, :, 1], top[:, :, 0], ALU.subtract).then_inc(s_gap, 1)

            def send(i, par, link):
                dve.wait_ge(s_place_ps, i - 1)
                link(dve.tensor_tensor(place[:, :, :], ps_place.rearrange("p (t e) -> p t e", t=ROW_TILES),
                                       region_start[:, :].unsqueeze(1).to_broadcast([P, ROW_TILES, EXPERTS]),
                                       ALU.add))
                for k in range(TOP_K):
                    ins = dve.tensor_tensor(picked2[:, :, k, :], chosen[:, :, k, :], place[:, :, :], ALU.mult)
                link(ins)
                link(dve.tensor_reduce(slotf[:, :, :], picked2[:, :, :, :], AX.X, ALU.add))
                dve.tensor_copy(slot[:, par, :], slotf[:, :, :].rearrange("p t k -> p (t k)"))
                link(dve.tensor_tensor(count[:, 1 - par, :], count[:, par, :], mask[:, 0, :], ALU.add))
                link(dve.tensor_tensor(count[:, 1 - par, :], count[:, 1 - par, :], mask[:, 1, :], ALU.add))
                dve.wait_ge(s_gexp, i - 1)
                link(dve.tensor_scalar(denom[:, :], gap_exp[:, :], 1.0, None, ALU.add))
                link(dve.reciprocal(prob[:, :, 0], denom[:, :]))
                link(dve.tensor_tensor(prob[:, :, 1], prob[:, :, 0], gap_exp[:, :], ALU.mult))
                pay = payload[:, par * 4:par * 4 + 4, :]
                dve.tensor_copy(pay[:, :, DIM // 2 + 1].bitcast(fp32), prob[:, :, :].rearrange("p t k -> p (t k)"))
                link(dve.tensor_copy(pay[:, :, DIM // 2], dest[:, :, :].rearrange("p t k -> p (t k)")))
                dve.tensor_scalar(dest[:, :, :], dest[:, :, :], SEQ, None, ALU.add).then_inc(s_slot, 1)

            def round_(i, par, pair):
                other = 1 - par
                x3, xn3 = rows(x_in[:, par, :]), rows(xn[:, :])
                if has(i, 0):
                    dve.wait_ge(s_x[par], 16 * (pair + 1))
                    link1, n1 = chain(dve, c_ln1, i * LN_LINKS)
                    norm_stats(link1, 0, x3)
                if has(i, 1):
                    link, n = chain(dve, c_sm, (i - 1) * SM_LINKS)
                    softmax_differences(i, other, link)
                if has(i, 2):
                    link2, n2 = chain(dve, c_out, (i - 2) * OUT_LINKS)
                    output_bias(i, link2)
                if has(i, 0):
                    wait(dve, s_xT_ps, i)
                    norm_rows(link1, 0, i, x3, [lambda t: xn3[:, t, :]], xn3).then_inc(s_xn, 1)
                    assert n1[0] == LN_LINKS
                if has(i, 1):
                    softmax_quotients(i, link)
                    assert n[0] == SM_LINKS, n
                if has(i, 2):
                    residual_sum(i, par, pair, link2)
                if has(i, 0):
                    projections(i, par)
                if has(i, 2):
                    expert_input(i, par, pair, link2)
                    assert n2[0] == OUT_LINKS, n2
                if has(i, 1):
                    dve.wait_ge(s_pT_ps, i)
                    wait(dve, s_y_ps, i - 1)
                    dve.tensor_copy(probsT[:, :], ps_pT).then_inc(s_pT, 1)
                if has(i, 0):
                    dve.wait_ge(s_hi, i + 1)
                    dve.tensor_tensor(stage[:, :], stage[:, :],
                                      gu_w[:, bass.ds(i * PARTS, 1), :].rearrange("p a n -> p (a n)"),
                                      ALU.subtract).then_inc(s_r1, 1)
                if has(i, 2):
                    link3, n3 = chain(dve, c_rt, (i - 2) * RT_LINKS)
                    route(i, par, link3)
                if has(i, 0):
                    dve.wait_ge(s_mid, i + 1)
                    dve.tensor_tensor(gu_w[:, bass.ds(i * PARTS + 2, 1), :].rearrange("p a n -> p (a n)"),
                                      stage[:, :],
                                      gu_w[:, bass.ds(i * PARTS + 1, 1), :].rearrange("p a n -> p (a n)"),
                                      ALU.subtract).then_inc(s_lo, 1)
                if has(i, 2):
                    send(i, par, link3)
                    assert n3[0] == RT_LINKS, n3

            dve.wait_ge(s_prep, 4)
            for i in range(4):
                round_(i, i % 2, i // 2)
            with dve.Fori(2, BATCHES // 2) as pair:
                round_(2 * pair, 0, pair)
                round_(2 * pair + 1, 1, pair)
            round_(BATCHES, 0, BATCHES // 2)
            round_(BATCHES + 1, 1, BATCHES // 2)

            link, _ = chain(dve, c_tab, 0)
            dve.wait_ge(s_total_ps, 1)
            dve.wait_ge(s_lo, BATCHES)
            link(dve.tensor_copy(total[:, :], ps_total))
            link(dve.tensor_tensor(pad_place[:, :], pad_place[:, :], total[:, :], ALU.add))
            dve.tensor_copy(pad_slot[:, :], pad_place[:, :]).then_inc(s_pad, 1)
            link(dve.tensor_tensor(filled, total[0:1, :].unsqueeze(2).to_broadcast([1, EXPERTS, 32]),
                                   tile_first[0:1, :].unsqueeze(1).to_broadcast([1, EXPERTS, 32]), ALU.is_gt))
            link(dve.tensor_reduce(tiles_of[:, :], filled, AX.X, ALU.add))
            link(dve.tensor_copy(tiles_upto[:, :], tiles_of[:, :]))
            for e in range(1, EXPERTS):
                link(dve.tensor_tensor(tiles_upto[:, e:e + 1], tiles_upto[:, e:e + 1], tiles_upto[:, e - 1:e],
                                       ALU.add))
            jt = [1, MOE_TILES, EXPERTS]
            link(dve.tensor_tensor(reached, tile_no[0:1, :].unsqueeze(2).to_broadcast(jt),
                                   tiles_upto[0:1, :].unsqueeze(1).to_broadcast(jt), ALU.is_ge))
            dve.tensor_tensor(passed, reached, tiles_of[0:1, :].unsqueeze(1).to_broadcast(jt), ALU.mult)
            link(dve.tensor_reduce(tile_expert[:, :], reached, AX.X, ALU.add))
            link(dve.tensor_reduce(tile_skipped[:, :], passed, AX.X, ALU.add))
            link(dve.tensor_tensor(tile_local[:, :], tile_no[:, :], tile_skipped[:, :], ALU.subtract))
            link(dve.tensor_scalar(tile_local[:, :], tile_local[:, :], float(P), None, ALU.mult))
            link(dve.tensor_scalar(tile_rowf[:, :], tile_expert[:, :], float(REGION), None, ALU.mult))
            link(dve.tensor_tensor(tile_rowf[:, :], tile_rowf[:, :], tile_local[:, :], ALU.add))
            dve.tensor_scalar(table[:, 0, :], tile_rowf[:, :], float(DUMMY_ROW), None, ALU.min
                              ).then_inc(s_table, 1)
            dve.tensor_scalar(table[:, 1, :], tile_expert[:, :], float(EXPERTS - 1), None, ALU.min
                              ).then_inc(s_table, 1)

            def rows_in(j, buf, scat):
                dve.wait_ge(s_xrow_ps, j + 1)
                dve.tensor_copy(xT_buf[:, buf, :, :].rearrange("p c t -> p (c t)"),
                                ps_x[:, :].bitcast(bf16)[:, 0:DIM]).then_inc(s_xrow, 1)
                wait(dve, s_scat[buf], scat)
                dve.tensor_copy(meta[:, buf, :], payload[:, buf, DIM // 2:]).then_inc(s_meta, 1)

            def multiply(j, n):
                dve.wait_ge(s_gated[n], j + 1)
                wait(dve, s_hT_ps[n], j)
                dve.tensor_tensor(hidden[:, n, :], gated[:, n, :], ps_up[n][:, 0:HALF], ALU.mult
                                  ).then_inc(s_h[n], 1)

            def hidden_in(j, n):
                dve.wait_ge(s_hT_ps[n], j + 1)
                size = PIECES[2]
                dve.tensor_copy(hT[:, n, 0:2, :].rearrange("p m t -> p (m t)"), ps_hT[n][:, 0:2 * P])
                dve.tensor_copy(hT[0:size, n, 2, :], ps_hT[n][0:size, 2 * P:3 * P]).then_inc(s_hT[n], 1)

            def tile(j, buf, scat, first_tile, last_tile):
                if not first_tile:
                    hidden_in(j - 1, 1)
                multiply(j, 0)
                if not last_tile:
                    rows_in(j + 1, (buf + 1) % 3, scat)
                hidden_in(j, 0)
                multiply(j, 1)

            rows_in(0, 0, 0)
            tile(0, 0, 0, True, False)

            def three_tiles(r):
                for n in range(3):
                    tile(3 * r + 1 + n, (1 + n) % 3, 16 * r if n == 0 else 16 * r + 16, False, False)
            three_tiles(0)
            with dve.Fori(1, (MOE_TILES - 2) // 3) as r:
                three_tiles(r)
            last = MOE_TILES - 1
            tile(last, last % 3, 0, False, True)
            hidden_in(last, 1)

            link, _ = chain(dve, c_tail, 0)
            for g in range(TAIL_GROUPS):
                dve.wait_ge(s_ty[g], 32)
                y0 = tail_y[:, g, 0].rearrange("p r d -> p (r d)")
                link(dve.tensor_tensor(y0, y0, tail_y[:, g, 1].rearrange("p r d -> p (r d)"), ALU.add))
                for r in range(TAIL_ROWS):
                    ins = dve.bn_stats(tail_stats[:, g % 2, r, :], tail_y[:, g, 0, r, :])
                link(ins)
                for r in range(TAIL_ROWS):
                    ins = dve.bn_aggr(tail_mv[:, g % 2, r, :], tail_stats[:, g % 2, r, :])
                link(ins)
                dve.tensor_scalar(tail_var[:, g % 2, :], tail_mv[:, g % 2, :, 1], EPS, None, ALU.add
                                  ).then_inc(s_tvar, 1)
                dve.wait_ge(s_troot, g + 1)
                dve.scalar_tensor_tensor(tail_shift[:, g % 2, :], tail_mv[:, g % 2, :, 0], -1.0,
                                         tail_inv[:, g % 2, :], ALU.mult, ALU.mult).then_inc(s_tshift, 1)
                dve.wait_ge(s_txs, g + 1)
                for r in range(TAIL_ROWS):
                    ins = dve.scalar_tensor_tensor(tail_y[:, g, 0, r, :], tail_y[:, g, 0, r, :],
                                                   tail_inv[:, g % 2, r:r + 1], tail_xs[:, g % 2, r, :],
                                                   ALU.mult, ALU.add)
                ins.then_inc(s_tdone, 1)


CONSTS = 14
EPS_BF16 = 1.0013580322265625e-05
SCALE_BF16 = 0.08837890625
LN_LINKS, SM_LINKS, OUT_LINKS, RT_LINKS = 4, 5, 11, 17


def kernel(**inputs):
    import numpy as _np
    import concourse.bacc as _bacc
    from concourse import mybir as _mybir
    from concourse.bass_utils import run_bass_kernel_spmd as _run

    def host(name):
        return _np.asarray(inputs[name])

    arrays = {"base": host("L0_attn_base")}
    for n, src in (("wqT", "Wq"), ("wkT", "Wk"), ("wvT", "Wv"), ("woT", "Wo")):
        arrays[n] = host("L0_attn_" + src).T
    for n in ("bq", "bk", "bv", "bo"):
        arrays[n] = host("L0_attn_" + n)
    arrays["routerT"] = host("L0_ffn_router_w").T
    gate = host("L0_ffn_gate_w").transpose(0, 2, 1)
    up = host("L0_ffn_up_w").transpose(0, 2, 1)
    arrays["gate_up"] = _np.concatenate([gate, up], axis=2).reshape(EXPERTS * CHUNKS, P, 2 * FFN)
    dn = host("L0_ffn_down_w").transpose(0, 2, 1)
    laid = _np.zeros((EXPERTS, P, 6, DIM), dn.dtype)
    at = 0
    for n in range(6):
        size = PIECES[n % 3]
        laid[:, :size, n, :] = dn[:, at:at + size, :]
        at += size
    arrays["down"] = laid.reshape(EXPERTS, P, 6 * DIM)

    nc = _bacc.Bacc("TRN2", target_bir_lowering=False, num_devices=1)
    args, named = [], {}
    for name, a in arrays.items():
        a = _np.ascontiguousarray(a)
        named[f"in_{name}_dram"] = a
        args.append(nc.dram_tensor(f"in_{name}_dram", a.shape, _mybir.dt.from_np(a.dtype), kind="ExternalInput").ap())
    out = nc.dram_tensor("out_dram", (TOKENS, DIM), _mybir.dt.float32, kind="ExternalOutput").ap()
    build(nc, *args, out)
    r = _run(nc, [named], core_ids=[0])
    return r.results[0]["out_dram"].reshape(BATCHES, SEQ, DIM)
```

```python
import concourse.bass as bass
from concourse import mybir
from contextlib import ExitStack

BATCHES, SEQ, DIM, HEADS = 16, 256, 256, 2
HEAD_DIM = DIM // HEADS
EXPERTS, FFN, TOP_K = 8, 688, 2
P = 128
TOKENS = BATCHES * SEQ
ROW_TILES = SEQ // P
CHUNKS = DIM // P
SLOTS = TOKENS * TOP_K
MOE_TILES = (SLOTS + EXPERTS * (P - 1)) // P
REGION = TOKENS + P
DUMMY_ROW = EXPERTS * REGION
ROW_WORDS = DIM // 2 + 2
NOWHERE = 1 << 20
THIRDS = (230, 230, FFN - 460)
THIRD_AT = (0, 2 * 230, 4 * 230)
PIECES = tuple((P, w - P) for w in THIRDS)
PARTS = 3
EPS = 1e-5
TAIL_ROWS = 4
TAIL_GROUPS = TOKENS // (P * TAIL_ROWS)
GROUP, LAGS = 4, 3
ROUNDS = BATCHES + LAGS
FIRST_ROUND = 6
GROUPS_IN_ROUNDS = ROUNDS - FIRST_ROUND
REST = MOE_TILES - GROUP * GROUPS_IN_ROUNDS
WEIGHT_CHUNKS = EXPERTS * CHUNKS
for _i in range(FIRST_ROUND, ROUNDS):
    assert (_i - LAGS) * SEQ * TOP_K - EXPERTS * (P - 1) >= GROUP * P * (_i + 1 - FIRST_ROUND)


def build(nc, base, wqT, wkT, wvT, woT, bq, bk, bv, bo, routerT, gate_up, down, out):
    fp32, bf16, i32 = mybir.dt.float32, mybir.dt.bfloat16, mybir.dt.int32
    ALU, ACT, AX = mybir.AluOpType, mybir.ActivationFunctionType, mybir.AxisListType

    dispatched = nc.dram_tensor("dispatched", [DUMMY_ROW + P, ROW_WORDS], i32, kind="Internal").ap()
    expert_out = nc.dram_tensor("expert_out", [SLOTS, DIM], fp32, kind="Internal").ap()
    residual = nc.dram_tensor("residual", [TOKENS, DIM], bf16, kind="Internal").ap()

    ctx = ExitStack()
    with ctx:
        def sb(name, shape, dt):
            return ctx.enter_context(nc.sbuf_tensor(name, shape, dt))

        def pb(name):
            return ctx.enter_context(nc.psum_tensor(name, [P, 512], fp32))

        def sem(name):
            return ctx.enter_context(nc.semaphore(name))

        gu_w = sb("gu_w", [P, EXPERTS * CHUNKS * PARTS, 2 * FFN], bf16)
        down_w = sb("down_w", [P, 2, 6 * DIM], fp32)
        payload = sb("payload", [P, 8, ROW_WORDS], i32)
        tile_rows = sb("tile_rows", [P, GROUP, ROW_WORDS], i32)
        gated = sb("gated", [P, 3, THIRDS[0]], fp32)
        hidden = sb("hidden", [P, 3, THIRDS[0]], fp32)
        attn_w = sb("attn_w", [P, 4, CHUNKS, DIM], bf16)
        qk_bias = sb("qk_bias", [P, 2, HEADS], bf16)
        qk_biasf = sb("qk_biasf", [P, 2, HEADS], fp32)
        row_bias = sb("row_bias", [P, 2, DIM], bf16)
        router32 = sb("router32", [P, CHUNKS, EXPERTS], fp32)
        router_w = sb("router_w", [P, PARTS, CHUNKS, EXPERTS], bf16)
        identf = sb("identf", [P, P], fp32)
        ident = sb("ident", [P, P], bf16)
        before = sb("before", [P, P], bf16)
        ones = sb("ones", [P, P], bf16)
        y_buf = sb("y_buf", [P, GROUP, DIM], fp32)
        xT_buf = sb("xT_buf", [P, 2, CHUNKS, P], bf16)
        meta = sb("meta", [P, GROUP, 2], i32)
        hT = sb("hT", [P, 3, 2, P], fp32)
        ln_stats = sb("ln_stats", [P, 3, ROW_TILES, 6], fp32)
        ln_mv = sb("ln_mv", [P, 3, ROW_TILES, 2], bf16)
        ln_var = sb("ln_var", [P, 3, ROW_TILES], bf16)
        ln_std = sb("ln_std", [P, 3, ROW_TILES], bf16)
        ln_inv = sb("ln_inv", [P, 3, ROW_TILES], fp32)
        ln_sum = sb("ln_sum", [P, 3, ROW_TILES], fp32)
        ln_mean = sb("ln_mean", [P, 3, ROW_TILES], bf16)
        half = sb("half", [P, ROW_TILES], bf16)
        pace = sb("pace", [P, 2], bf16)
        minus_half = sb("minus_half", [P, TAIL_ROWS], fp32)
        tail_var = sb("tail_var", [P, 2, TAIL_ROWS], fp32)
        sm_max = sb("sm_max", [P, 4], fp32)
        sm_total = sb("sm_total", [P, 4], fp32)
        sm_sum = sb("sm_sum", [P, 4], bf16)
        sm_inv = sb("sm_inv", [P, 4], fp32)
        logits = sb("logits", [P, ROW_TILES, EXPERTS], fp32)
        above = sb("above", [P, ROW_TILES, EXPERTS, EXPERTS], fp32)
        level = sb("level", [P, ROW_TILES, EXPERTS, EXPERTS], fp32)
        lower = sb("lower", [P, EXPERTS, EXPERTS], fp32)
        rank = sb("rank", [P, ROW_TILES, EXPERTS], fp32)
        chosen = sb("chosen", [P, ROW_TILES, TOP_K, EXPERTS], fp32)
        picked = sb("picked", [P, ROW_TILES, TOP_K, EXPERTS], fp32)
        picked2 = sb("picked2", [P, ROW_TILES, TOP_K, EXPERTS], fp32)
        top = sb("top", [P, ROW_TILES, TOP_K], fp32)
        gap = sb("gap", [P, ROW_TILES], fp32)
        gap_exp = sb("gap_exp", [P, ROW_TILES], fp32)
        denom = sb("denom", [P, ROW_TILES], fp32)
        prob = sb("prob", [P, ROW_TILES, TOP_K], fp32)
        mask = sb("mask", [P, ROW_TILES, EXPERTS], bf16)
        count = sb("count", [P, 2, EXPERTS], bf16)
        place = sb("place", [P, ROW_TILES, EXPERTS], fp32)
        region_start = sb("region_start", [P, EXPERTS], fp32)
        slotf = sb("slotf", [P, ROW_TILES, TOP_K], fp32)
        slot = sb("slot", [P, 2, ROW_TILES * TOP_K], i32)
        dest = sb("dest", [P, ROW_TILES, TOP_K], i32)
        pad_place = sb("pad_place", [P, EXPERTS], fp32)
        pad_slot = sb("pad_slot", [P, EXPERTS], i32)
        pad_row = sb("pad_row", [P, ROW_WORDS], i32)
        total = sb("total", [P, EXPERTS], fp32)
        tile_q = sb("tile_q", [1, EXPERTS], fp32)
        tiles_full = sb("tiles_full", [1, EXPERTS], fp32)
        tiles_run = sb("tiles_run", [1, EXPERTS], fp32)
        tiles_left = sb("tiles_left", [1, EXPERTS], fp32)
        left_below = sb("left_below", [1, EXPERTS, EXPERTS], fp32)
        below = sb("below", [1, EXPERTS], fp32)
        upto = sb("upto", [1, EXPERTS], fp32)
        full_less = sb("full_less", [1, EXPERTS], fp32)
        start_row = sb("start_row", [1, EXPERTS + 1], fp32)
        row_step = sb("row_step", [1, EXPERTS], fp32)
        taken = sb("taken", [1, EXPERTS], fp32)
        nth = sb("nth", [1, REST], fp32)
        nth_row = sb("nth_row", [1, REST], fp32)
        reached = sb("reached", [1, REST, EXPERTS], fp32)
        stepped = sb("stepped", [1, REST, EXPERTS], fp32)
        sel_row = sb("sel_row", [1, REST], fp32)
        sel_rowf = sb("sel_rowf", [1, REST], fp32)
        sel_expert = sb("sel_expert", [1, REST], fp32)
        chosen_tiles = sb("chosen_tiles", [1, 2, 2, GROUP], i32)
        rest_tiles = sb("rest_tiles", [1, 2, REST], i32)
        tail_stats = sb("tail_stats", [P, 2, TAIL_ROWS, 6], fp32)
        tail_mv = sb("tail_mv", [P, 2, TAIL_ROWS, 2], fp32)
        tail_inv = sb("tail_inv", [P, 2, TAIL_ROWS], fp32)
        tail_shift = sb("tail_shift", [P, 2, TAIL_ROWS], fp32)

        stage = down_w[:, :, 0:2 * FFN]
        work = sb("work", [P, 21 * ROW_TILES * DIM], bf16)
        used = [0]

        def carve(n):
            used[0] += n
            return work[:, used[0] - n:used[0]]

        def carve2(n):
            return carve(2 * n).rearrange("p (b n) -> p b n", b=2)

        W = ROW_TILES * DIM
        x_in, x_again, x1 = carve2(W), carve2(W), carve2(W)
        q_sb, k_sb, v_sb = carve2(W), carve2(W), carve2(W)
        xn, xnT, oo, yT, xfT = carve(W), carve(W), carve(W), carve(W), carve(W)
        probs, probsT = carve(4 * SEQ), carve(4 * SEQ)

        def rows(ap):
            return ap.rearrange("p (t d) -> p t d", t=ROW_TILES)

        TW = TAIL_ROWS * DIM
        over = gu_w[:, :, :].rearrange("p a n -> p (a n)")
        tail_y = over[:, 0:TAIL_GROUPS * 2 * TW * 2].bitcast(fp32).rearrange(
            "p (g k r d) -> p g k r d", g=TAIL_GROUPS, k=TOP_K, d=DIM)
        tail_x = over[:, TAIL_GROUPS * 4 * TW:TAIL_GROUPS * 5 * TW].rearrange(
            "p (g r d) -> p g r d", g=TAIL_GROUPS, d=DIM)
        tail_xs = over[:, TAIL_GROUPS * 5 * TW:TAIL_GROUPS * 5 * TW + 4 * TW].bitcast(fp32).rearrange(
            "p (g r d) -> p g r d", g=2, d=DIM)

        bank = [pb(f"bank{n}") for n in range(8)]
        bank_a, bank_b, bank_c = bank[5][:, :], bank[6][:, :], bank[7][:, :]
        ps_o, ps_v = bank_a, bank_a
        ps_xT = bank_a.bitcast(bf16)[:, 0:512].rearrange("p (c t) -> p c t", c=CHUNKS)
        ps_xfT = ps_xT
        ps_q, ps_k, ps_y = bank_b, bank_c, bank_c
        ps_s = [bank_b, bank_c]
        ps_pT = bank_b.bitcast(bf16)
        ps_logits = bank_b[:, 0:ROW_TILES * EXPERTS]
        ps_place = bank_c[:, 0:ROW_TILES * EXPERTS]
        ps_total = bank_c[:, 128:128 + EXPERTS]
        ps_gu = [bank[n][:, :] for n in range(3)]
        ps_hT = bank[3][:, 0:2 * P]
        ps_xrow = bank[2][:, 0:P].bitcast(bf16)
        ps_out = bank[4][:, 0:DIM]

        s_const = sem("s_const")
        s_ident = sem("s_ident")
        s_attn_w = sem("s_attn_w")
        s_small = sem("s_small")
        s_prep = sem("s_prep")
        s_router = sem("s_router")
        s_x = [sem(f"s_x_in{n}") for n in range(2)]
        s_xa = [sem(f"s_x_again{n}") for n in range(2)]
        s_xn = sem("s_xn")
        s_xT_ps = sem("s_xT_ps")
        s_xT = sem("s_xT")
        s_var = [sem(f"s_var{n}") for n in range(3)]
        s_root = [sem(f"s_root{n}") for n in range(3)]
        s_count, s_placed = sem("s_count"), sem("s_placed")
        s_paced = [sem("s_paced0"), sem("s_paced1")]
        s_tvar, s_troot = sem("s_tvar"), sem("s_troot")
        s_q_ps, s_k_ps, s_v_ps = sem("s_q_ps"), sem("s_k_ps"), sem("s_v_ps")
        s_q_raw, s_k_raw, s_v_raw = sem("s_q_raw"), sem("s_k_raw"), sem("s_v_raw")
        s_q, s_k, s_v = sem("s_q"), sem("s_k"), sem("s_v")
        s_v_sum = sem("s_v_sum")
        s_s_ps, s_s = sem("s_s_ps"), sem("s_s")
        s_sub, s_exp, s_p = sem("s_sub"), sem("s_exp"), sem("s_p")
        s_pT_ps, s_pT = sem("s_pT_ps"), sem("s_pT")
        s_y_ps, s_y = sem("s_y_ps"), sem("s_y")
        s_o_ps, s_o = sem("s_o_ps"), sem("s_o")
        s_x1, s_x1_saved = sem("s_x1"), [sem(f"s_x1_saved{n}") for n in range(2)]
        s_xf, s_xfT_ps, s_xfT = sem("s_xf"), sem("s_xfT_ps"), sem("s_xfT")
        s_lg_ps, s_mask = sem("s_lg_ps"), sem("s_mask")
        s_gap, s_gexp = sem("s_gap"), sem("s_gexp")
        s_place_ps, s_slot = sem("s_place_ps"), sem("s_slot")
        s_sent = [sem(f"s_sent{n}") for n in range(2)]
        s_stage = [sem("s_stage0"), sem("s_stage1")]
        s_hi, s_r1, s_mid, s_lo = sem("s_hi"), sem("s_r1"), sem("s_mid"), sem("s_lo")
        s_down = [sem("s_down0"), sem("s_down1")]
        c_ln1, c_sm, c_out, c_rt, c_send = sem("c_ln1"), sem("c_sm"), sem("c_out"), sem("c_rt"), sem("c_send")
        c_sel = sem("c_sel")
        s_pad, s_pad_sent, s_sel = sem("s_pad"), sem("s_pad_sent"), sem("s_sel")
        s_rows = [sem(f"s_rows{n}") for n in range(GROUP)]
        s_xrow_ps, s_xrow, s_meta = sem("s_xrow_ps"), sem("s_xrow"), sem("s_meta")
        s_gu, s_gated, s_h, s_hT_ps, s_hT = sem("s_gu"), sem("s_gated"), sem("s_h"), sem("s_hT_ps"), sem("s_hT")
        s_out_ps, s_out = sem("s_out_ps"), sem("s_out")
        s_scat = [sem(f"s_scat{n}") for n in range(GROUP)]
        s_ty = [sem(f"s_ty{n}") for n in range(TAIL_GROUPS)]
        s_tx = [sem(f"s_tx{n}") for n in range(TAIL_GROUPS)]
        c_tail = sem("c_tail")
        s_tshift, s_txs, s_tdone = sem("s_tshift"), sem("s_txs"), sem("s_tdone")
        s_stored = sem("s_stored")

        def wait(eng, semaphore, value):
            if isinstance(value, int) and value <= 0:
                return
            eng.wait_ge(semaphore, value)

        def chain(eng, semaphore, start):
            n = [0]

            def link(ins):
                n[0] += 1
                ins.then_inc(semaphore, 1)
                eng.wait_ge(semaphore, start + n[0])
            return link, n

        def rounds(eng, round_):
            for i in range(8):
                round_(i, i % 2, i - FIRST_ROUND, i // 2)
            with eng.Fori(4, BATCHES // 2) as pair:
                round_(2 * pair, 0, 2 * pair - FIRST_ROUND, pair)
                round_(2 * pair + 1, 1, 2 * pair + 1 - FIRST_ROUND, pair)
            for i in range(BATCHES, ROUNDS):
                round_(i, i % 2, i - FIRST_ROUND, i // 2)

        def has(i, lag):
            return not isinstance(i, int) or 0 <= i - lag < BATCHES

        def runs_tiles(group):
            return not isinstance(group, int) or group >= 0

        def rest_groups(eng, group_):
            with eng.Fori(GROUPS_IN_ROUNDS, MOE_TILES // GROUP) as m:
                group_(m, GROUP)
            group_(MOE_TILES // GROUP, MOE_TILES % GROUP)

        def weight_chunk(i, p):
            if isinstance(i, int) and i < FIRST_ROUND and 3 * i + p // 4 < WEIGHT_CHUNKS:
                return 3 * i + p // 4
            return None

        block = ctx.enter_context(nc.Block())

        @block.sync
        def _(sp):
            base_rows = base.rearrange("b (t p) d -> b p t d", p=P)
            for n, w in enumerate((wqT, wkT, wvT, woT)):
                sp.dma_start(attn_w[:, n, :, :], w.rearrange("(c p) n -> p c n", p=P)).then_inc(s_attn_w, 16)

            def load_x(b, buf):
                if not (isinstance(b, int) and b < 2):
                    wait(sp, s_xn, b - 1)
                sp.dma_start(rows(x_in[:, buf, :]), base_rows[b]).then_inc(s_x[buf], 16)

            load_x(0, 0)
            sp.dma_start(qk_bias[:, 0, :], bq.rearrange("(h p) -> p h", p=P),
                         allow_slow_non_contiguous=True).then_inc(s_small, 16)
            sp.dma_start(qk_bias[:, 1, :], bk.rearrange("(h p) -> p h", p=P),
                         allow_slow_non_contiguous=True).then_inc(s_small, 16)
            sp.dma_start(row_bias[:, 0, :], bv.rearrange("(a d) -> a d", a=1).to_broadcast([P, DIM])
                         ).then_inc(s_small, 16)
            sp.dma_start(row_bias[:, 1, :], bo.rearrange("(a d) -> a d", a=1).to_broadcast([P, DIM])
                         ).then_inc(s_small, 16)
            sp.dma_start(router32[:, :, :], routerT.rearrange("(c p) e -> p c e", p=P)).then_inc(s_small, 16)
            load_x(1, 1)

            def load_weights(c):
                wait(sp, s_lo, c - 1)
                sp.dma_start(stage[:, c % 2, :], gate_up[c]).then_inc(s_stage[c % 2], 16)

            def load_rows(m, n, table):
                rows_from(sp.value_load(table, min_val=0, max_val=DUMMY_ROW), m, n)

            def rows_from(row, m, n):
                wait(sp, s_meta, GROUP * m + n - 3)
                sp.dma_start(tile_rows[:, n, :], dispatched[bass.ds(row, P), :]).then_inc(s_rows[n], 16)

            def load_down(m, n, table, chosen_next=False):
                expert = sp.value_load(table, min_val=0, max_val=EXPERTS - 1)
                wait(sp, s_out_ps, GROUP * m + n - 1)
                if chosen_next:
                    sp.wait_ge(s_sel, 2 * (m + 2))
                sp.dma_start(down_w[:, n % 2, :], down[bass.ds(expert, 1), :, :].rearrange("e p n -> p (e n)")
                             ).then_inc(s_down[n % 2], 16)

            def chosen(kind, par, n):
                return chosen_tiles[0:1, par, kind, n:n + 1]

            def round_(i, par, m, pair):
                if isinstance(i, int) and 1 <= i < 7:
                    load_x(i + 1, 1 - par)
                elif has(i, 0) and not (isinstance(i, int) and i < 8):
                    load_x(i, par)
                if isinstance(i, int) and i == FIRST_ROUND:
                    sp.wait_ge(s_lo, WEIGHT_CHUNKS)
                if has(i, 2):
                    wait(sp, s_x1, i - 2)
                    sp.dma_start(rows(x_again[:, par, :]), base_rows[i - 2]).then_inc(s_xa[par], 16)
                for p in (0, 4, 8):
                    c = weight_chunk(i, p)
                    if c is not None and c + 2 < WEIGHT_CHUNKS:
                        load_weights(c + 2)
                for n in range(GROUP):
                    if n == 2 and has(i, 2):
                        wait(sp, s_x1, i - 1)
                        sp.dma_start(residual[bass.ds((i - 2) * SEQ, SEQ), :].rearrange("(t p) d -> p t d", p=P),
                                     rows(x1[:, par, :])).then_inc(s_x1_saved[par], 16)
                    last_round = isinstance(i, int) and i == ROUNDS - 1
                    if runs_tiles(m):
                        if n < GROUP - 1:
                            load_rows(m, n + 1, chosen(0, par, n + 1))
                        load_down(m, n, chosen(1, par, n), n == GROUP - 1)
                    if n == GROUP - 1 and not last_round and (runs_tiles(m) or m == -1):
                        if not runs_tiles(m):
                            sp.wait_ge(s_sel, 2)
                        row = sp.value_load(chosen(0, 1 - par, 0), min_val=0, max_val=DUMMY_ROW)
                        for q in range(2):
                            done = pair if par == 1 and q == 0 else pair - 1
                            sp.wait_ge(s_sent[q], SENT * done)
                        rows_from(row, m + 1, 0)

            load_weights(0)
            load_weights(1)
            rounds(sp, round_)

            sp.wait_ge(s_sel, 2 * (GROUPS_IN_ROUNDS + 1))
            for q in range(2):
                sp.wait_ge(s_sent[q], SENT * (BATCHES // 2))
            sp.wait_ge(s_pad_sent, 16 * (EXPERTS + 1))
            load_rows(GROUPS_IN_ROUNDS, 0, rest_tiles[0:1, 0, 0:1])

            def group_(m, tiles):
                for n in range(tiles):
                    at = GROUP * (m - GROUPS_IN_ROUNDS) + n
                    if isinstance(m, int) and GROUP * m + n + 1 >= MOE_TILES:
                        pass
                    elif n < GROUP - 1:
                        load_rows(m, n + 1, rest_tiles[0:1, 0, bass.ds(at + 1, 1)])
                    else:
                        load_rows(m + 1, 0, rest_tiles[0:1, 0, bass.ds(at + 1, 1)])
                    load_down(m, n, rest_tiles[0:1, 1, bass.ds(at, 1)])
            rest_groups(sp, group_)

            tok = residual.rearrange("(g p r) d -> g p r d", p=P, r=TAIL_ROWS)
            eo = expert_out.rearrange("(k g p r) d -> g p k r d", k=TOP_K, p=P, r=TAIL_ROWS)
            of = out.rearrange("(g p r) d -> g p r d", p=P, r=TAIL_ROWS)
            sp.wait_ge(s_gu, 3 * MOE_TILES)
            for n in range(2):
                sp.wait_ge(s_x1_saved[n], 16 * BATCHES // 2)
            for g in range(TAIL_GROUPS):
                sp.dma_start(tail_x[:, g], tok[g]).then_inc(s_tx[g], 16)
            for n in range(GROUP):
                sp.wait_ge(s_scat[n], 16 * len(range(n, MOE_TILES, GROUP)))
            for g in range(TAIL_GROUPS):
                for k in range(TOP_K):
                    sp.dma_start(tail_y[:, g, k], eo[g, :, k]).then_inc(s_ty[g], 16)
            for g in range(TAIL_GROUPS):
                sp.wait_ge(s_tdone, g + 1)
                sp.dma_start(of[g], tail_y[:, g, 0]).then_inc(s_stored, 16)
            sp.wait_ge(s_stored, 16 * TAIL_GROUPS)

        @block.gpsimd
        def _(pool):
            pool.memset(ones[:, :], 1.0).then_inc(s_const, 1)
            pool.memset(half[:, :], 0.5).then_inc(s_const, 1)
            pool.memset(minus_half[:, :], -0.5).then_inc(s_const, 1)
            pool.memset(ident[:, :], 0.0).then_inc(s_ident, 1)
            pool.memset(identf[:, :], 0.0).then_inc(s_ident, 1)
            pool.memset(before[:, :], 1.0).then_inc(s_ident, 1)
            pool.memset(lower[:, :, :], 1.0).then_inc(s_ident, 1)
            pool.memset(pad_row[:, :], 0).then_inc(s_ident, 1)
            pool.wait_ge(s_ident, 5)
            for m in (ident, identf):
                pool.affine_select(out=m[:, :], in_=m[:, :], compare_op=ALU.not_equal, fill=1.0, base=0,
                                   pattern=[[-1, P]], channel_multiplier=1).then_inc(s_const, 1)
            pool.affine_select(out=before[:, :], in_=before[:, :], compare_op=ALU.is_gt, fill=0.0, base=0,
                               pattern=[[1, P]], channel_multiplier=-1).then_inc(s_const, 1)
            pool.affine_select(out=lower[:, :, :], in_=lower[:, :, :], compare_op=ALU.is_gt, fill=0.0, base=0,
                               pattern=[[1, EXPERTS], [-1, EXPERTS]], channel_multiplier=0).then_inc(s_const, 1)
            pool.memset(pad_row[:, DIM // 2:DIM // 2 + 1], NOWHERE).then_inc(s_const, 1)
            pool.memset(count[:, 0, :], 0.0).then_inc(s_const, 1)
            pool.iota(dest[:, :, :], pattern=[[P, ROW_TILES], [TOKENS, TOP_K]], base=0,
                      channel_multiplier=1).then_inc(s_const, 1)
            pool.iota(region_start[:, :], pattern=[[REGION, EXPERTS]], base=0, channel_multiplier=0,
                      allow_small_or_imprecise_dtypes=True).then_inc(s_const, 1)
            pool.iota(pad_place[:, :], pattern=[[REGION, EXPERTS]], base=0, channel_multiplier=1,
                      allow_small_or_imprecise_dtypes=True).then_inc(s_const, 1)
            pool.iota(nth[:, :], pattern=[[1, REST]], base=0, channel_multiplier=0,
                      allow_small_or_imprecise_dtypes=True).then_inc(s_const, 1)
            pool.iota(nth_row[:, :], pattern=[[P, REST]], base=0, channel_multiplier=0,
                      allow_small_or_imprecise_dtypes=True).then_inc(s_const, 1)
            pool.memset(tiles_run[:, :], 0.0).then_inc(s_const, 1)
            pool.memset(start_row[:, EXPERTS:EXPERTS + 1], float(DUMMY_ROW)).then_inc(s_const, 1)
            pool.wait_ge(s_const, CONSTS)
            pool.dma_start(dispatched[DUMMY_ROW:DUMMY_ROW + P, :], pad_row[:, :]).then_inc(s_pad_sent, 16)

            last_row, last_slot = pool.to_reg(DUMMY_ROW - 1), pool.to_reg(SLOTS - 1)

            def carry_wait(which, earlier):
                wait(pool, s_paced[which], earlier)
                pool.tensor_tensor(pace[:, which:which + 1], half[:, 0:1], half[:, 0:1], ALU.mult
                                   ).then_inc(s_paced[which], 1)

            def dispatch(b, par):
                pool.wait_ge(s_slot, b + 1)
                carry_wait(0, b)
                for t in range(ROW_TILES):
                    for k in range(TOP_K):
                        n = t * TOP_K + k
                        pool.indirect_dma_start(
                            out=dispatched, out_offset=bass.IndirectOffsetOnAxis(ap=slot[:, par, n:n + 1], axis=0),
                            in_=payload[:, par * 4 + n, :], in_offset=None,
                            bounds_check=last_row, oob_is_err=False).then_inc(s_sent[par], 16)
            def root(which, b):
                pool.wait_ge(s_var[which], b + 1)
                pool.tensor_tensor(ln_std[:, which, :], ln_var[:, which, :], half[:, :], ALU.pow
                                   ).then_inc(s_root[which], 1)

            def send_back(m, n):
                pool.wait_ge(s_out, GROUP * m + n + 1)
                carry_wait(1, GROUP * m + n)
                pool.indirect_dma_start(
                    out=expert_out, out_offset=bass.IndirectOffsetOnAxis(ap=meta[:, n, 0:1], axis=0),
                    in_=y_buf[:, n, :], in_offset=None,
                    bounds_check=last_slot, oob_is_err=False).then_inc(s_scat[n], 16)

            def round_(i, par, m, pair):
                tiles = runs_tiles(m)
                if has(i, 0):
                    root(0, i)
                if has(i, 2):
                    root(1, i - 2)
                if tiles and not (isinstance(m, int) and m == 0):
                    send_back(m - 1, 2)
                if has(i, 2):
                    root(2, i - 2)
                if has(i, 3):
                    dispatch(i - 3, 1 - par)
                if isinstance(i, int) and i == ROUNDS - 1:
                    pool.wait_ge(s_pad, 1)
                    for e in range(EXPERTS):
                        pool.indirect_dma_start(
                            out=dispatched, out_offset=bass.IndirectOffsetOnAxis(ap=pad_slot[:, e:e + 1], axis=0),
                            in_=pad_row[:, :], in_offset=None,
                            bounds_check=last_row, oob_is_err=False).then_inc(s_pad_sent, 16)
                if tiles and not (isinstance(m, int) and m == 0):
                    send_back(m - 1, 3)
                if tiles:
                    send_back(m, 0)
                    send_back(m, 1)
            rounds(pool, round_)

            def group_(m, tiles):
                send_back(m - 1, 2)
                send_back(m - 1, 3)
                for n in range(max(0, tiles - (2 if tiles == GROUP else 0))):
                    send_back(m, n)
            rest_groups(pool, group_)

            for g in range(TAIL_GROUPS):
                pool.wait_ge(s_tvar, g + 1)
                pool.tensor_tensor(tail_inv[:, g % 2, :], tail_var[:, g % 2, :], minus_half[:, :], ALU.pow
                                   ).then_inc(s_troot, 1)

        @block.scalar
        def _(act):
            act.wait_ge(s_small, 16 * 5)
            act.activation(qk_biasf[:, :, :], qk_bias[:, :, :], ACT.Copy).then_inc(s_prep, 1)

            def tile_third(m, n, k):
                j = GROUP * m + n
                K = 3 * j + k
                w = THIRDS[k]
                if k == 0 and not (isinstance(j, int) and j < 2):
                    weighted_out(m if n >= 2 else m - 1, (n + 2) % GROUP)
                act.wait_ge(s_gu, K + 1)
                wait(act, s_h, K - 2)
                act.activation(gated[:, k, 0:w], ps_gu[k][:, 0:w], ACT.Silu).then_inc(s_gated, 1)
                if not (isinstance(j, int) and K < 2):
                    hidden_in(K - 2, (k + 1) % 3)

            def hidden_in(K, k):
                act.wait_ge(s_hT_ps, K + 1)
                act.activation(hT[:, k, 0, :], ps_hT[:, 0:P], ACT.Copy)
                size = PIECES[k][1]
                act.activation(hT[0:size, k, 1, :], ps_hT[0:size, P:2 * P], ACT.Copy).then_inc(s_hT, 1)

            def weighted_out(m, n):
                j = GROUP * m + n
                act.wait_ge(s_out_ps, j + 1)
                act.wait_ge(s_meta, j + 1)
                wait(act, s_scat[n], 16 * m)
                act.activation(y_buf[:, n, :], ps_out, ACT.Copy,
                               scale=meta[:, n, 1:2].bitcast(fp32)).then_inc(s_out, 1)

            def round_(i, par, m, pair):
                for p in range(12):
                    if runs_tiles(m):
                        tile_third(m, p // 3, p % 3)
                    if p == 0 and has(i, 2):
                        act.wait_ge(s_o_ps, i - 1)
                        wait(act, s_xf, i - 2)
                        act.activation(oo[:, :], ps_o, ACT.Copy).then_inc(s_o, 1)
                    if p in (0, 1) and has(i, 1):
                        wait(act, s_pT_ps, i - 1)
                        act.wait_ge(s_s_ps, 2 * i - 1 + p)
                        act.activation(probs[:, p * 512:(p + 1) * 512], ps_s[p], ACT.Copy).then_inc(s_s, 1)
                    if p == 3 and has(i, 0):
                        act.wait_ge(s_xT_ps, i + 1)
                        wait(act, s_v_ps, i)
                        act.activation(xnT[:, :], ps_xT.rearrange("p c t -> p (c t)"), ACT.Copy).then_inc(s_xT, 1)
                    if p == 4 and has(i, 1):
                        act.wait_ge(s_sub, i)
                        act.activation(probs[:, :], probs[:, :], ACT.Exp).then_inc(s_exp, 1)
                    if p == 4 and has(i, 0):
                        wait(act, s_s_ps, 2 * (i - 1))
                        act.wait_ge(s_q_ps, i + 1)
                        act.activation(q_sb[:, par, :], ps_q, ACT.Copy).then_inc(s_q_raw, 1)
                    if p == 5 and has(i, 0):
                        act.wait_ge(s_k_ps, i + 1)
                        act.activation(k_sb[:, par, :], ps_k, ACT.Copy).then_inc(s_k_raw, 1)
                    if p == 6 and has(i, 0):
                        wait(act, s_y_ps, i - 1)
                        act.wait_ge(s_v_ps, i + 1)
                        act.activation(v_sb[:, par, :], ps_v, ACT.Copy).then_inc(s_v_raw, 1)
                    if p == 8 and has(i, 2):
                        act.wait_ge(s_xfT_ps, i - 1)
                        wait(act, s_lg_ps, i - 2)
                        act.activation(xfT[:, :], ps_xfT.rearrange("p c t -> p (c t)"), ACT.Copy).then_inc(s_xfT, 1)
                    if p == 9 and has(i, 1):
                        act.wait_ge(s_y_ps, i)
                        wait(act, s_o_ps, i - 1)
                        act.activation(yT[:, :], ps_y, ACT.Copy).then_inc(s_y, 1)
                    if p == 11 and has(i, 2):
                        act.wait_ge(s_gap, i - 1)
                        act.activation(gap_exp[:, :], gap[:, :], ACT.Exp).then_inc(s_gexp, 1)
                    c = weight_chunk(i, p)
                    if c is not None and p % 4 == 0:
                        act.wait_ge(s_stage[c % 2], 16 * (c // 2 + 1))
                        act.activation(gu_w[:, c * PARTS, :], stage[:, c % 2, :], ACT.Copy).then_inc(s_hi, 1)
                    if c is not None and p % 4 == 2:
                        act.wait_ge(s_r1, c + 1)
                        act.activation(gu_w[:, c * PARTS + 1, :], stage[:, c % 2, :], ACT.Copy).then_inc(s_mid, 1)
            rounds(act, round_)

            def group_(m, tiles):
                for n in range(tiles):
                    for k in range(3):
                        tile_third(m, n, k)
            rest_groups(act, group_)
            K = 3 * MOE_TILES
            m, n = MOE_TILES // GROUP, MOE_TILES % GROUP - 1
            hidden_in(K - 2, 1)
            weighted_out(m, n - 1)
            hidden_in(K - 1, 2)
            weighted_out(m, n)

            for g in range(TAIL_GROUPS):
                act.wait_ge(s_tx[g], 16)
                act.wait_ge(s_tshift, g + 1)
                wait(act, s_tdone, g - 1)
                for r in range(TAIL_ROWS):
                    ins = act.activation(tail_xs[:, g % 2, r, :], tail_x[:, g, r, :], ACT.Identity,
                                         bias=tail_shift[:, g % 2, r:r + 1])
                ins.then_inc(s_txs, 1)

        @block.tensor
        def _(pe):
            pe.wait_ge(s_const, CONSTS)
            pe.wait_ge(s_attn_w, 16 * 4)

            def is_last(m, n):
                return isinstance(m, int) and GROUP * m + n + 1 == MOE_TILES

            def transpose_rows(dst, src):
                for c in range(CHUNKS):
                    for t in range(ROW_TILES):
                        last = pe.transpose(dst[:, c, t * P:(t + 1) * P], src(t, c), ident[:, :])
                return last

            def rows_transposed(m, n):
                pe.wait_ge(s_rows[n], 16 * (m + 1))
                wait(pe, s_h, 3 * (GROUP * m + n) - 3)
                for c in range(CHUNKS):
                    last = pe.transpose(ps_xrow[:, c * P:(c + 1) * P],
                                        tile_rows[:, n, c * 64:(c + 1) * 64].bitcast(bf16), ident[:, :])
                last.then_inc(s_xrow_ps, 1)

            def gate_up(m, n, k, first):
                j = GROUP * m + n
                if k == 0:
                    pe.wait_ge(s_xrow, j + 1)
                if k == 2 and not is_last(m, n):
                    pe.wait_ge(s_xrow, j + 2)
                wait(pe, s_h, 3 * j + k - 2)
                w = 2 * THIRDS[k]
                for q in range(CHUNKS * PARTS):
                    last = pe.matmul(ps_gu[k][:, 0:w], xT_buf[:, n % 2, q // PARTS, :],
                                     gu_w[:, bass.ds(first + q, 1), THIRD_AT[k]:THIRD_AT[k] + w]
                                     .rearrange("p a n -> p (a n)"),
                                     start=(q == 0), stop=(q == CHUNKS * PARTS - 1))
                last.then_inc(s_gu, 1)

            def hidden_transposed(K, k):
                pe.wait_ge(s_h, K + 1)
                wait(pe, s_hT, K)
                for q, size in enumerate(PIECES[k]):
                    last = pe.transpose(ps_hT[0:size, q * P:(q + 1) * P],
                                        hidden[:, k, q * P:q * P + size], identf[:, :])
                last.then_inc(s_hT_ps, 1)

            def down_third(m, n, k):
                j = GROUP * m + n
                pe.wait_ge(s_hT, 3 * j + k + 1)
                if k == 0:
                    pe.wait_ge(s_down[n % 2], 16 * (2 * m + n // 2 + 1))
                    wait(pe, s_out, j)
                for q, size in enumerate(PIECES[k]):
                    at = (2 * k + q) * DIM
                    last = pe.matmul(ps_out, hT[0:size, k, q, :], down_w[0:size, n % 2, at:at + DIM],
                                     start=(k == 0 and q == 0), stop=(k == 2 and q == 1))
                if k == 2:
                    last.then_inc(s_out_ps, 1)

            def tile_third(m, n, k, first, attention=None):
                j = GROUP * m + n
                started = not isinstance(j, int)
                gate_up(m, n, k, first)
                if started or 3 * j + k >= 2:
                    hidden_transposed(3 * j + k - 2, (k + 1) % 3)
                if k == 1 and not is_last(m, n):
                    if n < GROUP - 1:
                        rows_transposed(m, n + 1)
                    else:
                        if attention is not None:
                            pe.wait_ge(s_sel, 2 * (m + 2))
                        rows_transposed(m + 1, 0)
                if attention is not None:
                    attention()
                if started or j >= 1:
                    down_third(m if n else m - 1, (n - 1) % GROUP, k)

            def expert_of(table):
                return pe.value_load(table, min_val=0, max_val=EXPERTS - 1) * (CHUNKS * PARTS)

            def attention_part(i, par, p):
                other = 1 - par
                xT3 = xnT[:, :].rearrange("p (c t) -> p c t", c=CHUNKS)
                if p == 0 and has(i, 2):
                    pe.wait_ge(s_y, i - 1)
                    wait(pe, s_xfT, i - 2)
                    y3 = yT[:, :].rearrange("p (c t) -> p c t", c=CHUNKS)
                    for t in range(ROW_TILES):
                        for c in range(CHUNKS):
                            last = pe.matmul(ps_o[:, t * DIM:(t + 1) * DIM], y3[:, c, t * P:(t + 1) * P],
                                             attn_w[:, 3, c, :], start=(c == 0), stop=(c == CHUNKS - 1))
                    last.then_inc(s_o_ps, 1)
                if p in (0, 1) and has(i, 1):
                    if p == 0:
                        pe.wait_ge(s_q, i)
                        pe.wait_ge(s_k, i)
                        if has(i, 3):
                            pe.wait_ge(c_rt, (i - 3) * RT_LINKS + 1)
                        else:
                            wait(pe, s_pT, i - 1)
                    else:
                        wait(pe, s_y, i - 1)
                    for t in range(ROW_TILES):
                        last = pe.matmul(ps_s[p][:, t * SEQ:(t + 1) * SEQ],
                                         q_sb[:, other, p * SEQ + t * P:p * SEQ + (t + 1) * P],
                                         k_sb[:, other, p * SEQ:(p + 1) * SEQ], start=True, stop=True)
                    last.then_inc(s_s_ps, 1)
                if p == 2 and has(i, 3):
                    pe.wait_ge(s_count, i - 2)
                    if has(i, 1):
                        wait(pe, s_s, 2 * i)
                    for t in range(ROW_TILES):
                        dst = ps_place[:, t * EXPERTS:(t + 1) * EXPERTS]
                        pe.matmul(dst, before[:, :], mask[:, t, :], start=True, stop=False)
                        for u in range(t):
                            pe.matmul(dst, ones[:, :], mask[:, u, :], start=False, stop=False)
                        pe.matmul(dst, ones[:, :], count[:, other, :], start=False, stop=True)
                    pe.matmul(ps_total, ones[:, :], count[:, par, :], start=True, stop=True
                              ).then_inc(s_place_ps, 1)
                if p == 3 and has(i, 0):
                    pe.wait_ge(s_xn, i + 1)
                    if has(i, 2):
                        wait(pe, s_o, i - 1)
                    elif not has(i, 2):
                        wait(pe, s_v_raw, i)
                    transpose_rows(ps_xT, lambda t, c: xn[:, t * DIM + c * P:t * DIM + (c + 1) * P]
                                   ).then_inc(s_xT_ps, 1)
                if p in (4, 5) and has(i, 0):
                    n, ps, done = ((0, ps_q, s_q_ps), (1, ps_k, s_k_ps))[p - 4]
                    pe.wait_ge(s_xT, i + 1)
                    if p == 4 and has(i, 1):
                        wait(pe, s_s, 2 * i - 1)
                    if p == 5 and has(i, 1):
                        wait(pe, s_s, 2 * i)
                    if p == 5 and has(i, 3):
                        wait(pe, s_placed, i - 2)
                    for h in range(HEADS):
                        for c in range(CHUNKS):
                            last = pe.matmul(ps[:, h * SEQ:(h + 1) * SEQ],
                                             attn_w[:, n, c, h * HEAD_DIM:(h + 1) * HEAD_DIM],
                                             xT3[:, c, :], start=(c == 0), stop=(c == CHUNKS - 1))
                    last.then_inc(done, 1)
                if p == 6 and has(i, 0):
                    for t in range(ROW_TILES):
                        for c in range(CHUNKS):
                            last = pe.matmul(ps_v[:, t * DIM:(t + 1) * DIM], xT3[:, c, t * P:(t + 1) * P],
                                             attn_w[:, 2, c, :], start=(c == 0), stop=(c == CHUNKS - 1))
                    last.then_inc(s_v_ps, 1)
                if p == 7 and has(i, 1):
                    pe.wait_ge(s_p, i)
                    if has(i, 0):
                        wait(pe, s_q_raw, i + 1)
                    for h in range(HEADS):
                        for kt in range(ROW_TILES):
                            for t in range(ROW_TILES):
                                o = (h * ROW_TILES + kt) * SEQ + t * P
                                s = (h * ROW_TILES + t) * SEQ + kt * P
                                last = pe.transpose(ps_pT[:, o:o + P], probs[:, s:s + P], ident[:, :])
                    last.then_inc(s_pT_ps, 1)
                if p == 8 and has(i, 2):
                    pe.wait_ge(s_xf, i - 1)
                    if has(i, 0):
                        wait(pe, s_v_raw, i + 1)
                    transpose_rows(ps_xfT, lambda t, c: payload[:, par * 4 + t * TOP_K, c * 64:(c + 1) * 64]
                                   .bitcast(bf16)).then_inc(s_xfT_ps, 1)
                if p == 9 and has(i, 1):
                    pe.wait_ge(s_pT, i)
                    pe.wait_ge(s_v, i)
                    if has(i, 0):
                        wait(pe, s_k_raw, i + 1)
                    for h in range(HEADS):
                        for kt in range(ROW_TILES):
                            o = (h * ROW_TILES + kt) * SEQ
                            last = pe.matmul(ps_y[:, h * SEQ:(h + 1) * SEQ],
                                             v_sb[:, other, kt * DIM + h * HEAD_DIM:kt * DIM + (h + 1) * HEAD_DIM],
                                             probsT[:, o:o + SEQ], start=(kt == 0), stop=(kt == ROW_TILES - 1))
                    last.then_inc(s_y_ps, 1)
                if p == 10 and has(i, 2):
                    pe.wait_ge(s_xfT, i - 1)
                    if has(i, 1):
                        wait(pe, s_pT, i)
                    pe.wait_ge(s_router, 1)
                    f3 = xfT[:, :].rearrange("p (c t) -> p c t", c=CHUNKS)
                    for t in range(ROW_TILES):
                        for n in range(CHUNKS * PARTS):
                            c, part = n % CHUNKS, n // CHUNKS
                            last = pe.matmul(ps_logits[:, t * EXPERTS:(t + 1) * EXPERTS],
                                             f3[:, c, t * P:(t + 1) * P], router_w[:, part, c, :],
                                             start=(n == 0), stop=(n == CHUNKS * PARTS - 1))
                    last.then_inc(s_lg_ps, 1)

            def round_(i, par, m, pair):
                tiles = runs_tiles(m)
                if isinstance(m, int) and m == 0:
                    pe.wait_ge(s_lo, WEIGHT_CHUNKS)
                    pe.wait_ge(s_sel, 2)
                    rows_transposed(0, 0)
                if tiles:
                    firsts = [expert_of(chosen_tiles[0:1, par, 1, n:n + 1]) for n in range(GROUP)]
                for p in range(12):
                    n, k = p // 3, p % 3
                    if not tiles:
                        attention_part(i, par, p)
                        continue
                    tile_third(m, n, k, firsts[n], lambda: attention_part(i, par, p))
            rounds(pe, round_)

            def group_(m, tiles):
                for n in range(tiles):
                    at = GROUP * (m - GROUPS_IN_ROUNDS) + n
                    first = expert_of(rest_tiles[0:1, 1, bass.ds(at, 1)])
                    for k in range(3):
                        tile_third(m, n, k, first)
            rest_groups(pe, group_)
            last_k = 3 * MOE_TILES
            m, n = MOE_TILES // GROUP, MOE_TILES % GROUP - 1
            hidden_transposed(last_k - 2, 1)
            down_third(m, n, 0)
            hidden_transposed(last_k - 1, 2)
            down_third(m, n, 1)
            down_third(m, n, 2)

        @block.vector
        def _(dve):
            n_prep = [0]

            def prep(ins):
                n_prep[0] += 1
                ins.then_inc(s_prep, 1)
                dve.wait_ge(s_prep, n_prep[0] + 1)
            dve.wait_ge(s_small, 16 * 5)
            dve.wait_ge(s_const, CONSTS)
            prep(dve.tensor_copy(router_w[:, 0], router32[:, :, :]))
            prep(dve.tensor_tensor(router32[:, :, :], router32[:, :, :], router_w[:, 0], ALU.subtract))
            prep(dve.tensor_copy(router_w[:, 1], router32[:, :, :]))
            dve.tensor_tensor(router_w[:, 2], router32[:, :, :], router_w[:, 1], ALU.subtract).then_inc(s_router, 1)

            def norm_stats(link, which, src):
                for t in range(ROW_TILES):
                    ins = dve.bn_stats(ln_stats[:, which, t, :], src[:, t, :])
                link(ins)
                dve.tensor_tensor(ln_sum[:, which, :], ln_stats[:, which, :, 1], ln_stats[:, which, :, 4], ALU.add)
                for t in range(ROW_TILES):
                    ins = dve.bn_aggr(ln_mv[:, which, t, :], ln_stats[:, which, t, :])
                link(ins)
                dve.tensor_scalar(ln_mean[:, which, :], ln_sum[:, which, :], 0.5, None, ALU.mult)
                dve.tensor_scalar(ln_var[:, which, :], ln_mv[:, which, :, 1], EPS_BF16, None, ALU.add
                                  ).then_inc(s_var[which], 1)

            def norm_rows(link, which, b, src, dsts, centred):
                dve.wait_ge(s_root[which], b + 1)
                link(dve.reciprocal(ln_inv[:, which, :], ln_std[:, which, :]))
                for t in range(ROW_TILES):
                    ins = dve.tensor_scalar(centred[:, t, :], src[:, t, :], ln_mean[:, which, t:t + 1],
                                            None, ALU.subtract)
                link(ins)
                for d in dsts:
                    for t in range(ROW_TILES):
                        ins = dve.tensor_scalar(d(t), centred[:, t, :], ln_inv[:, which, t:t + 1], None, ALU.mult)
                return ins

            def softmax_maxima(i, link):
                dve.wait_ge(s_s, 2 * i)
                link(dve.tensor_scalar(probs[:, :], probs[:, :], SCALE_BF16, None, ALU.mult))
                p4 = probs[:, :].rearrange("p (u n) -> p u n", u=4)
                link(dve.tensor_reduce(sm_max[:, :], p4, AX.X, ALU.max))

            def softmax_differences():
                p4 = probs[:, :].rearrange("p (u n) -> p u n", u=4)
                for u in range(4):
                    ins = dve.tensor_scalar(p4[:, u, :], p4[:, u, :], sm_max[:, u:u + 1], None, ALU.subtract)
                ins.then_inc(s_sub, 1)

            def softmax_quotients(i, link):
                dve.wait_ge(s_exp, i)
                p4 = probs[:, :].rearrange("p (u n) -> p u n", u=4)
                link(dve.tensor_reduce(sm_total[:, :], p4, AX.X, ALU.add))
                link(dve.tensor_copy(sm_sum[:, :], sm_total[:, :]))
                link(dve.reciprocal(sm_inv[:, :], sm_sum[:, :]))
                for u in range(4):
                    ins = dve.tensor_scalar(p4[:, u, :], p4[:, u, :], sm_inv[:, u:u + 1], None, ALU.mult)
                ins.then_inc(s_p, 1)

            def projection(i, par, n):
                dst, raw, done = ((q_sb, s_q_raw, s_q), (k_sb, s_k_raw, s_k))[n]
                dve.wait_ge(raw, i + 1)
                for h in range(HEADS):
                    d = dst[:, par, h * SEQ:(h + 1) * SEQ]
                    ins = dve.tensor_scalar(d, d, qk_biasf[:, n, h:h + 1], 0.0, ALU.add, ALU.max)
                ins.then_inc(done, 1)

            def values(i, par):
                dve.wait_ge(s_v_raw, i + 1)
                v = rows(v_sb[:, par, :])
                dve.tensor_tensor(v, v, row_bias[:, 0:1, :].to_broadcast([P, ROW_TILES, DIM]), ALU.add
                                  ).then_inc(s_v_sum, 1)
                dve.wait_ge(s_v_sum, i + 1)
                dve.tensor_scalar(v, v, 0.0, None, ALU.max).then_inc(s_v, 1)

            def output_bias(i, link):
                dve.wait_ge(s_o, i - 1)
                o = rows(oo[:, :])
                link(dve.tensor_tensor(o, o, row_bias[:, 1:2, :].to_broadcast([P, ROW_TILES, DIM]), ALU.add))
                link(dve.tensor_scalar(o, o, 0.0, None, ALU.max))
                norm_stats(link, 1, o)

            def residual_sum(i, par, pair, link):
                o = rows(oo[:, :])
                link(norm_rows(link, 1, i - 2, o, [lambda t: o[:, t, :]], o))
                dve.wait_ge(s_xa[par], 16 * pair)
                wait(dve, s_x1_saved[par], 16 * (pair - 1))
                z = rows(x1[:, par, :])
                dve.tensor_tensor(z, rows(x_again[:, par, :]), o, ALU.add).then_inc(s_x1, 1)
                dve.wait_ge(s_x1, i - 1)
                norm_stats(link, 2, z)

            def expert_input(i, par, pair, link):
                wait(dve, s_sent[par], 16 * ROW_TILES * TOP_K * (pair - 1))
                norm_rows(link, 2, i - 2, rows(x1[:, par, :]), [
                    (lambda t, k=k: payload[:, par * 4 + t * TOP_K + k, 0:DIM // 2].bitcast(bf16))
                    for k in range(TOP_K)], rows(oo[:, :])).then_inc(s_xf, 1)

            def route(i, par, link):
                dve.wait_ge(s_lg_ps, i - 1)
                link(dve.tensor_copy(logits[:, :, :], ps_logits.rearrange("p (t e) -> p t e", t=ROW_TILES)))
                for t in range(ROW_TILES):
                    mine = logits[:, t, :].unsqueeze(2).to_broadcast([P, EXPERTS, EXPERTS])
                    theirs = logits[:, t, :].unsqueeze(1).to_broadcast([P, EXPERTS, EXPERTS])
                    dve.tensor_tensor(above[:, t], theirs, mine, ALU.is_gt)
                    ins = dve.tensor_tensor(level[:, t], theirs, mine, ALU.is_ge)
                link(ins)
                for t in range(ROW_TILES):
                    ins = dve.tensor_tensor(level[:, t], level[:, t], lower[:, :, :], ALU.mult)
                link(ins)
                link(dve.tensor_tensor(above[:, :, :, :], above[:, :, :, :], level[:, :, :, :], ALU.max))
                link(dve.tensor_reduce(rank[:, :, :], above[:, :, :, :], AX.X, ALU.add))
                dve.tensor_scalar(mask[:, :, :], rank[:, :, :], float(TOP_K), None, ALU.is_lt).then_inc(s_mask, 1)
                for k in range(TOP_K):
                    ins = dve.tensor_scalar(chosen[:, :, k, :], rank[:, :, :], float(k), None, ALU.is_equal)
                link(ins)
                for k in range(TOP_K):
                    ins = dve.tensor_tensor(picked[:, :, k, :], chosen[:, :, k, :], logits[:, :, :], ALU.mult)
                link(ins)
                link(dve.tensor_reduce(top[:, :, :], picked[:, :, :, :], AX.X, ALU.add))
                dve.tensor_tensor(gap[:, :], top[:, :, 1], top[:, :, 0], ALU.subtract).then_inc(s_gap, 1)
                link(dve.tensor_tensor(count[:, 1 - par, :], count[:, par, :], mask[:, 0, :], ALU.add))
                dve.tensor_tensor(count[:, 1 - par, :], count[:, 1 - par, :], mask[:, 1, :], ALU.add
                                  ).then_inc(s_count, 1)

            def send(i, par, link):
                dve.wait_ge(s_place_ps, i - 2)
                dve.tensor_copy(total[:, :], ps_total)
                link(dve.tensor_tensor(place[:, :, :], ps_place.rearrange("p (t e) -> p t e", t=ROW_TILES),
                                       region_start[:, :].unsqueeze(1).to_broadcast([P, ROW_TILES, EXPERTS]),
                                       ALU.add))
                for k in range(TOP_K):
                    ins = dve.tensor_tensor(picked2[:, :, k, :], chosen[:, :, k, :], place[:, :, :], ALU.mult)
                ins.then_inc(s_placed, 1)
                dve.wait_ge(s_placed, i - 2)
                link(dve.tensor_reduce(slotf[:, :, :], picked2[:, :, :, :], AX.X, ALU.add))
                dve.tensor_copy(slot[:, par, :], slotf[:, :, :].rearrange("p t k -> p (t k)"))
                dve.wait_ge(s_gexp, i - 2)
                link(dve.tensor_scalar(denom[:, :], gap_exp[:, :], 1.0, None, ALU.add))
                link(dve.reciprocal(prob[:, :, 0], denom[:, :]))
                link(dve.tensor_tensor(prob[:, :, 1], prob[:, :, 0], gap_exp[:, :], ALU.mult))
                pay = payload[:, par * 4:par * 4 + 4, :]
                dve.tensor_copy(pay[:, :, DIM // 2 + 1].bitcast(fp32), prob[:, :, :].rearrange("p t k -> p (t k)"))
                link(dve.tensor_copy(pay[:, :, DIM // 2], dest[:, :, :].rearrange("p t k -> p (t k)")))
                dve.tensor_scalar(dest[:, :, :], dest[:, :, :], SEQ, None, ALU.add).then_inc(s_slot, 1)

            def select(link, tiles, up, table):
                one = [1, tiles, EXPERTS]
                link(dve.tensor_scalar(tile_q[:, :], total[0:1, :], 1.0 / P, (0.5 - 0.5 / P) * (1 if up else -1),
                                       ALU.mult, ALU.add))
                link(dve.tensor_scalar(tiles_full[:, :], tile_q[:, :], ROUNDER, -ROUNDER, ALU.add, ALU.add))
                link(dve.tensor_tensor(tiles_left[:, :], tiles_full[:, :], tiles_run[:, :], ALU.subtract))
                link(dve.tensor_tensor(left_below[:, :, :], lower[0:1, :, :],
                                       tiles_left[:, :].unsqueeze(1).to_broadcast([1, EXPERTS, EXPERTS]), ALU.mult))
                link(dve.tensor_reduce(below[:, :], left_below[:, :, :], AX.X, ALU.add))
                link(dve.tensor_tensor(upto[:, :], below[:, :], tiles_left[:, :], ALU.add))
                dve.tensor_scalar(taken[:, :], below[:, :], -1.0, float(tiles), ALU.mult, ALU.add)
                link(dve.tensor_tensor(full_less[:, :], tiles_full[:, :], upto[:, :], ALU.subtract))
                link(dve.scalar_tensor_tensor(start_row[:, 0:EXPERTS], full_less[:, :], float(P),
                                              region_start[0:1, :], ALU.mult, ALU.add))
                dve.tensor_tensor(reached[:, 0:tiles, :], nth[:, 0:tiles].unsqueeze(2).to_broadcast(one),
                                  upto[:, :].unsqueeze(1).to_broadcast(one), ALU.is_ge)
                link(dve.tensor_tensor(row_step[:, :], start_row[:, 1:], start_row[:, 0:EXPERTS], ALU.subtract))
                dve.tensor_reduce(sel_expert[:, 0:tiles], reached[:, 0:tiles, :], AX.X, ALU.add)
                link(dve.tensor_tensor(stepped[:, 0:tiles, :], reached[:, 0:tiles, :],
                                       row_step[:, :].unsqueeze(1).to_broadcast(one), ALU.mult))
                link(dve.scalar_tensor_tensor(taken[:, :], taken[:, :], 0.0, tiles_left[:, :], ALU.max, ALU.min))
                link(dve.tensor_reduce(sel_row[:, 0:tiles], stepped[:, 0:tiles, :], AX.X, ALU.add))
                dve.tensor_tensor(tiles_run[:, :], tiles_run[:, :], taken[:, :], ALU.add)
                link(dve.scalar_tensor_tensor(sel_rowf[:, 0:tiles], sel_row[:, 0:tiles], start_row[:, 0:1],
                                              nth_row[:, 0:tiles], ALU.add, ALU.add))
                dve.tensor_scalar(table[0], sel_rowf[:, 0:tiles], float(DUMMY_ROW), None, ALU.min
                                  ).then_inc(s_sel, 1)
                dve.tensor_scalar(table[1], sel_expert[:, 0:tiles], float(EXPERTS - 1), None, ALU.min
                                  ).then_inc(s_sel, 1)

            def rows_in(m, n):
                j = GROUP * m + n
                dve.wait_ge(s_xrow_ps, j + 1)
                dve.tensor_copy(xT_buf[:, n % 2, :, :].rearrange("p c t -> p (c t)"), ps_xrow).then_inc(s_xrow, 1)
                wait(dve, s_scat[n], 16 * m)
                dve.tensor_copy(meta[:, n, :], tile_rows[:, n, DIM // 2:]).then_inc(s_meta, 1)

            def multiply(m, n, k):
                K = 3 * (GROUP * m + n) + k
                w = THIRDS[k]
                dve.wait_ge(s_gated, K + 1)
                wait(dve, s_hT_ps, K - 2)
                dve.tensor_tensor(hidden[:, k, 0:w], gated[:, k, 0:w], ps_gu[k][:, w:2 * w], ALU.mult
                                  ).then_inc(s_h, 1)

            def round_(i, par, m, pair):
                other = 1 - par
                x3, xn3 = rows(x_in[:, par, :]), rows(xn[:, :])
                link1, n1 = chain(dve, c_ln1, i * LN_LINKS)
                link2, n2 = chain(dve, c_out, (i - 2) * OUT_LINKS)
                link3, n3 = chain(dve, c_rt, (i - 2) * RT_LINKS)
                link4, n4 = chain(dve, c_send, (i - 3) * SEND_LINKS)
                link5, n5 = chain(dve, c_sm, (i - 1) * SM_LINKS)
                tiles = runs_tiles(m)
                if isinstance(m, int) and m == 0:
                    rows_in(0, 0)
                for p in range(12):
                    n, k = p // 3, p % 3
                    if p == 0 and has(i, 0):
                        dve.wait_ge(s_x[par], 16 * (pair + 1))
                        norm_stats(link1, 0, x3)
                    if p == 1 and has(i, 2):
                        output_bias(i, link2)
                    if p == 2 and has(i, 0):
                        wait(dve, s_xT_ps, i)
                        norm_rows(link1, 0, i, x3, [lambda t: xn3[:, t, :]], xn3).then_inc(s_xn, 1)
                        assert n1[0] == LN_LINKS
                    if p == 2 and has(i, 1):
                        softmax_maxima(i, link5)
                    if p == 3 and has(i, 1):
                        softmax_differences()
                    if p == 3 and has(i, 2):
                        residual_sum(i, par, pair, link2)
                    if p == 4 and has(i, 3):
                        send(i, other, link4)
                        assert n4[0] == SEND_LINKS, n4
                    if p == 5 and (tiles or isinstance(i, int) and i == FIRST_ROUND - 1):
                        if isinstance(i, int) and i == ROUNDS - 1:
                            link6, n6 = chain(dve, c_sel, (m + 1) * SEL_LINKS)
                            link6(dve.tensor_tensor(pad_place[:, :], pad_place[:, :], total[:, :], ALU.add))
                            dve.tensor_copy(pad_slot[:, :], pad_place[:, :]).then_inc(s_pad, 1)
                            select(link6, REST, True, [rest_tiles[:, t, :] for t in range(2)])
                        else:
                            link6, n6 = chain(dve, c_sel, (m + 1) * SEL_LINKS)
                            select(link6, GROUP, False, [chosen_tiles[:, other, t, :] for t in range(2)])
                            assert n6[0] == SEL_LINKS, n6
                    if p == 5 and has(i, 0):
                        projection(i, par, 0)
                    if p == 6 and has(i, 1):
                        softmax_quotients(i, link5)
                        assert n5[0] == SM_LINKS, n5
                    if p == 6 and has(i, 0):
                        projection(i, par, 1)
                    if p == 7 and has(i, 2):
                        expert_input(i, par, pair, link2)
                        assert n2[0] == OUT_LINKS, n2
                    if p == 7 and has(i, 0):
                        values(i, par)
                    if p == 8 and has(i, 1):
                        dve.wait_ge(s_pT_ps, i)
                        wait(dve, s_y_ps, i - 1)
                        dve.tensor_copy(probsT[:, :], ps_pT).then_inc(s_pT, 1)
                    if p == 11 and has(i, 2):
                        route(i, par, link3)
                        assert n3[0] == RT_LINKS, n3
                    c = weight_chunk(i, p)
                    if c is not None and p % 4 == 1:
                        dve.wait_ge(s_hi, c + 1)
                        dve.tensor_tensor(stage[:, c % 2, :], stage[:, c % 2, :], gu_w[:, c * PARTS, :],
                                          ALU.subtract).then_inc(s_r1, 1)
                    if c is not None and p % 4 == 3:
                        dve.wait_ge(s_mid, c + 1)
                        dve.tensor_tensor(gu_w[:, c * PARTS + 2, :], stage[:, c % 2, :],
                                          gu_w[:, c * PARTS + 1, :], ALU.subtract).then_inc(s_lo, 1)
                    if tiles:
                        if k == 1:
                            rows_in(m if n < GROUP - 1 else m + 1, (n + 1) % GROUP)
                        multiply(m, n, k)

            dve.wait_ge(s_prep, 4)
            rounds(dve, round_)

            def group_(m, tiles):
                for n in range(tiles):
                    for k in range(3):
                        if k == 1 and not (isinstance(m, int) and GROUP * m + n + 1 == MOE_TILES):
                            rows_in(m if n < GROUP - 1 else m + 1, (n + 1) % GROUP)
                        multiply(m, n, k)
            rest_groups(dve, group_)

            link, _ = chain(dve, c_tail, 0)
            for g in range(TAIL_GROUPS):
                dve.wait_ge(s_ty[g], 32)
                y0 = tail_y[:, g, 0].rearrange("p r d -> p (r d)")
                link(dve.tensor_tensor(y0, y0, tail_y[:, g, 1].rearrange("p r d -> p (r d)"), ALU.add))
                for r in range(TAIL_ROWS):
                    ins = dve.bn_stats(tail_stats[:, g % 2, r, :], tail_y[:, g, 0, r, :])
                link(ins)
                for r in range(TAIL_ROWS):
                    ins = dve.bn_aggr(tail_mv[:, g % 2, r, :], tail_stats[:, g % 2, r, :])
                link(ins)
                dve.tensor_scalar(tail_var[:, g % 2, :], tail_mv[:, g % 2, :, 1], EPS, None, ALU.add
                                  ).then_inc(s_tvar, 1)
                dve.wait_ge(s_troot, g + 1)
                dve.scalar_tensor_tensor(tail_shift[:, g % 2, :], tail_mv[:, g % 2, :, 0], -1.0,
                                         tail_inv[:, g % 2, :], ALU.mult, ALU.mult).then_inc(s_tshift, 1)
                dve.wait_ge(s_txs, g + 1)
                for r in range(TAIL_ROWS):
                    ins = dve.scalar_tensor_tensor(tail_y[:, g, 0, r, :], tail_y[:, g, 0, r, :],
                                                   tail_inv[:, g % 2, r:r + 1], tail_xs[:, g % 2, r, :],
                                                   ALU.mult, ALU.add)
                ins.then_inc(s_tdone, 1)


CONSTS = 16
SENT = 16 * ROW_TILES * TOP_K
EPS_BF16 = 1.0013580322265625e-05
SCALE_BF16 = 0.08837890625
LN_LINKS, SM_LINKS, OUT_LINKS, RT_LINKS, SEND_LINKS, SEL_LINKS = 4, 5, 11, 9, 6, 13
ROUNDER = 1.5 * 2 ** 23


def kernel(**inputs):
    import numpy as _np
    import concourse.bacc as _bacc
    from concourse import mybir as _mybir
    from concourse.bass_utils import run_bass_kernel_spmd as _run

    def host(name):
        return _np.asarray(inputs[name])

    arrays = {"base": host("L0_attn_base")}
    for n, src in (("wqT", "Wq"), ("wkT", "Wk"), ("wvT", "Wv"), ("woT", "Wo")):
        arrays[n] = host("L0_attn_" + src).T
    for n in ("bq", "bk", "bv", "bo"):
        arrays[n] = host("L0_attn_" + n)
    arrays["routerT"] = host("L0_ffn_router_w").T
    gate = host("L0_ffn_gate_w").transpose(0, 2, 1)
    up = host("L0_ffn_up_w").transpose(0, 2, 1)
    parts, at = [], 0
    for w in THIRDS:
        parts += [gate[:, :, at:at + w], up[:, :, at:at + w]]
        at += w
    arrays["gate_up"] = _np.concatenate(parts, axis=2).reshape(EXPERTS * CHUNKS, P, 2 * FFN)
    dn = host("L0_ffn_down_w").transpose(0, 2, 1)
    laid = _np.zeros((EXPERTS, P, 6, DIM), dn.dtype)
    at = 0
    for n in range(6):
        size = PIECES[n // 2][n % 2]
        laid[:, :size, n, :] = dn[:, at:at + size, :]
        at += size
    arrays["down"] = laid.reshape(EXPERTS, P, 6 * DIM)

    nc = _bacc.Bacc("TRN2", target_bir_lowering=False, num_devices=1)
    args, named = [], {}
    for name, a in arrays.items():
        a = _np.ascontiguousarray(a)
        named[f"in_{name}_dram"] = a
        args.append(nc.dram_tensor(f"in_{name}_dram", a.shape, _mybir.dt.from_np(a.dtype), kind="ExternalInput").ap())
    out = nc.dram_tensor("out_dram", (TOKENS, DIM), _mybir.dt.float32, kind="ExternalOutput").ap()
    build(nc, *args, out)
    r = _run(nc, [named], core_ids=[0])
    return r.results[0]["out_dram"].reshape(BATCHES, SEQ, DIM)
```

```python
import concourse.bass as bass
from concourse import mybir
from contextlib import ExitStack

BATCHES, SEQ, DIM, HEADS = 16, 256, 256, 2
HEAD_DIM = DIM // HEADS
EXPERTS, FFN, TOP_K = 8, 688, 2
P = 128
TOKENS = BATCHES * SEQ
ROW_TILES = SEQ // P
CHUNKS = DIM // P
SLOTS = TOKENS * TOP_K
MOE_TILES = (SLOTS + EXPERTS * (P - 1)) // P
REGION = TOKENS + P
DUMMY_ROW = EXPERTS * REGION
ROW_WORDS = DIM // 2 + 2
NOWHERE = 1 << 20
THIRDS = (230, 230, FFN - 460)
THIRD_AT = (0, 2 * 230, 4 * 230)
PIECES = tuple((P, w - P) for w in THIRDS)
PARTS = 3
EPS = 1e-5
TAIL_ROWS = 4
TAIL_GROUPS = TOKENS // (P * TAIL_ROWS)
GROUP, LAGS = 4, 3
ROUNDS = BATCHES + LAGS
FIRST_ROUND = 6
GROUPS_IN_ROUNDS = ROUNDS - FIRST_ROUND
REST = MOE_TILES - GROUP * GROUPS_IN_ROUNDS
WEIGHT_CHUNKS = EXPERTS * CHUNKS
HI_CHUNKS = 2
HI_PAIRS = WEIGHT_CHUNKS // HI_CHUNKS
SPLIT_AT = (0, 3, 5, 7, 9, 11, 14, 16, 19, 21, 24, 27, 31, 35, 39, 44)
assert len(SPLIT_AT) == WEIGHT_CHUNKS
for _i in range(FIRST_ROUND, ROUNDS):
    assert (_i - LAGS) * SEQ * TOP_K - EXPERTS * (P - 1) >= GROUP * P * (_i + 1 - FIRST_ROUND)


def build(nc, base, wqT, wkT, wvT, woT, bq, bk, bv, bo, routerT, gate_up, down, out):
    fp32, bf16, i32 = mybir.dt.float32, mybir.dt.bfloat16, mybir.dt.int32
    ALU, ACT, AX = mybir.AluOpType, mybir.ActivationFunctionType, mybir.AxisListType

    dispatched = nc.dram_tensor("dispatched", [DUMMY_ROW + P, ROW_WORDS], i32, kind="Internal").ap()
    expert_out = nc.dram_tensor("expert_out", [SLOTS, DIM], fp32, kind="Internal").ap()
    residual = nc.dram_tensor("residual", [TOKENS, DIM], bf16, kind="Internal").ap()

    ctx = ExitStack()
    with ctx:
        def sb(name, shape, dt):
            return ctx.enter_context(nc.sbuf_tensor(name, shape, dt))

        def pb(name):
            return ctx.enter_context(nc.psum_tensor(name, [P, 512], fp32))

        def sem(name):
            return ctx.enter_context(nc.semaphore(name))

        gu_w = sb("gu_w", [P, EXPERTS * CHUNKS * PARTS, 2 * FFN], bf16)
        down_w = sb("down_w", [P, 2, 6 * DIM], fp32)
        payload = sb("payload", [P, 8, ROW_WORDS], i32)
        tile_rows = sb("tile_rows", [P, GROUP, ROW_WORDS], i32)
        gated_hidden = sb("gated_hidden", [P, 2, 3, THIRDS[0]], fp32)
        gated, hidden = gated_hidden[:, 0], gated_hidden[:, 1]
        attn_w = sb("attn_w", [P, 4, CHUNKS, DIM], bf16)
        qk_bias = sb("qk_bias", [P, 2, HEADS], bf16)
        qk_biasf = sb("qk_biasf", [P, 2, HEADS], fp32)
        row_bias = sb("row_bias", [P, 2, DIM], bf16)
        router32 = sb("router32", [P, CHUNKS, EXPERTS], fp32)
        router_w = sb("router_w", [P, PARTS, CHUNKS, EXPERTS], bf16)
        identf = sb("identf", [P, P], fp32)
        ident = sb("ident", [P, P], bf16)
        before = sb("before", [P, P], bf16)
        ones = sb("ones", [P, P], bf16)
        y_buf = sb("y_buf", [P, GROUP, DIM], fp32)
        xT_buf = sb("xT_buf", [P, 2, CHUNKS, P], bf16)
        meta = sb("meta", [P, GROUP, 2], i32)
        hT = sb("hT", [P, 3, 2, P], fp32)
        ln_stats = sb("ln_stats", [P, 3, ROW_TILES, 6], fp32)
        ln_mv = sb("ln_mv", [P, 3, ROW_TILES, 2], bf16)
        ln_var = sb("ln_var", [P, 3, ROW_TILES], bf16)
        ln_std = sb("ln_std", [P, 3, ROW_TILES], bf16)
        ln_inv = sb("ln_inv", [P, 3, ROW_TILES], fp32)
        ln_sum = sb("ln_sum", [P, 3, ROW_TILES], fp32)
        ln_mean = sb("ln_mean", [P, 3, ROW_TILES], bf16)
        half = sb("half", [P, ROW_TILES], bf16)
        pace = sb("pace", [P, 2], bf16)
        minus_half = sb("minus_half", [P, TAIL_ROWS], fp32)
        tail_var = sb("tail_var", [P, 3, TAIL_ROWS], fp32)
        sm_max = sb("sm_max", [P, 4], fp32)
        sm_total = sb("sm_total", [P, 4], fp32)
        sm_sum = sb("sm_sum", [P, 4], bf16)
        sm_inv = sb("sm_inv", [P, 4], fp32)
        logits = sb("logits", [P, ROW_TILES, EXPERTS], fp32)
        above = sb("above", [P, ROW_TILES, EXPERTS, EXPERTS], fp32)
        level = sb("level", [P, ROW_TILES, EXPERTS, EXPERTS], fp32)
        lower = sb("lower", [P, EXPERTS, EXPERTS], fp32)
        rank = sb("rank", [P, ROW_TILES, EXPERTS], fp32)
        chosen = sb("chosen", [P, ROW_TILES, TOP_K, EXPERTS], fp32)
        picked = sb("picked", [P, ROW_TILES, TOP_K, EXPERTS], fp32)
        picked2 = sb("picked2", [P, ROW_TILES, TOP_K, EXPERTS], fp32)
        top = sb("top", [P, ROW_TILES, TOP_K], fp32)
        gap = sb("gap", [P, ROW_TILES], fp32)
        gap_exp = sb("gap_exp", [P, ROW_TILES], fp32)
        denom = sb("denom", [P, ROW_TILES], fp32)
        prob = sb("prob", [P, ROW_TILES, TOP_K], fp32)
        mask = sb("mask", [P, ROW_TILES, EXPERTS], bf16)
        count = sb("count", [P, 2, EXPERTS], bf16)
        place = sb("place", [P, ROW_TILES, EXPERTS], fp32)
        region_start = sb("region_start", [P, EXPERTS], fp32)
        slotf = sb("slotf", [P, ROW_TILES, TOP_K], fp32)
        slot = sb("slot", [P, 2, ROW_TILES * TOP_K], i32)
        dest = sb("dest", [P, ROW_TILES, TOP_K], i32)
        pad_place = sb("pad_place", [P, EXPERTS], fp32)
        pad_slot = sb("pad_slot", [P, EXPERTS], i32)
        pad_row = sb("pad_row", [P, ROW_WORDS], i32)
        total = sb("total", [P, EXPERTS], fp32)
        tile_q = sb("tile_q", [1, EXPERTS], fp32)
        tiles_full = sb("tiles_full", [1, EXPERTS], fp32)
        tiles_run = sb("tiles_run", [1, EXPERTS], fp32)
        tiles_left = sb("tiles_left", [1, EXPERTS], fp32)
        left_below = sb("left_below", [1, EXPERTS, EXPERTS], fp32)
        below = sb("below", [1, EXPERTS], fp32)
        upto = sb("upto", [1, EXPERTS], fp32)
        full_less = sb("full_less", [1, EXPERTS], fp32)
        start_row = sb("start_row", [1, EXPERTS + 1], fp32)
        row_step = sb("row_step", [1, EXPERTS], fp32)
        taken = sb("taken", [1, EXPERTS], fp32)
        nth = sb("nth", [1, REST], fp32)
        nth_row = sb("nth_row", [1, REST], fp32)
        reached = sb("reached", [1, REST, EXPERTS], fp32)
        stepped = sb("stepped", [1, REST, EXPERTS], fp32)
        sel_row = sb("sel_row", [1, REST], fp32)
        sel_rowf = sb("sel_rowf", [1, REST], fp32)
        sel_expert = sb("sel_expert", [1, REST], fp32)
        chosen_tiles = sb("chosen_tiles", [1, 2, 2, GROUP], i32)
        rest_tiles = sb("rest_tiles", [1, 2, REST], i32)
        tail_stats = sb("tail_stats", [P, 3, TAIL_ROWS, 6], fp32)
        tail_mv = sb("tail_mv", [P, 3, TAIL_ROWS, 2], fp32)
        tail_inv = sb("tail_inv", [P, 3, TAIL_ROWS], fp32)
        tail_shift = sb("tail_shift", [P, 3, TAIL_ROWS], fp32)

        parts = gu_w[:, :, :].rearrange("p (c a) n -> p c a n", a=PARTS)
        whole = gu_w[:, :, :].rearrange("p a n -> p (a n)").bitcast(fp32).rearrange(
            "p (c n) -> p c n", n=PARTS * FFN)[:, :, FFN:]
        left = [down_w[:, 0, 0:2 * FFN], down_w[:, 1, 0:2 * FFN],
                gated_hidden[:, :, :, :].rearrange("p a k n -> p (a k n)")[:, 0:2 * FFN]]
        work = sb("work", [P, 21 * ROW_TILES * DIM], bf16)
        used = [0]

        def carve(n):
            used[0] += n
            return work[:, used[0] - n:used[0]]

        def carve2(n):
            return carve(2 * n).rearrange("p (b n) -> p b n", b=2)

        W = ROW_TILES * DIM
        x_in, x_again, x1 = carve2(W), carve2(W), carve2(W)
        q_sb, k_sb, v_sb = carve2(W), carve2(W), carve2(W)
        xn, xnT, oo, yT, xfT = carve(W), carve(W), carve(W), carve(W), carve(W)
        probs, probsT = carve(4 * SEQ), carve(4 * SEQ)

        def rows(ap):
            return ap.rearrange("p (t d) -> p t d", t=ROW_TILES)

        TW = TAIL_ROWS * DIM
        over = gu_w[:, :, :].rearrange("p a n -> p (a n)")
        tail_y = over[:, 0:TAIL_GROUPS * 2 * TW * 2].bitcast(fp32).rearrange(
            "p (g k r d) -> p g k r d", g=TAIL_GROUPS, k=TOP_K, d=DIM)
        tail_x = over[:, TAIL_GROUPS * 4 * TW:TAIL_GROUPS * 5 * TW].rearrange(
            "p (g r d) -> p g r d", g=TAIL_GROUPS, d=DIM)

        bank = [pb(f"bank{n}") for n in range(8)]
        bank_a, bank_b, bank_c = bank[5][:, :], bank[6][:, :], bank[7][:, :]
        ps_o, ps_v = bank_a, bank_a
        ps_xT = bank_a.bitcast(bf16)[:, 0:512].rearrange("p (c t) -> p c t", c=CHUNKS)
        ps_xfT = ps_xT
        ps_q, ps_k, ps_y = bank_b, bank_c, bank_c
        ps_s = [bank_b, bank_c]
        ps_pT = bank_b.bitcast(bf16)
        ps_logits = bank_b[:, 0:ROW_TILES * EXPERTS]
        ps_place = bank_c[:, 0:ROW_TILES * EXPERTS]
        ps_total = bank_c[:, 128:128 + EXPERTS]
        ps_gu = [bank[n][:, :] for n in range(3)]
        ps_hT = bank[3][:, 0:2 * P]
        ps_xrow = bank[2][:, 0:P].bitcast(bf16)
        ps_out = bank[4][:, 0:DIM]

        s_const = sem("s_const")
        s_ident = sem("s_ident")
        s_attn_w = sem("s_attn_w")
        s_small = sem("s_small")
        s_prep = sem("s_prep")
        s_router = sem("s_router")
        s_x = [sem(f"s_x_in{n}") for n in range(2)]
        s_xa = [sem(f"s_x_again{n}") for n in range(2)]
        s_xn = sem("s_xn")
        s_xT_ps = sem("s_xT_ps")
        s_xT = sem("s_xT")
        s_var = [sem(f"s_var{n}") for n in range(3)]
        s_root = [sem(f"s_root{n}") for n in range(3)]
        s_count, s_placed = sem("s_count"), sem("s_placed")
        s_paced = [sem("s_paced0"), sem("s_paced1")]
        s_tvar, s_troot = sem("s_tvar"), sem("s_troot")
        s_q_ps, s_k_ps, s_v_ps = sem("s_q_ps"), sem("s_k_ps"), sem("s_v_ps")
        s_q_raw, s_k_raw, s_v_raw = sem("s_q_raw"), sem("s_k_raw"), sem("s_v_raw")
        s_q, s_k, s_v = sem("s_q"), sem("s_k"), sem("s_v")
        s_v_sum = sem("s_v_sum")
        s_s_ps, s_s = sem("s_s_ps"), sem("s_s")
        s_sub, s_exp, s_p = sem("s_sub"), sem("s_exp"), sem("s_p")
        s_pT_ps, s_pT = sem("s_pT_ps"), sem("s_pT")
        s_y_ps, s_y = sem("s_y_ps"), sem("s_y")
        s_o_ps, s_o = sem("s_o_ps"), sem("s_o")
        s_x1, s_x1_saved = sem("s_x1"), [sem(f"s_x1_saved{n}") for n in range(2)]
        s_xf, s_xfT_ps, s_xfT = sem("s_xf"), sem("s_xfT_ps"), sem("s_xfT")
        s_lg_ps = sem("s_lg_ps")
        s_gap, s_gexp = sem("s_gap"), sem("s_gexp")
        s_place_ps, s_slot = sem("s_place_ps"), sem("s_slot")
        s_sent = [sem(f"s_sent{n}") for n in range(2)]
        s_hi = [sem(f"s_hi{n}") for n in range(HI_PAIRS)]
        s_whole = [sem(f"s_whole{n}") for n in range(HI_PAIRS)]
        s_remainder, s_mid, s_lo = sem("s_remainder"), sem("s_mid"), sem("s_lo")
        s_down = [sem("s_down0"), sem("s_down1")]
        c_ln1, c_sm, c_out, c_rt, c_send = sem("c_ln1"), sem("c_sm"), sem("c_out"), sem("c_rt"), sem("c_send")
        c_sel = sem("c_sel")
        s_pad, s_pad_sent, s_sel = sem("s_pad"), sem("s_pad_sent"), sem("s_sel")
        s_rows = [sem(f"s_rows{n}") for n in range(GROUP)]
        s_xrow_ps, s_xrow, s_meta = sem("s_xrow_ps"), sem("s_xrow"), sem("s_meta")
        s_gu, s_gated, s_h, s_hT_ps, s_hT = sem("s_gu"), sem("s_gated"), sem("s_h"), sem("s_hT_ps"), sem("s_hT")
        s_out_ps, s_out = sem("s_out_ps"), sem("s_out")
        s_scat = [sem(f"s_scat{n}") for n in range(GROUP)]
        s_ty = [sem(f"s_ty{n}") for n in range(TAIL_GROUPS)]
        s_tx = [sem(f"s_tx{n}") for n in range(TAIL_GROUPS)]
        c_tail = sem("c_tail")
        s_tshift, s_tnorm, s_tdone = sem("s_tshift"), sem("s_tnorm"), sem("s_tdone")
        s_stored = sem("s_stored")

        def wait(eng, semaphore, value):
            if isinstance(value, int) and value <= 0:
                return
            eng.wait_ge(semaphore, value)

        def chain(eng, semaphore, start):
            n = [0]

            def link(ins):
                n[0] += 1
                ins.then_inc(semaphore, 1)
                eng.wait_ge(semaphore, start + n[0])
            return link, n

        def rounds(eng, round_):
            for i in range(7):
                round_(i, i % 2, i - FIRST_ROUND, i // 2)
            with eng.Fori(4, BATCHES // 2) as pair:
                round_(2 * pair - 1, 1, 2 * pair - 1 - FIRST_ROUND, pair - 1)
                round_(2 * pair, 0, 2 * pair - FIRST_ROUND, pair)
            for i in range(BATCHES - 1, ROUNDS):
                round_(i, i % 2, i - FIRST_ROUND, i // 2)

        def has(i, lag):
            return not isinstance(i, int) or 0 <= i - lag < BATCHES

        def before_tiles(i):
            return isinstance(i, int) and i < FIRST_ROUND

        def last_round(i):
            return isinstance(i, int) and i == ROUNDS - 1

        def runs_tiles(group):
            return not isinstance(group, int) or group >= 0

        def rest_groups(eng, group_):
            with eng.Fori(GROUPS_IN_ROUNDS, MOE_TILES // GROUP) as m:
                group_(m, GROUP)
            group_(MOE_TILES // GROUP, MOE_TILES % GROUP)

        def weight_chunk(i, p, step):
            at = 12 * i + p - step if isinstance(i, int) else -1
            return SPLIT_AT.index(at) if at in SPLIT_AT else None

        block = ctx.enter_context(nc.Block())

        @block.sync
        def _(sp):
            base_rows = base.rearrange("b (t p) d -> b p t d", p=P)
            for n, w in enumerate((wqT, wkT, wvT, woT)):
                sp.dma_start(attn_w[:, n, :, :], w.rearrange("(c p) n -> p c n", p=P)).then_inc(s_attn_w, 16)

            def load_x(b, buf):
                if not (isinstance(b, int) and b < 2):
                    wait(sp, s_xn, b - 1)
                sp.dma_start(rows(x_in[:, buf, :]), base_rows[b]).then_inc(s_x[buf], 16)

            load_x(0, 0)
            sp.dma_start(qk_bias[:, 0, :], bq.rearrange("(h p) -> p h", p=P),
                         allow_slow_non_contiguous=True).then_inc(s_small, 16)
            sp.dma_start(qk_bias[:, 1, :], bk.rearrange("(h p) -> p h", p=P),
                         allow_slow_non_contiguous=True).then_inc(s_small, 16)
            sp.dma_start(row_bias[:, 0, :], bv.rearrange("(a d) -> a d", a=1).to_broadcast([P, DIM])
                         ).then_inc(s_small, 16)
            sp.dma_start(row_bias[:, 1, :], bo.rearrange("(a d) -> a d", a=1).to_broadcast([P, DIM])
                         ).then_inc(s_small, 16)
            sp.dma_start(router32[:, :, :], routerT.rearrange("(c p) e -> p c e", p=P)).then_inc(s_small, 16)
            load_x(1, 1)

            def load_weights(n):
                at = n * HI_CHUNKS
                sp.dma_start(whole[:, at:at + HI_CHUNKS], gate_up[at:at + HI_CHUNKS].rearrange("c p n -> p c n")
                             ).then_inc(s_whole[n], 16)

            def load_rows(m, n, table):
                rows_from(sp.value_load(table, min_val=0, max_val=DUMMY_ROW), m, n)

            def rows_from(row, m, n):
                wait(sp, s_meta, GROUP * m + n - 3)
                sp.dma_start(tile_rows[:, n, :], dispatched[bass.ds(row, P), :]).then_inc(s_rows[n], 16)

            def load_down(m, n, table):
                expert = sp.value_load(table, min_val=0, max_val=EXPERTS - 1)
                wait(sp, s_out_ps, GROUP * m + n - 1)
                sp.dma_start(down_w[:, n % 2, :], down[bass.ds(expert, 1), :, :].rearrange("e p n -> p (e n)")
                             ).then_inc(s_down[n % 2], 16)

            def chosen(kind, par, n):
                return chosen_tiles[0:1, par, kind, n:n + 1]

            def round_(i, par, m, pair):
                if has(i, -1) and not (isinstance(i, int) and i < 1):
                    load_x(i + 1, 1 - par)
                if isinstance(i, int) and i == FIRST_ROUND:
                    sp.wait_ge(s_lo, WEIGHT_CHUNKS)
                if has(i, 2):
                    wait(sp, s_x1, i - 2)
                    sp.dma_start(rows(x_again[:, par, :]), base_rows[i - 2]).then_inc(s_xa[par], 16)
                if isinstance(i, int) and i < 2:
                    for n in range(HI_PAIRS // 2):
                        load_weights(i * HI_PAIRS // 2 + n)
                if runs_tiles(m):
                    for n in range(GROUP - 1):
                        load_rows(m, n + 1, chosen(0, par, n + 1))
                        load_down(m, n, chosen(1, par, n))
                if has(i, 2):
                    wait(sp, s_x1, i - 1)
                    if runs_tiles(m):
                        sp.wait_ge(s_sel, 2 * (m + 2))
                    sp.dma_start(residual[bass.ds((i - 2) * SEQ, SEQ), :].rearrange("(t p) d -> p t d", p=P),
                                 rows(x1[:, par, :])).then_inc(s_x1_saved[par], 16)
                if (runs_tiles(m) or m == -1) and not last_round(i):
                    if not runs_tiles(m):
                        sp.wait_ge(s_sel, 2)
                    row = sp.value_load(chosen(0, 1 - par, 0), min_val=0, max_val=DUMMY_ROW)
                    for q in range(2):
                        done = pair if par == 1 and q == 0 else pair - 1
                        sp.wait_ge(s_sent[q], SENT * done)
                    rows_from(row, m + 1, 0)
                if runs_tiles(m):
                    load_down(m, GROUP - 1, chosen(1, par, GROUP - 1))

            rounds(sp, round_)

            sp.wait_ge(s_sel, 2 * (GROUPS_IN_ROUNDS + 1))
            for q in range(2):
                sp.wait_ge(s_sent[q], SENT * (BATCHES // 2))
            sp.wait_ge(s_pad_sent, 16 * (EXPERTS + 1))
            load_rows(GROUPS_IN_ROUNDS, 0, rest_tiles[0:1, 0, 0:1])

            def group_(m, tiles):
                for n in range(tiles):
                    at = GROUP * (m - GROUPS_IN_ROUNDS) + n
                    if isinstance(m, int) and GROUP * m + n + 1 >= MOE_TILES:
                        pass
                    elif n < GROUP - 1:
                        load_rows(m, n + 1, rest_tiles[0:1, 0, bass.ds(at + 1, 1)])
                    else:
                        load_rows(m + 1, 0, rest_tiles[0:1, 0, bass.ds(at + 1, 1)])
                    load_down(m, n, rest_tiles[0:1, 1, bass.ds(at, 1)])
            rest_groups(sp, group_)

            tok = residual.rearrange("(g p r) d -> g p r d", p=P, r=TAIL_ROWS)
            eo = expert_out.rearrange("(k g p r) d -> g p k r d", k=TOP_K, p=P, r=TAIL_ROWS)
            of = out.rearrange("(g p r) d -> g p r d", p=P, r=TAIL_ROWS)
            sp.wait_ge(s_gu, 3 * MOE_TILES)
            for n in range(2):
                sp.wait_ge(s_x1_saved[n], 16 * BATCHES // 2)
            for g in range(TAIL_GROUPS):
                sp.dma_start(tail_x[:, g], tok[g]).then_inc(s_tx[g], 16)
            for n in range(GROUP):
                sp.wait_ge(s_scat[n], 16 * len(range(n, MOE_TILES, GROUP)))
            for g in range(TAIL_GROUPS):
                for k in range(TOP_K):
                    sp.dma_start(tail_y[:, g, k], eo[g, :, k]).then_inc(s_ty[g], 16)
            for g in range(TAIL_GROUPS):
                sp.wait_ge(s_tdone, g + 1)
                sp.dma_start(of[g], tail_y[:, g, 0]).then_inc(s_stored, 16)
            sp.wait_ge(s_stored, 16 * TAIL_GROUPS)

        @block.gpsimd
        def _(pool):
            pool.memset(ones[:, :], 1.0).then_inc(s_const, 1)
            pool.memset(half[:, :], 0.5).then_inc(s_const, 1)
            pool.memset(minus_half[:, :], -0.5).then_inc(s_const, 1)
            pool.memset(ident[:, :], 0.0).then_inc(s_ident, 1)
            pool.memset(identf[:, :], 0.0).then_inc(s_ident, 1)
            pool.memset(before[:, :], 1.0).then_inc(s_ident, 1)
            pool.memset(lower[:, :, :], 1.0).then_inc(s_ident, 1)
            pool.memset(pad_row[:, :], 0).then_inc(s_ident, 1)
            pool.wait_ge(s_ident, 5)
            for m in (ident, identf):
                pool.affine_select(out=m[:, :], in_=m[:, :], compare_op=ALU.not_equal, fill=1.0, base=0,
                                   pattern=[[-1, P]], channel_multiplier=1).then_inc(s_const, 1)
            pool.affine_select(out=before[:, :], in_=before[:, :], compare_op=ALU.is_gt, fill=0.0, base=0,
                               pattern=[[1, P]], channel_multiplier=-1).then_inc(s_const, 1)
            pool.affine_select(out=lower[:, :, :], in_=lower[:, :, :], compare_op=ALU.is_gt, fill=0.0, base=0,
                               pattern=[[1, EXPERTS], [-1, EXPERTS]], channel_multiplier=0).then_inc(s_const, 1)
            pool.memset(pad_row[:, DIM // 2:DIM // 2 + 1], NOWHERE).then_inc(s_const, 1)
            pool.memset(count[:, 0, :], 0.0).then_inc(s_const, 1)
            pool.iota(dest[:, :, :], pattern=[[P, ROW_TILES], [TOKENS, TOP_K]], base=0,
                      channel_multiplier=1).then_inc(s_const, 1)
            pool.iota(region_start[:, :], pattern=[[REGION, EXPERTS]], base=0, channel_multiplier=0,
                      allow_small_or_imprecise_dtypes=True).then_inc(s_const, 1)
            pool.iota(pad_place[:, :], pattern=[[REGION, EXPERTS]], base=0, channel_multiplier=1,
                      allow_small_or_imprecise_dtypes=True).then_inc(s_const, 1)
            pool.iota(nth[:, :], pattern=[[1, REST]], base=0, channel_multiplier=0,
                      allow_small_or_imprecise_dtypes=True).then_inc(s_const, 1)
            pool.iota(nth_row[:, :], pattern=[[P, REST]], base=0, channel_multiplier=0,
                      allow_small_or_imprecise_dtypes=True).then_inc(s_const, 1)
            pool.memset(tiles_run[:, :], 0.0).then_inc(s_const, 1)
            pool.memset(start_row[:, EXPERTS:EXPERTS + 1], float(DUMMY_ROW)).then_inc(s_const, 1)
            for n in range(HI_PAIRS):
                at = n * HI_CHUNKS
                pool.dma_start(parts[:, at:at + HI_CHUNKS, 0, :],
                               gate_up[at:at + HI_CHUNKS].rearrange("c p n -> p c n")).then_inc(s_hi[n], 16)
            pool.wait_ge(s_const, CONSTS)
            pool.dma_start(dispatched[DUMMY_ROW:DUMMY_ROW + P, :], pad_row[:, :]).then_inc(s_pad_sent, 16)

            last_row, last_slot = pool.to_reg(DUMMY_ROW - 1), pool.to_reg(SLOTS - 1)

            def carry_wait(which, earlier):
                wait(pool, s_paced[which], earlier)
                pool.tensor_tensor(pace[:, which:which + 1], half[:, 0:1], half[:, 0:1], ALU.mult
                                   ).then_inc(s_paced[which], 1)

            def dispatch(b, par):
                pool.wait_ge(s_slot, b + 1)
                carry_wait(0, b)
                for t in range(ROW_TILES):
                    for k in range(TOP_K):
                        n = t * TOP_K + k
                        pool.indirect_dma_start(
                            out=dispatched, out_offset=bass.IndirectOffsetOnAxis(ap=slot[:, par, n:n + 1], axis=0),
                            in_=payload[:, par * 4 + n, :], in_offset=None,
                            bounds_check=last_row, oob_is_err=False).then_inc(s_sent[par], 16)
            def root(which, b):
                pool.wait_ge(s_var[which], b + 1)
                pool.tensor_tensor(ln_std[:, which, :], ln_var[:, which, :], half[:, :], ALU.pow
                                   ).then_inc(s_root[which], 1)

            def send_back(m, n):
                pool.wait_ge(s_out, GROUP * m + n + 1)
                carry_wait(1, GROUP * m + n)
                pool.indirect_dma_start(
                    out=expert_out, out_offset=bass.IndirectOffsetOnAxis(ap=meta[:, n, 0:1], axis=0),
                    in_=y_buf[:, n, :], in_offset=None,
                    bounds_check=last_slot, oob_is_err=False).then_inc(s_scat[n], 16)

            def send_padding():
                pool.wait_ge(s_pad, 1)
                for e in range(EXPERTS):
                    pool.indirect_dma_start(
                        out=dispatched, out_offset=bass.IndirectOffsetOnAxis(ap=pad_slot[:, e:e + 1], axis=0),
                        in_=pad_row[:, :], in_offset=None,
                        bounds_check=last_row, oob_is_err=False).then_inc(s_pad_sent, 16)

            def split_remainders(i, positions):
                for p in positions:
                    c = weight_chunk(i, p, 0)
                    if c is not None:
                        pool.wait_ge(s_whole[c // HI_CHUNKS], 16)
                        pool.wait_ge(s_hi[c // HI_CHUNKS], 16)
                        wait(pool, s_lo, c - 2)
                        pool.tensor_tensor(left[c % 3], whole[:, c], gu_w[:, c * PARTS, :], ALU.subtract
                                           ).then_inc(s_remainder, 1)

            def round_(i, par, m, pair):
                tiles = runs_tiles(m)
                split_remainders(i, range(0, 2))
                if tiles and not (isinstance(m, int) and m == 0):
                    send_back(m - 1, 2)
                if last_round(i):
                    dispatch(i - 3, 1 - par)
                    send_padding()
                if has(i, 2):
                    root(1, i - 2)
                if tiles and not (isinstance(m, int) and m == 0):
                    send_back(m - 1, 3)
                split_remainders(i, range(2, 5))
                if has(i, 2):
                    root(2, i - 2)
                split_remainders(i, range(5, 10))
                if has(i, 3) and not last_round(i):
                    dispatch(i - 3, 1 - par)
                if tiles:
                    send_back(m, 0)
                    send_back(m, 1)
                if has(i, -1):
                    root(0, i + 1)
                split_remainders(i, range(10, 12))
            root(0, 0)
            rounds(pool, round_)

            def group_(m, tiles):
                send_back(m - 1, 2)
                send_back(m - 1, 3)
                for n in range(max(0, tiles - (2 if tiles == GROUP else 0))):
                    send_back(m, n)
            rest_groups(pool, group_)

            def add_residual(g):
                pool.wait_ge(s_tx[g], 16)
                pool.wait_ge(s_tnorm, g + 1)
                z = tail_y[:, g, 0].rearrange("p r d -> p (r d)")
                pool.tensor_tensor(z, z, tail_x[:, g].rearrange("p r d -> p (r d)"), ALU.add).then_inc(s_tdone, 1)

            for g in range(TAIL_GROUPS):
                pool.wait_ge(s_tvar, g + 1)
                pool.tensor_tensor(tail_inv[:, g % 3, :], tail_var[:, g % 3, :], minus_half[:, :], ALU.pow
                                   ).then_inc(s_troot, 1)
                if g >= 1:
                    add_residual(g - 1)
            add_residual(TAIL_GROUPS - 1)

        @block.scalar
        def _(act):
            act.wait_ge(s_small, 16 * 5)
            act.activation(qk_biasf[:, :, :], qk_bias[:, :, :], ACT.Copy).then_inc(s_prep, 1)

            def tile_third(m, n, k):
                j = GROUP * m + n
                K = 3 * j + k
                w = THIRDS[k]
                if k == 0 and not (isinstance(j, int) and j < 2):
                    weighted_out(m if n >= 2 else m - 1, (n + 2) % GROUP)
                act.wait_ge(s_gu, K + 1)
                wait(act, s_h, K - 2)
                act.activation(gated[:, k, 0:w], ps_gu[k][:, 0:w], ACT.Silu).then_inc(s_gated, 1)
                if not (isinstance(j, int) and K < 2):
                    hidden_in(K - 2, (k + 1) % 3)

            def hidden_in(K, k):
                act.wait_ge(s_hT_ps, K + 1)
                act.activation(hT[:, k, 0, :], ps_hT[:, 0:P], ACT.Copy)
                size = PIECES[k][1]
                act.activation(hT[0:size, k, 1, :], ps_hT[0:size, P:2 * P], ACT.Copy).then_inc(s_hT, 1)

            def weighted_out(m, n):
                j = GROUP * m + n
                act.wait_ge(s_out_ps, j + 1)
                act.wait_ge(s_meta, j + 1)
                wait(act, s_scat[n], 16 * m)
                act.activation(y_buf[:, n, :], ps_out, ACT.Copy,
                               scale=meta[:, n, 1:2].bitcast(fp32)).then_inc(s_out, 1)

            def projection(i, dst, ps, n, raw, done):
                act.activation(dst, ps, ACT.Copy).then_inc(raw, 1)
                if not before_tiles(i):
                    return
                act.wait_ge(raw, i + 1)
                for h in range(HEADS):
                    d = dst[:, h * SEQ:(h + 1) * SEQ]
                    ins = act.activation(d, d, ACT.Relu, bias=qk_biasf[:, n, h:h + 1])
                ins.then_inc(done, 1)

            def round_(i, par, m, pair):
                for p in range(12):
                    if runs_tiles(m):
                        tile_third(m, p // 3, p % 3)
                    if p == 0 and has(i, 2):
                        act.wait_ge(s_o_ps, i - 1)
                        wait(act, s_xf, i - 2)
                        act.activation(oo[:, :], ps_o, ACT.Copy).then_inc(s_o, 1)
                    if p in (0, 1) and has(i, 1):
                        wait(act, s_pT_ps, i - 1)
                        act.wait_ge(s_s_ps, 2 * i - 1 + p)
                        act.activation(probs[:, p * 512:(p + 1) * 512], ps_s[p], ACT.Copy).then_inc(s_s, 1)
                    if p == 3 and has(i, 0):
                        act.wait_ge(s_xT_ps, i + 1)
                        wait(act, s_v_ps, i)
                        act.activation(xnT[:, :], ps_xT.rearrange("p c t -> p (c t)"), ACT.Copy).then_inc(s_xT, 1)
                    if p == (0 if last_round(i) else 4) and has(i, 3):
                        act.wait_ge(s_gap, i - 2)
                        act.activation(gap_exp[:, :], gap[:, :], ACT.Exp).then_inc(s_gexp, 1)
                    if p == 4 and has(i, 1):
                        act.wait_ge(s_sub, i)
                        act.activation(probs[:, :], probs[:, :], ACT.Exp).then_inc(s_exp, 1)
                    if p == 4 and has(i, 0):
                        wait(act, s_s_ps, 2 * (i - 1))
                        act.wait_ge(s_q_ps, i + 1)
                        projection(i, q_sb[:, par, :], ps_q, 0, s_q_raw, s_q)
                    if p == 5 and has(i, 0):
                        act.wait_ge(s_k_ps, i + 1)
                        projection(i, k_sb[:, par, :], ps_k, 1, s_k_raw, s_k)
                    if p == 6 and has(i, 0):
                        wait(act, s_y_ps, i - 1)
                        act.wait_ge(s_v_ps, i + 1)
                        act.activation(v_sb[:, par, :], ps_v, ACT.Copy).then_inc(s_v_raw, 1)
                    if p == 9 and has(i, 2):
                        act.wait_ge(s_xfT_ps, i - 1)
                        wait(act, s_lg_ps, i - 2)
                        act.activation(xfT[:, :], ps_xfT.rearrange("p c t -> p (c t)"), ACT.Copy).then_inc(s_xfT, 1)
                    if p == 9 and has(i, 1):
                        act.wait_ge(s_y_ps, i)
                        wait(act, s_o_ps, i - 1)
                        act.activation(yT[:, :], ps_y, ACT.Copy).then_inc(s_y, 1)
                    c = weight_chunk(i, p, 1)
                    if c is not None:
                        act.wait_ge(s_remainder, c + 1)
                        act.activation(gu_w[:, c * PARTS + 1, :], left[c % 3], ACT.Copy).then_inc(s_mid, 1)
            rounds(act, round_)

            def group_(m, tiles):
                for n in range(tiles):
                    for k in range(3):
                        tile_third(m, n, k)
            rest_groups(act, group_)
            K = 3 * MOE_TILES
            m, n = MOE_TILES // GROUP, MOE_TILES % GROUP - 1
            hidden_in(K - 2, 1)
            weighted_out(m, n - 1)
            hidden_in(K - 1, 2)
            weighted_out(m, n)

            for g in range(TAIL_GROUPS):
                act.wait_ge(s_tshift, g + 1)
                for r in range(TAIL_ROWS):
                    ins = act.activation(tail_y[:, g, 0, r, :], tail_y[:, g, 0, r, :], ACT.Identity,
                                         bias=tail_shift[:, g % 3, r:r + 1], scale=tail_inv[:, g % 3, r:r + 1])
                ins.then_inc(s_tnorm, 1)

        @block.tensor
        def _(pe):
            pe.wait_ge(s_const, CONSTS)
            pe.wait_ge(s_attn_w, 16 * 4)

            def is_last(m, n):
                return isinstance(m, int) and GROUP * m + n + 1 == MOE_TILES

            def transpose_rows(dst, src):
                for c in range(CHUNKS):
                    for t in range(ROW_TILES):
                        last = pe.transpose(dst[:, c, t * P:(t + 1) * P], src(t, c), ident[:, :])
                return last

            def rows_transposed(m, n):
                pe.wait_ge(s_rows[n], 16 * (m + 1))
                wait(pe, s_h, 3 * (GROUP * m + n) - 3)
                for c in range(CHUNKS):
                    last = pe.transpose(ps_xrow[:, c * P:(c + 1) * P],
                                        tile_rows[:, n, c * 64:(c + 1) * 64].bitcast(bf16), ident[:, :])
                last.then_inc(s_xrow_ps, 1)

            def gate_up(m, n, k, first):
                j = GROUP * m + n
                if k == 0:
                    pe.wait_ge(s_xrow, j + 1)
                if k == 2 and not is_last(m, n):
                    pe.wait_ge(s_xrow, j + 2)
                wait(pe, s_h, 3 * j + k - 2)
                w = 2 * THIRDS[k]
                for q in range(CHUNKS * PARTS):
                    last = pe.matmul(ps_gu[k][:, 0:w], xT_buf[:, n % 2, q // PARTS, :],
                                     gu_w[:, bass.ds(first + q, 1), THIRD_AT[k]:THIRD_AT[k] + w]
                                     .rearrange("p a n -> p (a n)"),
                                     start=(q == 0), stop=(q == CHUNKS * PARTS - 1))
                last.then_inc(s_gu, 1)

            def hidden_transposed(K, k):
                pe.wait_ge(s_h, K + 1)
                wait(pe, s_hT, K)
                for q, size in enumerate(PIECES[k]):
                    last = pe.transpose(ps_hT[0:size, q * P:(q + 1) * P],
                                        hidden[:, k, q * P:q * P + size], identf[:, :])
                last.then_inc(s_hT_ps, 1)

            def down_third(m, n, k):
                j = GROUP * m + n
                pe.wait_ge(s_hT, 3 * j + k + 1)
                if k == 0:
                    pe.wait_ge(s_down[n % 2], 16 * (2 * m + n // 2 + 1))
                    wait(pe, s_out, j)
                for q, size in enumerate(PIECES[k]):
                    at = (2 * k + q) * DIM
                    last = pe.matmul(ps_out, hT[0:size, k, q, :], down_w[0:size, n % 2, at:at + DIM],
                                     start=(k == 0 and q == 0), stop=(k == 2 and q == 1))
                if k == 2:
                    last.then_inc(s_out_ps, 1)

            def tile_third(m, n, k, first, attention=None):
                j = GROUP * m + n
                started = not isinstance(j, int)
                if k == 1 and not is_last(m, n):
                    if n < GROUP - 1:
                        rows_transposed(m, n + 1)
                    else:
                        if attention is not None:
                            pe.wait_ge(s_sel, 2 * (m + 2))
                        rows_transposed(m + 1, 0)
                gate_up(m, n, k, first)
                if started or 3 * j + k >= 2:
                    hidden_transposed(3 * j + k - 2, (k + 1) % 3)
                if attention is not None:
                    attention()
                if started or j >= 1:
                    down_third(m if n else m - 1, (n - 1) % GROUP, k)

            def expert_of(table):
                return pe.value_load(table, min_val=0, max_val=EXPERTS - 1) * (CHUNKS * PARTS)

            def attention_part(i, par, p):
                other = 1 - par
                xT3 = xnT[:, :].rearrange("p (c t) -> p c t", c=CHUNKS)
                if p == 0 and has(i, 2):
                    pe.wait_ge(s_y, i - 1)
                    wait(pe, s_xfT, i - 2)
                    y3 = yT[:, :].rearrange("p (c t) -> p c t", c=CHUNKS)
                    for t in range(ROW_TILES):
                        for c in range(CHUNKS):
                            last = pe.matmul(ps_o[:, t * DIM:(t + 1) * DIM], y3[:, c, t * P:(t + 1) * P],
                                             attn_w[:, 3, c, :], start=(c == 0), stop=(c == CHUNKS - 1))
                    last.then_inc(s_o_ps, 1)
                if p in (0, 1) and has(i, 1):
                    if p == 0:
                        pe.wait_ge(s_q, i)
                        pe.wait_ge(s_k, i)
                        if has(i, 3):
                            pe.wait_ge(c_rt, (i - 3) * RT_LINKS + 1)
                        else:
                            wait(pe, s_pT, i - 1)
                    else:
                        wait(pe, s_y, i - 1)
                    for t in range(ROW_TILES):
                        last = pe.matmul(ps_s[p][:, t * SEQ:(t + 1) * SEQ],
                                         q_sb[:, other, p * SEQ + t * P:p * SEQ + (t + 1) * P],
                                         k_sb[:, other, p * SEQ:(p + 1) * SEQ], start=True, stop=True)
                    last.then_inc(s_s_ps, 1)
                if p == (0 if last_round(i) else 2) and has(i, 3):
                    pe.wait_ge(s_count, i - 2)
                    if has(i, 1):
                        wait(pe, s_s, 2 * i)
                    for t in range(ROW_TILES):
                        dst = ps_place[:, t * EXPERTS:(t + 1) * EXPERTS]
                        pe.matmul(dst, before[:, :], mask[:, t, :], start=True, stop=False)
                        for u in range(t):
                            pe.matmul(dst, ones[:, :], mask[:, u, :], start=False, stop=False)
                        pe.matmul(dst, ones[:, :], count[:, other, :], start=False, stop=True)
                    pe.matmul(ps_total, ones[:, :], count[:, par, :], start=True, stop=True
                              ).then_inc(s_place_ps, 1)
                if p == 3 and has(i, 0):
                    pe.wait_ge(s_xn, i + 1)
                    if has(i, 2):
                        wait(pe, s_o, i - 1)
                    elif not has(i, 2):
                        wait(pe, s_v_raw, i)
                    transpose_rows(ps_xT, lambda t, c: xn[:, t * DIM + c * P:t * DIM + (c + 1) * P]
                                   ).then_inc(s_xT_ps, 1)
                if p in (4, 5) and has(i, 0):
                    n, ps, done = ((0, ps_q, s_q_ps), (1, ps_k, s_k_ps))[p - 4]
                    pe.wait_ge(s_xT, i + 1)
                    if p == 4 and has(i, 1):
                        wait(pe, s_s, 2 * i - 1)
                    if p == 5 and has(i, 1):
                        wait(pe, s_s, 2 * i)
                    if p == 5 and has(i, 3):
                        wait(pe, s_placed, i - 2)
                    for h in range(HEADS):
                        for c in range(CHUNKS):
                            last = pe.matmul(ps[:, h * SEQ:(h + 1) * SEQ],
                                             attn_w[:, n, c, h * HEAD_DIM:(h + 1) * HEAD_DIM],
                                             xT3[:, c, :], start=(c == 0), stop=(c == CHUNKS - 1))
                    last.then_inc(done, 1)
                if p == 6 and has(i, 0):
                    for t in range(ROW_TILES):
                        for c in range(CHUNKS):
                            last = pe.matmul(ps_v[:, t * DIM:(t + 1) * DIM], xT3[:, c, t * P:(t + 1) * P],
                                             attn_w[:, 2, c, :], start=(c == 0), stop=(c == CHUNKS - 1))
                    last.then_inc(s_v_ps, 1)
                if p == 7 and has(i, 1):
                    pe.wait_ge(s_p, i)
                    if has(i, 0):
                        wait(pe, s_q_raw, i + 1)
                    for h in range(HEADS):
                        for kt in range(ROW_TILES):
                            for t in range(ROW_TILES):
                                o = (h * ROW_TILES + kt) * SEQ + t * P
                                s = (h * ROW_TILES + t) * SEQ + kt * P
                                last = pe.transpose(ps_pT[:, o:o + P], probs[:, s:s + P], ident[:, :])
                    last.then_inc(s_pT_ps, 1)
                if p == 9 and has(i, 2):
                    pe.wait_ge(s_xf, i - 1)
                    if has(i, 0):
                        wait(pe, s_v_raw, i + 1)
                    transpose_rows(ps_xfT, lambda t, c: payload[:, par * 4 + t * TOP_K, c * 64:(c + 1) * 64]
                                   .bitcast(bf16)).then_inc(s_xfT_ps, 1)
                if p == 9 and has(i, 1):
                    pe.wait_ge(s_pT, i)
                    pe.wait_ge(s_v, i)
                    if has(i, 0):
                        wait(pe, s_k_raw, i + 1)
                    for h in range(HEADS):
                        for kt in range(ROW_TILES):
                            o = (h * ROW_TILES + kt) * SEQ
                            last = pe.matmul(ps_y[:, h * SEQ:(h + 1) * SEQ],
                                             v_sb[:, other, kt * DIM + h * HEAD_DIM:kt * DIM + (h + 1) * HEAD_DIM],
                                             probsT[:, o:o + SEQ], start=(kt == 0), stop=(kt == ROW_TILES - 1))
                    last.then_inc(s_y_ps, 1)
                if p == 10 and has(i, 2):
                    pe.wait_ge(s_xfT, i - 1)
                    if has(i, 1):
                        wait(pe, s_pT, i)
                    pe.wait_ge(s_router, 1)
                    f3 = xfT[:, :].rearrange("p (c t) -> p c t", c=CHUNKS)
                    for t in range(ROW_TILES):
                        for n in range(CHUNKS * PARTS):
                            c, part = n % CHUNKS, n // CHUNKS
                            last = pe.matmul(ps_logits[:, t * EXPERTS:(t + 1) * EXPERTS],
                                             f3[:, c, t * P:(t + 1) * P], router_w[:, part, c, :],
                                             start=(n == 0), stop=(n == CHUNKS * PARTS - 1))
                    last.then_inc(s_lg_ps, 1)

            def round_(i, par, m, pair):
                tiles = runs_tiles(m)
                if isinstance(m, int) and m == 0:
                    pe.wait_ge(s_lo, WEIGHT_CHUNKS)
                    pe.wait_ge(s_sel, 2)
                    rows_transposed(0, 0)
                for p in range(12):
                    n, k = p // 3, p % 3
                    if not tiles:
                        attention_part(i, par, p)
                        continue
                    if k == 0:
                        first = expert_of(chosen_tiles[0:1, par, 1, n:n + 1])
                    tile_third(m, n, k, first, lambda: attention_part(i, par, p))
            rounds(pe, round_)

            def group_(m, tiles):
                for n in range(tiles):
                    at = GROUP * (m - GROUPS_IN_ROUNDS) + n
                    first = expert_of(rest_tiles[0:1, 1, bass.ds(at, 1)])
                    for k in range(3):
                        tile_third(m, n, k, first)
            rest_groups(pe, group_)
            last_k = 3 * MOE_TILES
            m, n = MOE_TILES // GROUP, MOE_TILES % GROUP - 1
            hidden_transposed(last_k - 2, 1)
            down_third(m, n, 0)
            hidden_transposed(last_k - 1, 2)
            down_third(m, n, 1)
            down_third(m, n, 2)

        @block.vector
        def _(dve):
            n_prep = [0]

            def prep(ins):
                n_prep[0] += 1
                ins.then_inc(s_prep, 1)
                dve.wait_ge(s_prep, n_prep[0] + 1)
            dve.wait_ge(s_small, 16 * 5)
            dve.wait_ge(s_const, CONSTS)
            prep(dve.tensor_copy(router_w[:, 0], router32[:, :, :]))
            prep(dve.tensor_tensor(router32[:, :, :], router32[:, :, :], router_w[:, 0], ALU.subtract))
            prep(dve.tensor_copy(router_w[:, 1], router32[:, :, :]))
            dve.tensor_tensor(router_w[:, 2], router32[:, :, :], router_w[:, 1], ALU.subtract).then_inc(s_router, 1)

            def norm_stats(link, which, src):
                for t in range(ROW_TILES):
                    ins = dve.bn_stats(ln_stats[:, which, t, :], src[:, t, :])
                link(ins)
                dve.tensor_tensor(ln_sum[:, which, :], ln_stats[:, which, :, 1], ln_stats[:, which, :, 4], ALU.add)
                for t in range(ROW_TILES):
                    ins = dve.bn_aggr(ln_mv[:, which, t, :], ln_stats[:, which, t, :])
                link(ins)
                dve.tensor_scalar(ln_mean[:, which, :], ln_sum[:, which, :], 0.5, None, ALU.mult)
                dve.tensor_scalar(ln_var[:, which, :], ln_mv[:, which, :, 1], EPS_BF16, None, ALU.add
                                  ).then_inc(s_var[which], 1)

            def norm_rows(link, which, b, src, dsts, centred):
                dve.wait_ge(s_root[which], b + 1)
                link(dve.reciprocal(ln_inv[:, which, :], ln_std[:, which, :]))
                for t in range(ROW_TILES):
                    ins = dve.tensor_scalar(centred[:, t, :], src[:, t, :], ln_mean[:, which, t:t + 1],
                                            None, ALU.subtract)
                link(ins)
                for d in dsts:
                    for t in range(ROW_TILES):
                        ins = dve.tensor_scalar(d(t), centred[:, t, :], ln_inv[:, which, t:t + 1], None, ALU.mult)
                return ins

            def softmax_maxima(i, link):
                dve.wait_ge(s_s, 2 * i)
                link(dve.tensor_scalar(probs[:, :], probs[:, :], SCALE_BF16, None, ALU.mult))
                p4 = probs[:, :].rearrange("p (u n) -> p u n", u=4)
                link(dve.tensor_reduce(sm_max[:, :], p4, AX.X, ALU.max))

            def softmax_differences():
                p4 = probs[:, :].rearrange("p (u n) -> p u n", u=4)
                for u in range(4):
                    ins = dve.tensor_scalar(p4[:, u, :], p4[:, u, :], sm_max[:, u:u + 1], None, ALU.subtract)
                ins.then_inc(s_sub, 1)

            def softmax_quotients(i, link):
                dve.wait_ge(s_exp, i)
                p4 = probs[:, :].rearrange("p (u n) -> p u n", u=4)
                link(dve.tensor_reduce(sm_total[:, :], p4, AX.X, ALU.add))
                link(dve.tensor_copy(sm_sum[:, :], sm_total[:, :]))
                link(dve.reciprocal(sm_inv[:, :], sm_sum[:, :]))
                for u in range(4):
                    ins = dve.tensor_scalar(p4[:, u, :], p4[:, u, :], sm_inv[:, u:u + 1], None, ALU.mult)
                ins.then_inc(s_p, 1)

            def projection(i, par, n):
                dst, raw, done = ((q_sb, s_q_raw, s_q), (k_sb, s_k_raw, s_k))[n]
                if before_tiles(i):
                    return
                dve.wait_ge(raw, i + 1)
                for h in range(HEADS):
                    d = dst[:, par, h * SEQ:(h + 1) * SEQ]
                    ins = dve.tensor_scalar(d, d, qk_biasf[:, n, h:h + 1], 0.0, ALU.add, ALU.max)
                ins.then_inc(done, 1)

            def values(i, par):
                dve.wait_ge(s_v_raw, i + 1)
                v = rows(v_sb[:, par, :])
                dve.tensor_tensor(v, v, row_bias[:, 0:1, :].to_broadcast([P, ROW_TILES, DIM]), ALU.add
                                  ).then_inc(s_v_sum, 1)
                dve.wait_ge(s_v_sum, i + 1)
                dve.tensor_scalar(v, v, 0.0, None, ALU.max).then_inc(s_v, 1)

            def output_bias(i, link):
                dve.wait_ge(s_o, i - 1)
                o = rows(oo[:, :])
                link(dve.tensor_tensor(o, o, row_bias[:, 1:2, :].to_broadcast([P, ROW_TILES, DIM]), ALU.add))
                link(dve.tensor_scalar(o, o, 0.0, None, ALU.max))
                norm_stats(link, 1, o)

            def residual_sum(i, par, pair, link):
                o = rows(oo[:, :])
                link(norm_rows(link, 1, i - 2, o, [lambda t: o[:, t, :]], o))
                dve.wait_ge(s_xa[par], 16 * pair)
                wait(dve, s_x1_saved[par], 16 * (pair - 1))
                z = rows(x1[:, par, :])
                dve.tensor_tensor(z, rows(x_again[:, par, :]), o, ALU.add).then_inc(s_x1, 1)
                dve.wait_ge(s_x1, i - 1)

            def expert_input(i, par, pair, link):
                wait(dve, s_sent[par], 16 * ROW_TILES * TOP_K * (pair - 1))
                norm_rows(link, 2, i - 2, rows(x1[:, par, :]), [
                    (lambda t, k=k: payload[:, par * 4 + t * TOP_K + k, 0:DIM // 2].bitcast(bf16))
                    for k in range(TOP_K)], rows(oo[:, :])).then_inc(s_xf, 1)

            def route(i, par, link):
                dve.wait_ge(s_lg_ps, i - 1)
                link(dve.tensor_copy(logits[:, :, :], ps_logits.rearrange("p (t e) -> p t e", t=ROW_TILES)))
                for t in range(ROW_TILES):
                    mine = logits[:, t, :].unsqueeze(2).to_broadcast([P, EXPERTS, EXPERTS])
                    theirs = logits[:, t, :].unsqueeze(1).to_broadcast([P, EXPERTS, EXPERTS])
                    dve.tensor_tensor(above[:, t], theirs, mine, ALU.is_gt)
                    ins = dve.tensor_tensor(level[:, t], theirs, mine, ALU.is_ge)
                link(ins)
                for t in range(ROW_TILES):
                    ins = dve.tensor_tensor(level[:, t], level[:, t], lower[:, :, :], ALU.mult)
                link(ins)
                link(dve.tensor_tensor(above[:, :, :, :], above[:, :, :, :], level[:, :, :, :], ALU.max))
                link(dve.tensor_reduce(rank[:, :, :], above[:, :, :, :], AX.X, ALU.add))
                dve.tensor_scalar(mask[:, :, :], rank[:, :, :], float(TOP_K), None, ALU.is_lt)
                for k in range(TOP_K):
                    ins = dve.tensor_scalar(chosen[:, :, k, :], rank[:, :, :], float(k), None, ALU.is_equal)
                link(ins)
                for k in range(TOP_K):
                    ins = dve.tensor_tensor(picked[:, :, k, :], chosen[:, :, k, :], logits[:, :, :], ALU.mult)
                link(ins)
                link(dve.tensor_reduce(top[:, :, :], picked[:, :, :, :], AX.X, ALU.add))
                dve.tensor_tensor(gap[:, :], top[:, :, 1], top[:, :, 0], ALU.subtract).then_inc(s_gap, 1)
                link(dve.tensor_tensor(count[:, 1 - par, :], count[:, par, :], mask[:, 0, :], ALU.add))
                dve.tensor_tensor(count[:, 1 - par, :], count[:, 1 - par, :], mask[:, 1, :], ALU.add
                                  ).then_inc(s_count, 1)

            def places(i, link):
                dve.wait_ge(s_place_ps, i - 2)
                dve.tensor_copy(total[:, :], ps_total)
                link(dve.tensor_tensor(place[:, :, :], ps_place.rearrange("p (t e) -> p t e", t=ROW_TILES),
                                       region_start[:, :].unsqueeze(1).to_broadcast([P, ROW_TILES, EXPERTS]),
                                       ALU.add))
                for k in range(TOP_K):
                    ins = dve.tensor_tensor(picked2[:, :, k, :], chosen[:, :, k, :], place[:, :, :], ALU.mult)
                ins.then_inc(s_placed, 1)

            def send(i, par, link):
                dve.wait_ge(s_placed, i - 2)
                link(dve.tensor_reduce(slotf[:, :, :], picked2[:, :, :, :], AX.X, ALU.add))
                dve.tensor_copy(slot[:, par, :], slotf[:, :, :].rearrange("p t k -> p (t k)"))
                dve.wait_ge(s_gexp, i - 2)
                link(dve.tensor_scalar(denom[:, :], gap_exp[:, :], 1.0, None, ALU.add))
                link(dve.reciprocal(prob[:, :, 0], denom[:, :]))
                link(dve.tensor_tensor(prob[:, :, 1], prob[:, :, 0], gap_exp[:, :], ALU.mult))
                pay = payload[:, par * 4:par * 4 + 4, :]
                dve.tensor_copy(pay[:, :, DIM // 2 + 1].bitcast(fp32), prob[:, :, :].rearrange("p t k -> p (t k)"))
                link(dve.tensor_copy(pay[:, :, DIM // 2], dest[:, :, :].rearrange("p t k -> p (t k)")))
                dve.tensor_scalar(dest[:, :, :], dest[:, :, :], SEQ, None, ALU.add).then_inc(s_slot, 1)

            def select(link, tiles, up):
                link(dve.tensor_scalar(tile_q[:, :], total[0:1, :], 1.0 / P, (0.5 - 0.5 / P) * (1 if up else -1),
                                       ALU.mult, ALU.add))
                link(dve.tensor_scalar(tiles_full[:, :], tile_q[:, :], ROUNDER, -ROUNDER, ALU.add, ALU.add))
                link(dve.tensor_tensor(tiles_left[:, :], tiles_full[:, :], tiles_run[:, :], ALU.subtract))
                link(dve.tensor_tensor(left_below[:, :, :], lower[0:1, :, :],
                                       tiles_left[:, :].unsqueeze(1).to_broadcast([1, EXPERTS, EXPERTS]), ALU.mult))
                link(dve.tensor_reduce(below[:, :], left_below[:, :, :], AX.X, ALU.add))
                link(dve.tensor_tensor(upto[:, :], below[:, :], tiles_left[:, :], ALU.add))
                dve.tensor_scalar(taken[:, :], below[:, :], -1.0, float(tiles), ALU.mult, ALU.add)
                link(dve.tensor_tensor(full_less[:, :], tiles_full[:, :], upto[:, :], ALU.subtract))
                link(dve.scalar_tensor_tensor(start_row[:, 0:EXPERTS], full_less[:, :], float(P),
                                              region_start[0:1, :], ALU.mult, ALU.add))

            def selected(link, tiles, table):
                one = [1, tiles, EXPERTS]
                dve.tensor_tensor(reached[:, 0:tiles, :], nth[:, 0:tiles].unsqueeze(2).to_broadcast(one),
                                  upto[:, :].unsqueeze(1).to_broadcast(one), ALU.is_ge)
                link(dve.tensor_tensor(row_step[:, :], start_row[:, 1:], start_row[:, 0:EXPERTS], ALU.subtract))
                dve.tensor_reduce(sel_expert[:, 0:tiles], reached[:, 0:tiles, :], AX.X, ALU.add)
                link(dve.tensor_tensor(stepped[:, 0:tiles, :], reached[:, 0:tiles, :],
                                       row_step[:, :].unsqueeze(1).to_broadcast(one), ALU.mult))
                link(dve.scalar_tensor_tensor(taken[:, :], taken[:, :], 0.0, tiles_left[:, :], ALU.max, ALU.min))
                link(dve.tensor_reduce(sel_row[:, 0:tiles], stepped[:, 0:tiles, :], AX.X, ALU.add))
                dve.tensor_tensor(tiles_run[:, :], tiles_run[:, :], taken[:, :], ALU.add)
                link(dve.scalar_tensor_tensor(sel_rowf[:, 0:tiles], sel_row[:, 0:tiles], start_row[:, 0:1],
                                              nth_row[:, 0:tiles], ALU.add, ALU.add))
                dve.tensor_scalar(table[0], sel_rowf[:, 0:tiles], float(DUMMY_ROW), None, ALU.min
                                  ).then_inc(s_sel, 1)
                dve.tensor_scalar(table[1], sel_expert[:, 0:tiles], float(EXPERTS - 1), None, ALU.min
                                  ).then_inc(s_sel, 1)

            def rows_in(m, n):
                j = GROUP * m + n
                dve.wait_ge(s_xrow_ps, j + 1)
                dve.tensor_copy(xT_buf[:, n % 2, :, :].rearrange("p c t -> p (c t)"), ps_xrow).then_inc(s_xrow, 1)
                wait(dve, s_scat[n], 16 * m)
                dve.tensor_copy(meta[:, n, :], tile_rows[:, n, DIM // 2:]).then_inc(s_meta, 1)

            def multiply(m, n, k):
                K = 3 * (GROUP * m + n) + k
                w = THIRDS[k]
                dve.wait_ge(s_gated, K + 1)
                wait(dve, s_hT_ps, K - 2)
                dve.tensor_tensor(hidden[:, k, 0:w], gated[:, k, 0:w], ps_gu[k][:, w:2 * w], ALU.mult
                                  ).then_inc(s_h, 1)

            def round_(i, par, m, pair):
                other = 1 - par
                x3, xn3 = rows(x_in[:, par, :]), rows(xn[:, :])
                link0, _ = chain(dve, c_ln1, i * LN_LINKS + 2)
                link1, _ = chain(dve, c_ln1, (i + 1) * LN_LINKS)
                link2, n2 = chain(dve, c_out, (i - 2) * OUT_LINKS)
                link3, n3 = chain(dve, c_rt, (i - 2) * RT_LINKS)
                link4, n4 = chain(dve, c_send, (i - 3) * SEND_LINKS)
                link5, n5 = chain(dve, c_sm, (i - 1) * SM_LINKS)
                tiles = runs_tiles(m)
                selects = (tiles or m == -1) and not last_round(i)
                if isinstance(m, int) and m == 0:
                    rows_in(0, 0)
                for p in range(12):
                    n, k = p // 3, p % 3
                    if p == 0 and has(i, 0):
                        wait(dve, s_xT_ps, i)
                        norm_rows(link0, 0, i, x3, [lambda t: xn3[:, t, :]], xn3).then_inc(s_xn, 1)
                    if p == 1 and has(i, 2):
                        output_bias(i, link2)
                    if p == 2 and has(i, 1):
                        softmax_maxima(i, link5)
                    if p == 3 and has(i, 1):
                        softmax_differences()
                    if p == (0 if last_round(i) else 3) and has(i, 3):
                        places(i, link4)
                    if p == 4 and has(i, 2):
                        residual_sum(i, par, pair, link2)
                    if p == 5 and has(i, 2):
                        norm_stats(link2, 2, rows(x1[:, par, :]))
                    if p == (1 if last_round(i) else 5) and has(i, 3):
                        send(i, other, link4)
                        assert n4[0] == SEND_LINKS, n4
                    if p == 5 and has(i, 0):
                        projection(i, par, 0)
                    if p == 6 and has(i, 1):
                        softmax_quotients(i, link5)
                        assert n5[0] == SM_LINKS, n5
                    if p == 2 and last_round(i):
                        link6, _ = chain(dve, c_sel, (m + 1) * SEL_LINKS)
                        link6(dve.tensor_tensor(pad_place[:, :], pad_place[:, :], total[:, :], ALU.add))
                        dve.tensor_copy(pad_slot[:, :], pad_place[:, :]).then_inc(s_pad, 1)
                        select(link6, REST, True)
                        selected(link6, REST, [rest_tiles[:, t, :] for t in range(2)])
                    if p == 7 and has(i, 2):
                        expert_input(i, par, pair, link2)
                        assert n2[0] == OUT_LINKS, n2
                    if p == 4 and selects:
                        link6, n6 = chain(dve, c_sel, (m + 1) * SEL_LINKS)
                        select(link6, GROUP, False)
                    if p == 8 and has(i, 1):
                        dve.wait_ge(s_pT_ps, i)
                        wait(dve, s_y_ps, i - 1)
                        dve.tensor_copy(probsT[:, :], ps_pT).then_inc(s_pT, 1)
                    if p == 7 and selects:
                        selected(link6, GROUP, [chosen_tiles[:, other, t, :] for t in range(2)])
                        assert n6[0] == SEL_LINKS, n6
                    if p == 9 and has(i, 0):
                        projection(i, par, 1)
                        values(i, par)
                    if p == 10 and has(i, -1):
                        batch_in(i + 1, other, pair + 1 if par == 0 else pair + 2, link1)
                    if p == 11 and has(i, 2):
                        route(i, par, link3)
                        assert n3[0] == RT_LINKS, n3
                    c = weight_chunk(i, p, 2)
                    if c is not None:
                        dve.wait_ge(s_mid, c + 1)
                        dve.tensor_tensor(gu_w[:, c * PARTS + 2, :], left[c % 3],
                                          gu_w[:, c * PARTS + 1, :], ALU.subtract).then_inc(s_lo, 1)
                    if tiles:
                        multiply(m, n, k)
                        if k == 0:
                            rows_in(m if n < GROUP - 1 else m + 1, (n + 1) % GROUP)

            def batch_in(b, par, loads, link):
                dve.wait_ge(s_x[par], 16 * loads)
                norm_stats(link, 0, rows(x_in[:, par, :]))

            dve.wait_ge(s_prep, 4)
            batch_in(0, 0, 1, chain(dve, c_ln1, 0)[0])
            rounds(dve, round_)

            def group_(m, tiles):
                for n in range(tiles):
                    for k in range(3):
                        multiply(m, n, k)
                        if k == 0 and not (isinstance(m, int) and GROUP * m + n + 1 == MOE_TILES):
                            rows_in(m if n < GROUP - 1 else m + 1, (n + 1) % GROUP)
            rest_groups(dve, group_)

            link, _ = chain(dve, c_tail, 0)
            def sums(g):
                dve.wait_ge(s_ty[g], 32)
                y0 = tail_y[:, g, 0].rearrange("p r d -> p (r d)")
                link(dve.tensor_tensor(y0, y0, tail_y[:, g, 1].rearrange("p r d -> p (r d)"), ALU.add))
                if g >= 3:
                    dve.wait_ge(s_tnorm, g - 2)
                for r in range(TAIL_ROWS):
                    ins = dve.bn_stats(tail_stats[:, g % 3, r, :], tail_y[:, g, 0, r, :])
                link(ins)
                for r in range(TAIL_ROWS):
                    ins = dve.bn_aggr(tail_mv[:, g % 3, r, :], tail_stats[:, g % 3, r, :])
                link(ins)
                dve.tensor_scalar(tail_var[:, g % 3, :], tail_mv[:, g % 3, :, 1], EPS, None, ALU.add
                                  ).then_inc(s_tvar, 1)

            def shift(g):
                dve.wait_ge(s_troot, g + 1)
                dve.scalar_tensor_tensor(tail_shift[:, g % 3, :], tail_mv[:, g % 3, :, 0], -1.0,
                                         tail_inv[:, g % 3, :], ALU.mult, ALU.mult).then_inc(s_tshift, 1)

            for g in range(TAIL_GROUPS + 1):
                if g < TAIL_GROUPS:
                    sums(g)
                if g >= 1:
                    shift(g - 1)


CONSTS = 16
SENT = 16 * ROW_TILES * TOP_K
EPS_BF16 = 1.0013580322265625e-05
SCALE_BF16 = 0.08837890625
LN_LINKS, SM_LINKS, OUT_LINKS, RT_LINKS, SEND_LINKS, SEL_LINKS = 4, 5, 11, 9, 6, 13
ROUNDER = 1.5 * 2 ** 23


def kernel(**inputs):
    import numpy as _np
    import concourse.bacc as _bacc
    from concourse import mybir as _mybir
    from concourse.bass_utils import run_bass_kernel_spmd as _run

    def host(name):
        return _np.asarray(inputs[name])

    arrays = {"base": host("L0_attn_base")}
    for n, src in (("wqT", "Wq"), ("wkT", "Wk"), ("wvT", "Wv"), ("woT", "Wo")):
        arrays[n] = host("L0_attn_" + src).T
    for n in ("bq", "bk", "bv", "bo"):
        arrays[n] = host("L0_attn_" + n)
    arrays["routerT"] = host("L0_ffn_router_w").T
    gate = host("L0_ffn_gate_w").transpose(0, 2, 1)
    up = host("L0_ffn_up_w").transpose(0, 2, 1)
    parts, at = [], 0
    for w in THIRDS:
        parts += [gate[:, :, at:at + w], up[:, :, at:at + w]]
        at += w
    arrays["gate_up"] = _np.concatenate(parts, axis=2).reshape(EXPERTS * CHUNKS, P, 2 * FFN)
    dn = host("L0_ffn_down_w").transpose(0, 2, 1)
    laid = _np.zeros((EXPERTS, P, 6, DIM), dn.dtype)
    at = 0
    for n in range(6):
        size = PIECES[n // 2][n % 2]
        laid[:, :size, n, :] = dn[:, at:at + size, :]
        at += size
    arrays["down"] = laid.reshape(EXPERTS, P, 6 * DIM)

    nc = _bacc.Bacc("TRN2", target_bir_lowering=False, num_devices=1)
    args, named = [], {}
    for name, a in arrays.items():
        a = _np.ascontiguousarray(a)
        named[f"in_{name}_dram"] = a
        args.append(nc.dram_tensor(f"in_{name}_dram", a.shape, _mybir.dt.from_np(a.dtype), kind="ExternalInput").ap())
    out = nc.dram_tensor("out_dram", (TOKENS, DIM), _mybir.dt.float32, kind="ExternalOutput").ap()
    build(nc, *args, out)
    r = _run(nc, [named], core_ids=[0])
    return r.results[0]["out_dram"].reshape(BATCHES, SEQ, DIM)
```
